# Optimizing a Trainium2 kernel written in Bass

```python
import numpy as np
import jax
import jax.numpy as jnp

def _softmax(x, axis=-1):
    return jax.nn.softmax(x, axis=axis)

def _gelu(x):
    return jax.nn.gelu(x, approximate=True)

def _silu(x):
    return jax.nn.silu(x)

def _sigmoid(x):
    return jax.nn.sigmoid(x)

def _layernorm(x, axis=-1, eps=1e-05):
    m = jnp.mean(x, axis=axis, keepdims=True)
    v = jnp.var(x, axis=axis, keepdims=True)
    return (x - m) / jnp.sqrt(v + eps)

def _scatter_add(tgt, idx, src, axis=0):
    return tgt.at[idx].add(src)

def _segment_sum(src, seg, n):
    return jax.ops.segment_sum(src, seg, n)
kernel_name = 'mk_prb_d2_jaxref_r8_6533b6'

def setup_inputs(seed: int=0):
    np.random.seed(seed)
    _w = jnp.asarray

    def _L0_attn_setup():
        import jax, jax.numpy as jnp
        import numpy as np
        import math
        D_MODEL = 128
        D_QUERY = 64
        key = jax.random.key(seed)
        k1, k2, k3, k4 = jax.random.split(key, 4)
        X = jax.random.normal(k1, (4, 512, D_MODEL), dtype=jnp.float32)
        Wq = jax.random.normal(k2, (D_MODEL, D_QUERY), dtype=jnp.float32) * (1.0 / math.sqrt(D_MODEL))
        Wk = jax.random.normal(k3, (D_MODEL, D_QUERY), dtype=jnp.float32) * (1.0 / math.sqrt(D_MODEL))
        Wv = jax.random.normal(k4, (D_MODEL, D_MODEL), dtype=jnp.float32) * (1.0 / math.sqrt(D_MODEL))
        return {'X': X, 'Wq': Wq, 'Wk': Wk, 'Wv': Wv}
    _L0_attn_in = _L0_attn_setup()

    def _L0_ffn_setup():
        import jax, jax.numpy as jnp
        import numpy as np
        DIM = 128
        DEPTH = 2
        HEADS = 8
        DIM_HEAD = 64
        WINDOW = 64
        INNER = HEADS * DIM_HEAD
        HID = int(DIM * 4 * 2 / 3)
        B, N = (2, 1024)
        QK_SCALE = 8.0

        def shift_token(t):
            t1, t2 = jnp.split(t, 2, axis=-1)
            t2 = jnp.pad(t2, ((0, 0), (1, 0), (0, 0)))[:, :-1]
            return jnp.concatenate([t1, t2], axis=-1)

        def l2norm(t):
            return t / jnp.clip(jnp.linalg.norm(t, axis=-1, keepdims=True), 1e-12)

        def rotate_half(x):
            x1, x2 = jnp.split(x, 2, axis=-1)
            return jnp.concatenate([-x2, x1], axis=-1)

        def rotary_xpos(q, k):
            n = q.shape[-2]
            half_idx = jnp.arange(0, DIM_HEAD, 2, dtype=jnp.float32)
            inv_freq = 1.0 / 10000.0 ** (half_idx / DIM_HEAD)
            t = jnp.arange(n, dtype=jnp.float32)
            freqs = t[:, None] * inv_freq[None, :]
            freqs = jnp.concatenate([freqs, freqs], axis=-1)
            base = (half_idx + 0.4 * DIM_HEAD) / (1.4 * DIM_HEAD)
            power = (t - n // 2) / float(WINDOW // 2)
            scale = base[None, :] ** power[:, None]
            scale = jnp.concatenate([scale, scale], axis=-1)
            cos, sin = (jnp.cos(freqs), jnp.sin(freqs))
            q = q * cos * scale + rotate_half(q) * sin * scale
            k = k * cos / scale + rotate_half(k) * sin / scale
            return (q, k)

        def local_attention(q, k, v):
            b, h, n, d = q.shape
            w = n // WINDOW
            bq = q.reshape(b, h, w, WINDOW, d) * QK_SCALE
            bk = k.reshape(b, h, w, WINDOW, d)
            bv = v.reshape(b, h, w, WINDOW, d)

            def look_around(t):
                p = jnp.pad(t, ((0, 0), (0, 0), (1, 0), (0, 0), (0, 0)))
                return jnp.concatenate([p[:, :, :w], p[:, :, 1:]], axis=3)
            bk, bv = (look_around(bk), look_around(bv))
            bt = jnp.arange(n).reshape(w, WINDOW)
            btp = jnp.pad(bt, ((1, 0), (0, 0)), constant_values=-1)
            btk = jnp.concatenate([btp[:w], btp[1:]], axis=1)
            sim = jnp.einsum('bhwid,bhwjd->bhwij', bq, bk)
            i = bt[:, :, None]
            j = btk[:, None, :]
            mask = (i < j) | (i > j + WINDOW) | (j == -1)
            sim = jnp.where(mask, -jnp.finfo(sim.dtype).max, sim)
            attn = jax.nn.softmax(sim, axis=-1)
            out = jnp.einsum('bhwij,bhwjd->bhwid', attn, bv)
            return out.reshape(b, h, n, d)

        def _layer(x, wqkv, qs, ksc, wo, lg, lb, w1, b1, w2, b2):
            b, n, _ = x.shape
            h = shift_token(x)
            qkv = h @ wqkv
            q, k, v = jnp.split(qkv, 3, axis=-1)
            to_heads = lambda t: t.reshape(b, n, HEADS, DIM_HEAD).transpose(0, 2, 1, 3)
            q, k, v = (to_heads(q), to_heads(k), to_heads(v))
            q = l2norm(q) * qs
            k = l2norm(k) * ksc
            q, k = rotary_xpos(q, k)
            o = local_attention(q, k, v)
            o = o.transpose(0, 2, 1, 3).reshape(b, n, INNER)
            x = x + o @ wo
            h = shift_token(x)
            mu = h.mean(-1, keepdims=True)
            var = h.var(-1, keepdims=True)
            h = (h - mu) / jnp.sqrt(var + 1e-05) * lg + lb
            h = h @ w1 + b1
            a, g = jnp.split(h, 2, axis=-1)
            h = a * jax.nn.gelu(g, approximate=False)
            x = x + h @ w2 + b2
            return x
        key = jax.random.key(seed)
        ks = jax.random.split(key, 6)
        return {'x': jax.random.normal(ks[0], (B, N, DIM), jnp.float32), 'wqkv': jax.random.normal(ks[1], (DEPTH, DIM, 3 * INNER), jnp.float32) * 0.02, 'q_scale': jnp.ones((DEPTH, DIM_HEAD), jnp.float32), 'k_scale': jnp.ones((DEPTH, DIM_HEAD), jnp.float32), 'wo': jax.random.normal(ks[2], (DEPTH, INNER, DIM), jnp.float32) * 0.02, 'ln_g': jnp.ones((DEPTH, DIM), jnp.float32), 'ln_b': jnp.zeros((DEPTH, DIM), jnp.float32), 'w1': jax.random.normal(ks[3], (DEPTH, DIM, 2 * HID), jnp.float32) * 0.02, 'b1': jnp.zeros((DEPTH, 2 * HID), jnp.float32), 'w2': jax.random.normal(ks[4], (DEPTH, HID, DIM), jnp.float32) * 0.02, 'b2': jnp.zeros((DEPTH, DIM), jnp.float32)}
    _L0_ffn_in = _L0_ffn_setup()

    def _L1_attn_setup():
        import jax, jax.numpy as jnp
        import numpy as np
        DIM_IN, DIM_K, DIM_V, N_QUERY = (128, 128, 128, 8)

        def _kaiming_uniform(key, shape):
            fan_in = shape[-2] if len(shape) > 1 else shape[-1]
            gain = 1.0 / np.sqrt(3.0)
            bound = gain * np.sqrt(3.0 / fan_in)
            return jax.random.uniform(key, shape, jnp.float32, -bound, bound)
        key = jax.random.key(seed)
        kx, kq, kk, kv, ko = jax.random.split(key, 5)
        x = jax.random.normal(kx, (4, 256, DIM_IN), dtype=jnp.float32)
        proj_q = _kaiming_uniform(kq, (N_QUERY, DIM_IN, DIM_K))
        proj_k = _kaiming_uniform(kk, (DIM_IN, DIM_K))
        proj_v = _kaiming_uniform(kv, (DIM_IN, DIM_V))
        proj_o = _kaiming_uniform(ko, (N_QUERY, DIM_IN, DIM_V))
        return {'x': x, 'proj_q': proj_q, 'proj_k': proj_k, 'proj_v': proj_v, 'proj_o': proj_o}
    _L1_attn_in = _L1_attn_setup()

    def _L1_ffn_setup():
        import jax, jax.numpy as jnp
        import numpy as np
        DIM = 128
        HIDDEN = 384
        SCALE = 1.0 / 127.0

        def _dequant(w_int, dtype):
            return w_int.astype(dtype) * jnp.asarray(SCALE, dtype)
        key = jax.random.key(seed)
        k_x, k_g, k_u, k_d = jax.random.split(key, 4)
        x = jax.random.normal(k_x, (4, 256, DIM), dtype=jnp.float32)
        w_gate = jax.random.randint(k_g, (HIDDEN, DIM), -127, 128, dtype=jnp.int32)
        w_up = jax.random.randint(k_u, (HIDDEN, DIM), -127, 128, dtype=jnp.int32)
        w_down = jax.random.randint(k_d, (DIM, HIDDEN), -127, 128, dtype=jnp.int32)
        return {'x': x, 'w_gate': w_gate, 'w_up': w_up, 'w_down': w_down}
    _L1_ffn_in = _L1_ffn_setup()
    _d = {'L0_attn_X': _L0_attn_in['X'], 'L0_attn_Wq': _L0_attn_in['Wq'], 'L0_attn_Wk': _L0_attn_in['Wk'], 'L0_attn_Wv': _L0_attn_in['Wv'], 'L0_ffn_wqkv': _L0_ffn_in['wqkv'], 'L0_ffn_q_scale': _L0_ffn_in['q_scale'], 'L0_ffn_k_scale': _L0_ffn_in['k_scale'], 'L0_ffn_wo': _L0_ffn_in['wo'], 'L0_ffn_ln_g': _L0_ffn_in['ln_g'], 'L0_ffn_ln_b': _L0_ffn_in['ln_b'], 'L0_ffn_w1': _L0_ffn_in['w1'], 'L0_ffn_b1': _L0_ffn_in['b1'], 'L0_ffn_w2': _L0_ffn_in['w2'], 'L0_ffn_b2': _L0_ffn_in['b2'], 'L1_attn_proj_q': _L1_attn_in['proj_q'], 'L1_attn_proj_k': _L1_attn_in['proj_k'], 'L1_attn_proj_v': _L1_attn_in['proj_v'], 'L1_attn_proj_o': _L1_attn_in['proj_o'], 'L1_ffn_w_gate': _L1_ffn_in['w_gate'], 'L1_ffn_w_up': _L1_ffn_in['w_up'], 'L1_ffn_w_down': _L1_ffn_in['w_down']}
    _x0 = _d['L0_attn_X']
    _d['L0_attn_X'] = jax.random.normal(jax.random.fold_in(jax.random.key(seed), 1), (4, 512, 128), dtype=_x0.dtype)
    del _x0
    return _d

def reference(L0_attn_X, L0_attn_Wq, L0_attn_Wk, L0_attn_Wv, L0_ffn_wqkv, L0_ffn_q_scale, L0_ffn_k_scale, L0_ffn_wo, L0_ffn_ln_g, L0_ffn_ln_b, L0_ffn_w1, L0_ffn_b1, L0_ffn_w2, L0_ffn_b2, L1_attn_proj_q, L1_attn_proj_k, L1_attn_proj_v, L1_attn_proj_o, L1_ffn_w_gate, L1_ffn_w_up, L1_ffn_w_down):

    def _L0_attn_ref(X, Wq, Wk, Wv):
        import jax, jax.numpy as jnp
        import numpy as np
        import math
        D_MODEL = 128
        D_QUERY = 64
        B, T, _ = X.shape
        Q = X @ Wq
        K = X @ Wk
        V = X @ Wv
        scores = jnp.einsum('btd,bsd->bts', Q, K)
        causal = jnp.tril(jnp.ones((T, T), dtype=bool))
        scores = jnp.where(causal[None, :, :], scores, -jnp.inf)
        attn = jax.nn.softmax(scores / math.sqrt(D_QUERY), axis=2)
        return attn @ V

    def _L0_ffn_ref(x, wqkv, q_scale, k_scale, wo, ln_g, ln_b, w1, b1, w2, b2):
        import jax, jax.numpy as jnp
        import numpy as np
        DIM = 128
        DEPTH = 2
        HEADS = 8
        DIM_HEAD = 64
        WINDOW = 64
        INNER = HEADS * DIM_HEAD
        HID = int(DIM * 4 * 2 / 3)
        B, N = (2, 1024)
        QK_SCALE = 8.0

        def shift_token(t):
            t1, t2 = jnp.split(t, 2, axis=-1)
            t2 = jnp.pad(t2, ((0, 0), (1, 0), (0, 0)))[:, :-1]
            return jnp.concatenate([t1, t2], axis=-1)

        def l2norm(t):
            return t / jnp.clip(jnp.linalg.norm(t, axis=-1, keepdims=True), 1e-12)

        def rotate_half(x):
            x1, x2 = jnp.split(x, 2, axis=-1)
            return jnp.concatenate([-x2, x1], axis=-1)

        def rotary_xpos(q, k):
            n = q.shape[-2]
            half_idx = jnp.arange(0, DIM_HEAD, 2, dtype=jnp.float32)
            inv_freq = 1.0 / 10000.0 ** (half_idx / DIM_HEAD)
            t = jnp.arange(n, dtype=jnp.float32)
            freqs = t[:, None] * inv_freq[None, :]
            freqs = jnp.concatenate([freqs, freqs], axis=-1)
            base = (half_idx + 0.4 * DIM_HEAD) / (1.4 * DIM_HEAD)
            power = (t - n // 2) / float(WINDOW // 2)
            scale = base[None, :] ** power[:, None]
            scale = jnp.concatenate([scale, scale], axis=-1)
            cos, sin = (jnp.cos(freqs), jnp.sin(freqs))
            q = q * cos * scale + rotate_half(q) * sin * scale
            k = k * cos / scale + rotate_half(k) * sin / scale
            return (q, k)

        def local_attention(q, k, v):
            b, h, n, d = q.shape
            w = n // WINDOW
            bq = q.reshape(b, h, w, WINDOW, d) * QK_SCALE
            bk = k.reshape(b, h, w, WINDOW, d)
            bv = v.reshape(b, h, w, WINDOW, d)

            def look_around(t):
                p = jnp.pad(t, ((0, 0), (0, 0), (1, 0), (0, 0), (0, 0)))
                return jnp.concatenate([p[:, :, :w], p[:, :, 1:]], axis=3)
            bk, bv = (look_around(bk), look_around(bv))
            bt = jnp.arange(n).reshape(w, WINDOW)
            btp = jnp.pad(bt, ((1, 0), (0, 0)), constant_values=-1)
            btk = jnp.concatenate([btp[:w], btp[1:]], axis=1)
            sim = jnp.einsum('bhwid,bhwjd->bhwij', bq, bk)
            i = bt[:, :, None]
            j = btk[:, None, :]
            mask = (i < j) | (i > j + WINDOW) | (j == -1)
            sim = jnp.where(mask, -jnp.finfo(sim.dtype).max, sim)
            attn = jax.nn.softmax(sim, axis=-1)
            out = jnp.einsum('bhwij,bhwjd->bhwid', attn, bv)
            return out.reshape(b, h, n, d)

        def _layer(x, wqkv, qs, ksc, wo, lg, lb, w1, b1, w2, b2):
            b, n, _ = x.shape
            h = shift_token(x)
            qkv = h @ wqkv
            q, k, v = jnp.split(qkv, 3, axis=-1)
            to_heads = lambda t: t.reshape(b, n, HEADS, DIM_HEAD).transpose(0, 2, 1, 3)
            q, k, v = (to_heads(q), to_heads(k), to_heads(v))
            q = l2norm(q) * qs
            k = l2norm(k) * ksc
            q, k = rotary_xpos(q, k)
            o = local_attention(q, k, v)
            o = o.transpose(0, 2, 1, 3).reshape(b, n, INNER)
            x = x + o @ wo
            h = shift_token(x)
            mu = h.mean(-1, keepdims=True)
            var = h.var(-1, keepdims=True)
            h = (h - mu) / jnp.sqrt(var + 1e-05) * lg + lb
            h = h @ w1 + b1
            a, g = jnp.split(h, 2, axis=-1)
            h = a * jax.nn.gelu(g, approximate=False)
            x = x + h @ w2 + b2
            return x
        for l in range(DEPTH):
            x = _layer(x, wqkv[l], q_scale[l], k_scale[l], wo[l], ln_g[l], ln_b[l], w1[l], b1[l], w2[l], b2[l])
        return x

    def _L1_attn_ref(x, proj_q, proj_k, proj_v, proj_o):
        import jax, jax.numpy as jnp
        import numpy as np
        DIM_IN, DIM_K, DIM_V, N_QUERY = (128, 128, 128, 8)

        def _kaiming_uniform(key, shape):
            fan_in = shape[-2] if len(shape) > 1 else shape[-1]
            gain = 1.0 / np.sqrt(3.0)
            bound = gain * np.sqrt(3.0 / fan_in)
            return jax.random.uniform(key, shape, jnp.float32, -bound, bound)
        Q = jnp.einsum('bnd,hdk->bhnk', x, proj_q)
        K = jnp.einsum('bmd,dk->bmk', x, proj_k)
        V = jnp.einsum('bmd,dv->bmv', x, proj_v)
        logits = jnp.einsum('bhnk,bmk->bhnm', Q, K)
        weights = jax.nn.softmax(logits, axis=-1)
        O = jnp.einsum('bhnm,bmv->bhnv', weights, V)
        Y = jnp.einsum('bhnv,hdv->bnd', O, proj_o)
        return Y

    def _L1_ffn_ref(x, w_gate, w_up, w_down):
        import jax, jax.numpy as jnp
        import numpy as np
        DIM = 128
        HIDDEN = 384
        SCALE = 1.0 / 127.0

        def _dequant(w_int, dtype):
            return w_int.astype(dtype) * jnp.asarray(SCALE, dtype)
        wg = _dequant(w_gate, x.dtype)
        wu = _dequant(w_up, x.dtype)
        wd = _dequant(w_down, x.dtype)
        gate = jnp.einsum('bsd,hd->bsh', x, wg)
        up = jnp.einsum('bsd,hd->bsh', x, wu)
        h = jax.nn.silu(gate) * up
        return jnp.einsum('bsh,dh->bsd', h, wd)
    x = L0_attn_X
    xn = _layernorm(x, axis=-1)
    x = x + _L0_attn_ref(xn, L0_attn_Wq, L0_attn_Wk, L0_attn_Wv) + _L0_ffn_ref(xn, L0_ffn_wqkv, L0_ffn_q_scale, L0_ffn_k_scale, L0_ffn_wo, L0_ffn_ln_g, L0_ffn_ln_b, L0_ffn_w1, L0_ffn_b1, L0_ffn_w2, L0_ffn_b2)
    xn = _layernorm(x, axis=-1)
    x = x + _L1_attn_ref(xn, L1_attn_proj_q, L1_attn_proj_k, L1_attn_proj_v, L1_attn_proj_o) + _L1_ffn_ref(xn, L1_ffn_w_gate, L1_ffn_w_up, L1_ffn_w_down)
    return x

_drawn_inputs = setup_inputs


def setup_inputs(seed=0):
    import zlib

    import numpy as np

    out = dict(_drawn_inputs(seed))
    spreads = {'L0_ffn_q_scale': (1.0, 0.6),
     'L0_ffn_k_scale': (1.0, 0.6),
     'L0_ffn_ln_g': (1.0, 0.6),
     'L0_ffn_ln_b': (0.0, 0.8),
     'L0_ffn_b1': (0.0, 0.8),
     'L0_ffn_b2': (0.0, 0.1)}
    factors = {'L0_ffn_wqkv': 2.682,
     'L0_ffn_wo': 2.685,
     'L0_ffn_w1': 4.333,
     'L0_ffn_w2': 4.281,
     'L1_attn_proj_q': 8.0,
     'L1_attn_proj_k': 8.0,
     'L1_attn_proj_v': 8.0,
     'L1_attn_proj_o': 8.0}
    for name, (base, spread) in spreads.items():
        noise = np.random.default_rng([zlib.crc32(name.encode()), seed]).standard_normal(out[name].shape)
        drawn = base * np.exp(spread * noise) if base else spread * noise
        out[name] = jnp.asarray(drawn.astype(out[name].dtype))
    for name, factor in factors.items():
        out[name] = (out[name] * factor).astype(out[name].dtype)
    return out
```

```python
from contextlib import ExitStack

import concourse.bass as bass
from concourse import mybir

F32 = mybir.dt.float32
F32R = mybir.dt.float32r
BF16 = mybir.dt.bfloat16
I32 = mybir.dt.int32
ALU = mybir.AluOpType
ACT = mybir.ActivationFunctionType
AX_X = mybir.AxisListType.X

P = 128
B, N = 4, 512
NI = N // P
DQ = 64
DEPTH, HEADS, DH = 2, 8, 64
WIN = 64
NW = N // WIN
INNER = HEADS * DH
HID = 341
CH = [(0, 128), (128, 128), (256, 85)]
NQ = 8
FF = 384
FC = FF // P
MASKED = -1.0e30
LN_EPS = 1e-5
NORM_FLOOR = 1e-24
RSQRT_MAGIC = float(0x5F3759DF)
XB = 3
LAG = 3
NP = 4


def f32(ap):
    return ap.bitcast(F32)


class Ring:

    def __init__(self, order, uses_act, uses_dve):
        self.at = {job: j for j, job in enumerate(order)}
        self.order = order
        self.act, self.dve = {}, {}
        a = d = 0
        for job in order:
            if uses_act(job):
                a += 1
                self.act[job] = a
            if uses_dve(job):
                d += 1
                self.dve[job] = d

    def bank(self, job):
        return self.at[job] % XB

    def filled(self, job):
        return self.at[job] + 1

    def before(self, job):
        j = self.at[job] - XB
        return self.order[j] if j >= 0 else None


def split_matmul(nc, out, lhs, rhs, start=True, stop=True):
    (lh, ll), (rh, rl) = lhs, rhs
    nc.tensor.matmul(out, lh, rh, start=start, stop=False)
    nc.tensor.matmul(out, lh, rl, start=False, stop=False)
    return nc.tensor.matmul(out, ll, rh, start=False, stop=stop)


def chained(eng, sem, count):
    def link(ins):
        count[0] += 1
        ins.then_inc(sem, 1)
        eng.wait_ge(sem, count[0])
    return link


def rsqrt_on_dve(nc, link, v, y, t, n):
    link(nc.vector.tensor_scalar(y[:, 0:n].bitcast(I32), v[:, 0:n].bitcast(I32), 1, None,
                                 ALU.logical_shift_right))
    link(nc.vector.tensor_scalar(y[:, 0:n].bitcast(I32), y[:, 0:n].bitcast(I32), -1.0, RSQRT_MAGIC,
                                 ALU.mult, ALU.add))
    for _ in range(3):
        link(nc.vector.scalar_tensor_tensor(t[:, 0:n], y[:, 0:n], -0.5, y[:, 0:n], ALU.mult, ALU.mult))
        link(nc.vector.tensor_tensor(t[:, 0:n], t[:, 0:n], v[:, 0:n], ALU.mult))
        link(nc.vector.scalar_tensor_tensor(y[:, 0:n], t[:, 0:n], 1.5, y[:, 0:n], ALU.add, ALU.mult))


def attention_block(nc, tag, keep, io, causal):
    x_tok, xresT, ident = keep["x_tok"], keep["xresT"], keep["ident"]
    heads = 1 if causal else NQ
    jobs = [(b, h) for b in range(B) for h in range(heads)]
    tiles = [(j, i) for j in range(len(jobs)) for i in range(NI)]
    NT = len(tiles)

    before_slot = {g: [] for g in range(NT + LAG + 4)}
    pre = [("LN", b) for b in range(B)]
    if not causal:
        pre = [x for b in range(B) for x in (("X1", b), ("LN", b))]
    for j, (b, h) in enumerate(jobs):
        first = j * NI
        if h == 0:
            before_slot[max(first - 3, 0)].append(("K", b))
        before_slot[max(first - 1, 0)].append(("Q", j))
        if h == 0:
            before_slot[first].append(("V", b))
        before_slot[first + NI + LAG].append(("AV", j))
        if causal:
            before_slot[min(first + NI + LAG + 1, NT + LAG + 3)].append(("OT", j))
            if j in (1, 3):
                before_slot[first + 2].append(("W", j // 2))
        else:
            before_slot[min(first + NI + LAG + 1, NT + LAG + 3)].append(("OP", j))
            if h < 6 and h % 2 == 0:
                c = h // 2
                before_slot[first + 5].append(("GATE", b, c))
                before_slot[first + 6].append(("UP", b, c))
            if h == 5:
                before_slot[first + 9].append(("DOWN", b))
            if h == heads - 1:
                before_slot[min(first + NI + LAG + 1, NT + LAG + 3)].append(("YT", b))
    items = list(pre)
    for g in range(NT + LAG + 4):
        items += before_slot[g]
        items.append(("SLOT", g))
    in_ring = [x for x in items if x[0] not in ("SLOT", "OP", "DOWN", "W")]
    by_act = {"LN", "K", "V", "Q", "AV", "GATE"}
    by_dve = {"K", "V", "Q", "X1", "OT", "YT", "UP", "GATE"}
    if not causal:
        by_dve.add("AV")
    ring = Ring(in_ring, lambda x: x[0] in by_act, lambda x: x[0] in by_dve)

    with ExitStack() as ctx:
        def sb(name, shape, dt=F32):
            return ctx.enter_context(nc.sbuf_tensor(f"{tag}_{name}", shape, dt))

        def psum(name, shape):
            return ctx.enter_context(nc.psum_tensor(f"{tag}_{name}", shape, F32))

        def sem(name):
            return ctx.enter_context(nc.semaphore(f"{tag}_{name}"))

        scores = psum("scores", [P, 2, 512])
        wT_ps = psum("wT_ps", [P, 2, 512])
        bank = psum("bank", [P, XB, 512])
        y_ps = psum("y_ps", [P, 512])

        xn_tok = sb("xn_tok", [P, NI, P])
        stats = sb("stats", [P, NI, 6])
        mv = sb("mv", [P, NI, 2])
        var = sb("var", [P, NI])
        rstd = sb("rstd", [P, NI])
        newton = sb("newton", [P, NI])
        xnT = xresT if causal else sb("xnT", [P, B, N])
        xh, xl = sb("xh", [P, B, N], F32R), sb("xl", [P, B, N], F32R)
        QH, QL = sb("QH", [P, 2, N], F32R), sb("QL", [P, 2, N], F32R)
        KH = sb("KH", [P, 2, N], F32R)
        KL = None if causal else sb("KL", [P, 2, N], F32R)
        VH, VL = sb("VH", [P, 2, NI, P], F32R), sb("VL", [P, 2, NI, P], F32R)
        negmax = sb("negmax", [P, 8])
        rowsum = sb("rowsum", [P, 8])
        inv = sb("inv", [P, 8])
        weights = sb("weights", [P, NP, N])
        WH, WL = sb("WH", [P, 2, NI, N], F32R), sb("WL", [P, 2, NI, N], F32R)
        oT = sb("oT", [P, N])
        if causal:
            raw = sb("raw", [P, W_LAYER])
            qk_raw = sb("qk_raw", [P, 2, P])
            wqk_h, wqk_l = sb("wqk_h", [P, 2, P], F32R), sb("wqk_l", [P, 2, P], F32R)
            wv = sb("wv", [P, P])
            mask32 = sb("mask32", [P, 3, P])
            h32 = keep["h32"]
            tab = sb("tab", [P, 2, 2, NI, DH])
            scl = sb("scl", [P, DEPTH, 2, 2, DH])
        else:
            nw = io["w_all"].shape[1]
            raw = sb("raw", [P, nw])
            w_h, w_l = sb("w_h", [P, nw], F32R), sb("w_l", [P, nw], F32R)
            int_w = sb("int_w", [P, 3 * FF], I32)
            wv = sb("wv", [P, P])
            OH, OL = sb("OH", [P, 2, N], F32R), sb("OL", [P, 2, N], F32R)
            tanh_g = sb("tanh_g", [P, N])
            silu_g = sb("silu_g", [P, 2, N])
            hid = sb("hid", [P, N])
            HH, HL = sb("HH", [P, FC, N], F32R), sb("HL", [P, FC, N], F32R)
            out_tok = sb("out_tok", [P, 2, NI, P])

        x_loaded = [sem(f"x_loaded{b}") for b in range(B)]
        consts_loaded = sem("consts_loaded")
        w_loaded = sem("w_loaded")
        w_split = sem("w_split")
        dve_link = sem("dve_link")
        consts_ready = sem("consts_ready")
        zeros_ready = sem("zeros_ready")
        xn_ready = sem("xn_ready")
        xT_split = sem("xT_split")
        bank_filled = sem("bank_filled")
        act_used = sem("act_used")
        dve_used = sem("dve_used")
        scores_ready = sem("scores_ready")
        max_ready = sem("max_ready")
        exp_ready = sem("exp_ready")
        inv_ready = sem("inv_ready")
        weights_ready = sem("weights_ready")
        wT_ready = sem("wT_ready")
        high_ready = sem("high_ready")
        low_ready = sem("low_ready")
        out_proj_done = sem("out_proj_done")
        y_taken = sem("y_taken")
        down_done = sem("down_done")
        stored = [sem(f"stored{k}") for k in range(2)]

        if not causal:
            wq_c = lambda w, h: w[:, h * P:(h + 1) * P]
            wk_c = lambda w: w[:, NQ * P:(NQ + 1) * P]
            wo_c = lambda w, h: w[:, (NQ + 1 + h) * P:(NQ + 2 + h) * P]
            g0 = (2 * NQ + 1) * P
            wg_c = lambda w, c: w[:, g0 + c * P:g0 + (c + 1) * P]
            wu_c = lambda w, c: w[:, g0 + FF + c * P:g0 + FF + (c + 1) * P]
            wd_c = lambda w, c: w[:, g0 + 2 * FF + c * P:g0 + 2 * FF + (c + 1) * P]

        with nc.Block() as block:

            @block.sync
            def _(sp):
                if causal:
                    for b in range(B):
                        sp.dma_start(x_tok[:, b * NI:(b + 1) * NI, :],
                                     io["x"][b].rearrange("(i p) d -> p i d", p=P)).then_inc(x_loaded[b], 16)
                    sp.dma_start(ident[:], io["ident"]).then_inc(consts_loaded, 16)
                    sp.dma_start(mask32[:], io["masks"]).then_inc(consts_loaded, 16)
                    sp.dma_start(tab[:], io["rotary"]).then_inc(consts_loaded, 16)
                    sp.dma_start(scl[:], io["qk_scales"]).then_inc(consts_loaded, 16)
                    sp.dma_start(keep["cols"][:], io["cols"]).then_inc(consts_loaded, 16)
                    for m in range(2):
                        for r in range(2):
                            sp.dma_start(qk_raw[:, m, r * DQ:(r + 1) * DQ], (io["Wq"], io["Wk"])[m])\
                              .then_inc(consts_loaded, 16)
                    sp.dma_start(wv[:], io["Wv"]).then_inc(consts_loaded, 16)
                    for l in range(DEPTH):
                        if l:
                            sp.wait_ge(w_split, 2 * l)
                        sp.dma_start(raw[:], io["w_all"][:, l * W_LAYER:(l + 1) * W_LAYER]).then_inc(w_loaded, 16)
                else:
                    sp.dma_start(wv[:], io["Wv"]).then_inc(consts_loaded, 16)
                    sp.dma_start(raw[:, 0:g0], io["w_all"][:, 0:g0]).then_inc(w_loaded, 16)
                    sp.dma_start(int_w[:], io["w_int"]).then_inc(w_loaded, 16)
                    for b in range(B):
                        sp.wait_ge(dve_used, ring.dve[("YT", b)])
                        sp.dma_start(io["out"][b].rearrange("(i p) d -> p i d", p=P),
                                     out_tok[:, b % 2]).then_inc(stored[b % 2], 16)
                    for k in range(2):
                        sp.wait_ge(stored[k], 16 * B // 2)

            @block.gpsimd
            def _(pool):
                if causal:
                    nc.gpsimd.memset(WH[:, :, NI - 1, 2 * P:3 * P].bitcast(F32), 0.0).then_inc(zeros_ready, 1)
                    nc.gpsimd.memset(WL[:, :, NI - 1, 2 * P:3 * P].bitcast(F32), 0.0).then_inc(zeros_ready, 1)
                    nc.gpsimd.memset(h32[:], 0.0).then_inc(zeros_ready, 1)
                for item in items:
                    if item[0] != "SLOT":
                        continue
                    T = item[1] - 1
                    if 0 <= T < NT:
                        j, i = tiles[T]
                        n = P * (i + 1) if causal else N
                        pool.wait_ge(inv_ready, T + 1)
                        w = weights[:, T % NP, 0:n]
                        nc.gpsimd.tensor_tensor(w, w, inv[:, T % 8:T % 8 + 1].to_broadcast([P, n]), ALU.mult)\
                            .then_inc(weights_ready, 1)

            @block.scalar
            def _(act):
                for item in items:
                    kind = item[0]
                    if kind in by_act:
                        act.wait_ge(bank_filled, ring.filled(item))
                        ps = bank[:, ring.bank(item), :]
                    if kind == "LN":
                        b = item[1]
                        nc.scalar.copy(xnT[:, b, :], ps).then_inc(act_used, 1)
                    elif kind == "K":
                        b = item[1]
                        if b >= 2:
                            act.wait_ge(scores_ready, (b - 1) * heads * NI)
                        nc.scalar.copy(KH[:, b % 2, :], ps).then_inc(act_used, 1)
                    elif kind == "V":
                        b = item[1]
                        if b >= 2:
                            act.wait_ge(bank_filled, ring.filled(("AV", (b - 1) * heads - 1)))
                        nc.scalar.copy(VH[:, b % 2], ps).then_inc(act_used, 1)
                    elif kind == "Q":
                        j = item[1]
                        if j >= 2:
                            act.wait_ge(scores_ready, (j - 1) * NI)
                        nc.scalar.activation(QH[:, j % 2, :], ps, ACT.Copy, scale=0.125 if causal else 1.0)\
                            .then_inc(act_used, 1)
                    elif kind == "AV":
                        j = item[1]
                        if causal:
                            if j >= 1:
                                act.wait_ge(bank_filled, ring.filled(("OT", j - 1)))
                            nc.scalar.copy(oT[:], ps).then_inc(act_used, 1)
                        else:
                            if j >= 2:
                                act.wait_ge(out_proj_done, j - 1)
                            nc.scalar.copy(OH[:, j % 2, :], ps).then_inc(act_used, 1)
                    elif kind == "GATE":
                        _, b, c = item
                        if b or c:
                            last = (b, c - 1) if c else (b - 1, FC - 1)
                            act.wait_ge(dve_used, ring.dve[("GATE", *last)])
                        nc.scalar.activation(tanh_g[:], ps, ACT.Tanh, scale=0.5).then_inc(act_used, 1)
                    elif kind == "YT" and not causal:
                        b = item[1]
                        act.wait_ge(out_proj_done, NQ * (b + 1))
                        if b >= 1:
                            act.wait_ge(bank_filled, ring.filled(("YT", b - 1)))
                        nc.scalar.copy(oT[:], y_ps[:]).then_inc(y_taken, 1)
                    elif kind == "SLOT":
                        g = item[1]
                        if LAG <= g < NT + LAG:
                            T = g - LAG
                            j, i = tiles[T]
                            n = i + 1 if causal else NI
                            act.wait_ge(wT_ready, T + 1)
                            if j >= 2:
                                act.wait_ge(bank_filled, ring.filled(("AV", j - 2)))
                            nc.scalar.copy(WH[:, j % 2, 0:n, i * P:(i + 1) * P],
                                           wT_ps[:, T % 2, 0:n * P].rearrange("p (k q) -> p k q", q=P))\
                                .then_inc(high_ready, 1)
                        if g < NT:
                            T = g
                            i = tiles[T][1]
                            n = P * (i + 1) if causal else N
                            act.wait_ge(max_ready, T + 1)
                            if T >= NP:
                                act.wait_ge(wT_ready, T - NP + 1)
                            nc.scalar.activation(weights[:, T % NP, 0:n], scores[:, T % 2, 0:n], ACT.Exp,
                                                 bias=negmax[:, T % 8:T % 8 + 1],
                                                 accum_out=rowsum[:, T % 8:T % 8 + 1]).then_inc(exp_ready, 1)

            @block.vector
            def _(dve):
                link = chained(dve, dve_link, [0])

                def layernorm(b):
                    for i in range(NI):
                        link(nc.vector.bn_stats(stats[:, i, :], x_tok[:, b * NI + i, :]))
                    for i in range(NI):
                        link(nc.vector.bn_aggr(mv[:, i, :], stats[:, i, :]))
                    link(nc.vector.tensor_scalar(var[:], mv[:, :, 1], LN_EPS, None, ALU.add))
                    rsqrt_on_dve(nc, link, var, rstd, newton, NI)
                    if b >= 1:
                        dve.wait_ge(bank_filled, ring.filled(("LN", b - 1)))
                    for i in range(NI):
                        nc.vector.tensor_scalar(xn_tok[:, i, :], x_tok[:, b * NI + i, :], mv[:, i, 0:1],
                                                rstd[:, i:i + 1], ALU.subtract, ALU.mult).then_inc(xn_ready, 1)
                    dve.wait_ge(xn_ready, NI * (b + 1))

                if causal:
                    dve.wait_ge(consts_loaded, 16 * 10)
                    nc.vector.tensor_copy(keep["ident_bf"][:], ident[:]).then_inc(consts_ready, 1)
                    nc.vector.tensor_copy(keep["masks"][:], mask32[:]).then_inc(consts_ready, 1)
                    nc.vector.tensor_copy(wqk_h[:], qk_raw[:]).then_inc(consts_ready, 1)
                    dve.wait_ge(consts_ready, 3)
                    nc.vector.tensor_tensor(wqk_l[:], qk_raw[:], f32(wqk_h[:]), ALU.subtract)\
                        .then_inc(consts_ready, 1)
                    for l in range(DEPTH):
                        for m in range(2):
                            for r in range(2):
                                nc.vector.tensor_tensor(
                                    keep["tables"][:, l, r, m], tab[:, r, m],
                                    scl[:, l, m, r:r + 1, :].to_broadcast([P, NI, DH]), ALU.mult)\
                                    .then_inc(consts_ready, 1)
                    for b in range(B):
                        dve.wait_ge(x_loaded[b], 16)
                n_const = 4 + 8
                if not causal:
                    dve.wait_ge(w_loaded, 32)
                    link(nc.vector.tensor_copy(raw[:, g0:], int_w[:]))
                    link(nc.vector.tensor_scalar(raw[:, g0:], raw[:, g0:], 1.0 / 127.0, None, ALU.mult))
                    link(nc.vector.tensor_copy(w_h[:], raw[:]))
                    nc.vector.tensor_tensor(w_l[:], raw[:], f32(w_h[:]), ALU.subtract).then_inc(consts_ready, 1)

                for item in items:
                    kind = item[0]
                    if kind == "LN" :
                        b = item[1]
                        layernorm(b)
                        dve.wait_ge(act_used, ring.act[item])
                        nc.vector.tensor_copy(xh[:, b, :], xnT[:, b, :]).then_inc(xT_split, 1)
                        dve.wait_ge(xT_split, 2 * b + 1)
                        nc.vector.tensor_tensor(xl[:, b, :], xnT[:, b, :], f32(xh[:, b, :]), ALU.subtract)\
                            .then_inc(xT_split, 1)
                        if causal:
                            dve.wait_ge(zeros_ready, 3)
                            link(nc.vector.tensor_copy(h32[0:64, 0:N], xnT[0:64, b, :]))
                            link(nc.vector.tensor_copy(h32[64:128, 1:N + 1], xnT[64:128, b, :]))
                            link(nc.vector.tensor_copy(keep["hh"][:, b, :], h32[:, 0:N]))
                            link(nc.vector.tensor_tensor(keep["hl"][:, b, :], h32[:, 0:N],
                                                         f32(keep["hh"][:, b, :]), ALU.subtract))
                    elif kind == "W":
                        l = item[1]
                        dve.wait_ge(w_loaded, 16 * (l + 1))
                        cs = slice(l * W_LAYER, (l + 1) * W_LAYER)
                        nc.vector.tensor_copy(keep["w_h"][:, cs], raw[:]).then_inc(w_split, 1)
                        dve.wait_ge(w_split, 2 * l + 1)
                        nc.vector.tensor_tensor(keep["w_l"][:, cs], raw[:], f32(keep["w_h"][:, cs]),
                                                ALU.subtract).then_inc(w_split, 1)
                    elif kind == "X1":
                        b = item[1]
                        dve.wait_ge(bank_filled, ring.filled(item))
                        xt = x_tok[:, b * NI:(b + 1) * NI, :]
                        nc.vector.tensor_tensor(xt, bank[:, ring.bank(item), :].rearrange("p (i d) -> p i d", d=P),
                                                xt, ALU.add).then_inc(dve_used, 1)
                        dve.wait_ge(dve_used, ring.dve[item])
                    elif kind == "K":
                        b = item[1]
                        dve.wait_ge(act_used, ring.act[item])
                        ps = bank[:, ring.bank(item), :]
                        if causal:
                            nc.vector.tensor_tensor(KH[64:128, b % 2, :], ps[64:128, :],
                                                    f32(KH[64:128, b % 2, :]), ALU.subtract)\
                                .then_inc(dve_used, 1)
                        else:
                            nc.vector.tensor_tensor(KL[:, b % 2, :], ps, f32(KH[:, b % 2, :]), ALU.subtract)\
                                .then_inc(dve_used, 1)
                    elif kind == "V":
                        b = item[1]
                        dve.wait_ge(act_used, ring.act[item])
                        nc.vector.tensor_tensor(VL[:, b % 2], bank[:, ring.bank(item), :]
                                                .rearrange("p (i d) -> p i d", d=P), f32(VH[:, b % 2]),
                                                ALU.subtract).then_inc(dve_used, 1)
                    elif kind == "Q":
                        j = item[1]
                        dve.wait_ge(act_used, ring.act[item])
                        nc.vector.scalar_tensor_tensor(QL[:, j % 2, :], bank[:, ring.bank(item), :],
                                                       0.125 if causal else 1.0, f32(QH[:, j % 2, :]),
                                                       ALU.mult, ALU.subtract).then_inc(dve_used, 1)
                    elif kind == "AV" and not causal:
                        j = item[1]
                        dve.wait_ge(act_used, ring.act[item])
                        nc.vector.tensor_tensor(OL[:, j % 2, :], bank[:, ring.bank(item), :],
                                                f32(OH[:, j % 2, :]), ALU.subtract).then_inc(dve_used, 1)
                    elif kind == "OT":
                        j = item[1]
                        dve.wait_ge(bank_filled, ring.filled(item))
                        xt = x_tok[:, j * NI:(j + 1) * NI, :]
                        nc.vector.tensor_tensor(xt, bank[:, ring.bank(item), :].rearrange("p (i d) -> p i d", d=P),
                                                xt, ALU.add).then_inc(dve_used, 1)
                    elif kind == "GATE":
                        _, b, c = item
                        dve.wait_ge(act_used, ring.act[item])
                        if b or c >= 2:
                            k = b * FC + c - 2
                            if k >= 0:
                                dve.wait_ge(dve_used, ring.dve[("UP", k // FC, k % FC)])
                        nc.vector.scalar_tensor_tensor(silu_g[:, (b * FC + c) % 2, :], tanh_g[:], 1.0,
                                                       bank[:, ring.bank(item), :], ALU.add, ALU.mult)\
                            .then_inc(dve_used, 1)
                    elif kind == "UP":
                        _, b, c = item
                        dve.wait_ge(bank_filled, ring.filled(item))
                        dve.wait_ge(dve_used, ring.dve[("GATE", b, c)])
                        if b >= 1:
                            dve.wait_ge(down_done, b)
                        link(nc.vector.scalar_tensor_tensor(hid[:], silu_g[:, (b * FC + c) % 2, :], 0.5,
                                                            bank[:, ring.bank(item), :], ALU.mult, ALU.mult))
                        link(nc.vector.tensor_copy(HH[:, c, :], hid[:]))
                        nc.vector.tensor_tensor(HL[:, c, :], hid[:], f32(HH[:, c, :]), ALU.subtract)\
                            .then_inc(dve_used, 1)
                        dve.wait_ge(dve_used, ring.dve[item])
                    elif kind == "YT":
                        b = item[1]
                        dve.wait_ge(bank_filled, ring.filled(item))
                        if b >= 2:
                            dve.wait_ge(stored[b % 2], 16 * (b // 2))
                        nc.vector.tensor_tensor(out_tok[:, b % 2], bank[:, ring.bank(item), :]
                                                .rearrange("p (i d) -> p i d", d=P),
                                                x_tok[:, b * NI:(b + 1) * NI, :], ALU.add)\
                            .then_inc(dve_used, 1)
                    elif kind == "SLOT":
                        g = item[1]
                        if g < NT:
                            T = g
                            i = tiles[T][1]
                            n = P * (i + 1) if causal else N
                            dve.wait_ge(scores_ready, T + 1)
                            if T >= 8:
                                dve.wait_ge(exp_ready, T - 7)
                            nc.vector.tensor_reduce(negmax[:, T % 8:T % 8 + 1], scores[:, T % 2, 0:n], AX_X,
                                                    ALU.max, negate=True).then_inc(max_ready, 1)
                        if 1 <= g <= NT:
                            T = g - 1
                            dve.wait_ge(exp_ready, T + 1)
                            if T >= 8:
                                dve.wait_ge(weights_ready, T - 7)
                            nc.vector.reciprocal(inv[:, T % 8:T % 8 + 1], rowsum[:, T % 8:T % 8 + 1])\
                                .then_inc(inv_ready, 1)
                        if LAG <= g < NT + LAG:
                            T = g - LAG
                            j, i = tiles[T]
                            n = i + 1 if causal else NI
                            dve.wait_ge(high_ready, T + 1)
                            nc.vector.tensor_tensor(WL[:, j % 2, 0:n, i * P:(i + 1) * P],
                                                    wT_ps[:, T % 2, 0:n * P].rearrange("p (k q) -> p k q", q=P),
                                                    f32(WH[:, j % 2, 0:n, i * P:(i + 1) * P]), ALU.subtract)\
                                .then_inc(low_ready, 1)

            @block.tensor
            def _(pe):
                def claim(item):
                    old = ring.before(item)
                    if old is not None:
                        if old in ring.dve:
                            pe.wait_ge(dve_used, ring.dve[old])
                        if old in ring.act:
                            pe.wait_ge(act_used, ring.act[old])
                    return bank[:, ring.bank(item), :]

                if causal:
                    pe.wait_ge(consts_loaded, 16 * 10)
                    pe.wait_ge(consts_ready, 4)
                else:
                    pe.wait_ge(consts_loaded, 16)
                for item in items:
                    kind = item[0]
                    if kind == "LN":
                        b = item[1]
                        ps = claim(item)
                        pe.wait_ge(xn_ready, NI * (b + 1))
                        for i in range(NI):
                            last = nc.tensor.transpose(ps[:, i * P:(i + 1) * P], xn_tok[:, i, :], ident[:])
                        last.then_inc(bank_filled, 1)
                    elif kind == "X1":
                        b = item[1]
                        ps = claim(item)
                        for i in range(NI):
                            last = nc.tensor.transpose(ps[:, i * P:(i + 1) * P],
                                                       xresT[:, b, i * P:(i + 1) * P], ident[:])
                        last.then_inc(bank_filled, 1)
                    elif kind == "K":
                        b = item[1]
                        ps = claim(item)
                        pe.wait_ge(xT_split, 2 * (b + 1))
                        if causal:
                            w = (wqk_h[:, 1, :], wqk_l[:, 1, :])
                        else:
                            pe.wait_ge(consts_ready, 1)
                            w = (wk_c(w_h), wk_c(w_l))
                        split_matmul(nc, ps, w, (xh[:, b, :], xl[:, b, :])).then_inc(bank_filled, 1)
                    elif kind == "V":
                        b = item[1]
                        ps = claim(item)
                        for i in range(NI):
                            last = nc.tensor.matmul(ps[:, i * P:(i + 1) * P], xnT[:, b, i * P:(i + 1) * P],
                                                    wv[:], start=True, stop=True)
                        last.then_inc(bank_filled, 1)
                    elif kind == "Q":
                        b, h = jobs[item[1]]
                        ps = claim(item)
                        w = (wqk_h[:, 0, :], wqk_l[:, 0, :]) if causal else (wq_c(w_h, h), wq_c(w_l, h))
                        split_matmul(nc, ps, w, (xh[:, b, :], xl[:, b, :])).then_inc(bank_filled, 1)
                    elif kind == "AV":
                        j = item[1]
                        b = jobs[j][0]
                        ps = claim(item)
                        pe.wait_ge(low_ready, NI * (j + 1))
                        pe.wait_ge(dve_used, ring.dve[("V", b)])
                        if causal:
                            pe.wait_ge(zeros_ready, 2)
                        for k in range(NI):
                            q0 = min(P * k, N - 2 * P) if causal else 0
                            last = split_matmul(nc, ps[:, q0:N], (VH[:, b % 2, k, :], VL[:, b % 2, k, :]),
                                                (WH[:, j % 2, k, q0:N], WL[:, j % 2, k, q0:N]),
                                                start=k == 0, stop=k == NI - 1)
                        last.then_inc(bank_filled, 1)
                    elif kind == "OT":
                        ps = claim(item)
                        pe.wait_ge(act_used, ring.act[("AV", item[1])])
                        for i in range(NI):
                            last = nc.tensor.transpose(ps[:, i * P:(i + 1) * P], oT[:, i * P:(i + 1) * P], ident[:])
                        last.then_inc(bank_filled, 1)
                    elif kind == "OP":
                        j = item[1]
                        b, h = jobs[j]
                        pe.wait_ge(dve_used, ring.dve[("AV", j)])
                        if h == 0 and b >= 1:
                            pe.wait_ge(y_taken, b)
                        ins = split_matmul(nc, y_ps[:], (wo_c(w_h, h), wo_c(w_l, h)),
                                           (OH[:, j % 2, :], OL[:, j % 2, :]), start=h == 0, stop=h == NQ - 1)
                        ins.then_inc(out_proj_done, 1)
                    elif kind in ("GATE", "UP"):
                        _, b, c = item
                        ps = claim(item)
                        wc = wg_c if kind == "GATE" else wu_c
                        split_matmul(nc, ps, (wc(w_h, c), wc(w_l, c)), (xh[:, b, :], xl[:, b, :]))\
                            .then_inc(bank_filled, 1)
                    elif kind == "DOWN":
                        b = item[1]
                        pe.wait_ge(dve_used, ring.dve[("UP", b, FC - 1)])
                        for c in range(FC):
                            last = split_matmul(nc, y_ps[:], (wd_c(w_h, c), wd_c(w_l, c)),
                                                (HH[:, c, :], HL[:, c, :]), start=False, stop=False)
                        last.then_inc(down_done, 1)
                    elif kind == "YT":
                        b = item[1]
                        ps = claim(item)
                        pe.wait_ge(y_taken, b + 1)
                        for i in range(NI):
                            last = nc.tensor.transpose(ps[:, i * P:(i + 1) * P], oT[:, i * P:(i + 1) * P], ident[:])
                        last.then_inc(bank_filled, 1)
                    elif kind == "SLOT":
                        g = item[1]
                        if LAG <= g < NT + LAG:
                            T = g - LAG
                            j, i = tiles[T]
                            n = i + 1 if causal else NI
                            pe.wait_ge(weights_ready, T + 1)
                            if T >= 2:
                                pe.wait_ge(low_ready, T - 1)
                            for k in range(n):
                                last = nc.tensor.transpose(wT_ps[:, T % 2, k * P:(k + 1) * P],
                                                           weights[:, T % NP, k * P:(k + 1) * P], ident[:])
                            last.then_inc(wT_ready, 1)
                        if g < NT:
                            T = g
                            j, i = tiles[T]
                            b = jobs[j][0]
                            pe.wait_ge(dve_used, ring.dve[("Q", j)])
                            if T >= 2:
                                pe.wait_ge(exp_ready, T - 1)
                            qh, ql = QH[:, j % 2, i * P:(i + 1) * P], QL[:, j % 2, i * P:(i + 1) * P]
                            if causal:
                                n = max(P * (i + 1), 2 * P)
                                ps = scores[:, T % 2, 0:n]
                                nc.tensor.matmul(ps, qh, KH[:, b % 2, 0:n], start=True, stop=False)
                                nc.tensor.matmul(ps, ql, KH[:, b % 2, 0:n], start=False, stop=False)
                                nc.tensor.matmul(scores[:, T % 2, i * P:(i + 1) * P], keep["ident_bf"][:],
                                                 keep["masks"][:, 0, :], start=False, stop=True)\
                                    .then_inc(scores_ready, 1)
                            else:
                                split_matmul(nc, scores[:, T % 2, :], (qh, ql),
                                             (KH[:, b % 2, :], KL[:, b % 2, :])).then_inc(scores_ready, 1)


W_LAYER = 3 * INNER + 4 * P + 2 * HID + 3 * P
COLS = 3 + 6


def windowed_block(nc, keep):
    tag = "win"
    xresT, hh, hl, h32, ident = keep["xresT"], keep["hh"], keep["hl"], keep["h32"], keep["ident"]
    cols = keep["cols"]
    S = DEPTH * B
    U = 2 * S
    TU = NW // 2
    NT = U * TU
    unit_step = lambda u: u // 2
    LAST = NT + LAG + 12

    before = {g: [] for g in range(LAST)}
    for u in range(U):
        at = TU * (u - 1)
        for i in range(NI):
            before[max(at + i // 2, 0)].append(("QK", u, i))
            before[TU * u + i // 2].append(("VP", u, i))
        before[max(at + 1, 0)].append(("NORM", u))
        for m in range(2):
            for p in range(2):
                before[TU * u].append(("QT", u, m, p))
    for g in range(0, NT, TU):
        before[g].sort(key=lambda x: (x[0] in ("VP",), x[0] == "QK" and x[1] * TU > g))
    for s in range(S):
        at = 2 * TU * s + 2 * TU - 1 + LAG + 2
        before[at].append(("WO", s))
        before[at + 1].append(("LT", s))
        before[at + 2].append(("LB", s))
        before[at + 3] += [("G", s, c) for c in range(3)]
        before[at + 4] += [("A", s, c) for c in range(3)]
        before[at + 5].append(("W2", s))
    for g in range(NT):
        before[g + LAG + 1].append(("AV", g))
    items = [x for g in range(LAST) for x in before[g] + [("SLOT", g)]]
    acts = {"QK", "VP", "AV", "LB", "G"}
    dves = {"QK", "AV", "WO", "LT", "A", "W2"}
    ring = Ring([x for x in items if x[0] not in ("SLOT", "NORM")],
                lambda x: x[0] in acts or x[0] == "QT" and x[2] == 0,
                lambda x: x[0] in dves or x[0] == "QT" and x[2] == 1)

    def layer_w(w, l):
        o = l * W_LAYER
        qkv = w[:, o:o + 3 * INNER].rearrange("p (m n) -> p m n", m=3)
        wo = w[:, o + 3 * INNER:o + 3 * INNER + 4 * P].rearrange("p (c n) -> p c n", c=4)
        o += 3 * INNER + 4 * P
        w1 = w[:, o:o + 2 * HID]
        w2 = w[:, o + 2 * HID:o + 2 * HID + 3 * P].rearrange("p (c n) -> p c n", c=3)
        return qkv, wo, w1, w2

    LWH = [layer_w(keep["w_h"], l) for l in range(DEPTH)]
    LWL = [layer_w(keep["w_l"], l) for l in range(DEPTH)]

    with ExitStack() as ctx:
        def sb(name, shape, dt=F32):
            return ctx.enter_context(nc.sbuf_tensor(f"{tag}_{name}", shape, dt))

        def psum(name, shape):
            return ctx.enter_context(nc.psum_tensor(f"{tag}_{name}", shape, F32))

        def sem(name):
            return ctx.enter_context(nc.semaphore(f"{tag}_{name}"))

        scores = psum("scores", [P, 2, 4 * P])
        wT_ps = psum("wT_ps", [P, 2, 4 * P])
        bank = psum("bank", [P, XB, 512])
        QBD = sb("QBD", [P, 2, 2, NW, 2, WIN])
        KT = sb("KT", [P, 2, 2, N])
        V = sb("V", [P, 2, NW - 1, 2 * P])
        rot = sb("rot", [P, NI, 2 * 2 * P])
        rot_a = sb("rot_a", [P, 2, 512])
        rot_b = sb("rot_b", [P, 2, 512])
        sq = sb("sq", [P, 2, 512])
        sumsq = sb("sumsq", [P, 2, 32])
        norm_inv = sb("norm_inv", [P, 2, 32])
        newton = sb("newton", [P, 32])
        negmax = sb("negmax", [P, 8, 4])
        rowsum = sb("rowsum", [P, 8, 4])
        inv = sb("inv", [P, 8, 4])
        weights = sb("weights", [P, NP, 4 * P])
        wT = sb("wT", [P, 2, 4 * P])
        OTH, OTL = sb("OTH", [P, 4, N], F32R), sb("OTL", [P, 4, N], F32R)
        stats = sb("stats", [P, NI, 6])
        mv = sb("mv", [P, NI, 2])
        var = sb("var", [P, NI])
        rstd = sb("rstd", [P, NI])
        hn = sb("hn", [P, NI, P])
        n32 = sb("n32", [P, N])
        nH, nL = sb("nH", [P, N], F32R), sb("nL", [P, N], F32R)
        gelu_g = sb("gelu_g", [P, 3, N])
        hid = sb("hid", [P, N])
        HH, HL = sb("HH", [P, 3, N], F32R), sb("HL", [P, 3, N], F32R)

        dve_link = sem("dve_link")
        zeros_ready = sem("zeros_ready")
        bank_filled = sem("bank_filled")
        act_used = sem("act_used")
        dve_used = sem("dve_used")
        sumsq_done = sem("sumsq_done")
        rot_added = sem("rot_added")
        norm_ready = sem("norm_ready")
        norm_applied = sem("norm_applied")
        scores_ready = sem("scores_ready")
        max_ready = sem("max_ready")
        exp_ready = sem("exp_ready")
        inv_ready = sem("inv_ready")
        weights_ready = sem("weights_ready")
        wT_ready = sem("wT_ready")
        wT_copied = sem("wT_copied")
        h32_ready = sem("h32_ready")
        n_ready = sem("n_ready")
        hid_ready = sem("hid_ready")
        h_split = sem("h_split")

        with nc.Block() as block:

            @block.gpsimd
            def _(pool):
                nc.gpsimd.memset(QBD[:], 0.0).then_inc(zeros_ready, 1)
                for item in items:
                    kind = item[0]
                    if kind == "QK":
                        _, u, i = item
                        n = NI * u + i
                        pool.wait_ge(dve_used, ring.dve[item])
                        if u >= 1:
                            pool.wait_ge(bank_filled, ring.filled(("QT", u - 1, 1, 1)))
                        nc.gpsimd.tensor_tensor(rot[:, i, :], rot_a[:, n % 2, :], rot_b[:, n % 2, :], ALU.add)\
                            .then_inc(rot_added, 1)
                    elif kind == "NORM":
                        u = item[1]
                        pool.wait_ge(norm_ready, u + 1)
                        pool.wait_ge(rot_added, NI * (u + 1))
                        for i in range(NI):
                            r = rot[:, i, :].rearrange("p (h d) -> p h d", d=DH)
                            k = norm_inv[:, u % 2, 8 * i:8 * i + 8].unsqueeze(2).to_broadcast([P, 8, DH])
                            nc.gpsimd.tensor_tensor(r, r, k, ALU.mult).then_inc(norm_applied, 1)
                    elif kind == "SLOT":
                        T = item[1] - 1
                        if 0 <= T < NT:
                            pool.wait_ge(inv_ready, T + 1)
                            w = weights[:, T % NP, :].rearrange("p (c k) -> p c k", k=P)
                            k = inv[:, T % 8, :].unsqueeze(2).to_broadcast([P, 4, P])
                            nc.gpsimd.tensor_tensor(w, w, k, ALU.mult).then_inc(weights_ready, 1)

            @block.scalar
            def _(act):
                h32_count = 0

                def shifted(b):
                    nc.scalar.copy(h32[0:64, 0:N], xresT[0:64, b, :])
                    nc.scalar.copy(h32[64:128, 1:N + 1], xresT[64:128, b, :]).then_inc(h32_ready, 1)

                for item in items:
                    kind = item[0]
                    if item in ring.act:
                        act.wait_ge(bank_filled, ring.filled(item))
                        ps = bank[:, ring.bank(item), :]
                    if kind == "QK":
                        _, u, i = item
                        n = NI * u + i
                        if n >= 2:
                            act.wait_ge(sumsq_done, n - 1)
                        nc.scalar.activation(sq[:, n % 2, :], ps, ACT.Square).then_inc(act_used, 1)
                    elif kind == "VP":
                        _, u, v = item
                        if u >= 2:
                            act.wait_ge(bank_filled, ring.filled(("AV", TU * (u - 1) - 1)))
                        n = 2 if v < NI - 1 else 1
                        nc.scalar.copy(V[:, u % 2, 2 * v:2 * v + n, :],
                                       ps[:, 0:n * 2 * P].rearrange("p (j d) -> p j d", j=n)).then_inc(act_used, 1)
                    elif kind == "QT" and item[2] == 0:
                        _, u, _, p = item
                        if u >= 2:
                            act.wait_ge(scores_ready, TU * (u - 1))
                        act.wait_ge(zeros_ready, 1)
                        src = ps.rearrange("p (w q) -> p w q", w=NW)
                        nc.scalar.copy(QBD[0:64, u % 2, p, :, 0, :], src[0:64])
                        nc.scalar.copy(QBD[64:128, u % 2, p, :, 1, :], src[64:128]).then_inc(act_used, 1)
                    elif kind == "AV":
                        g = item[1]
                        u, t = g // TU, g % TU
                        s = unit_step(u)
                        if s >= 1:
                            act.wait_ge(bank_filled, ring.filled(("WO", s - 1)))
                        p0 = 2 * (u % 2)
                        nc.scalar.copy(OTH[:, p0:p0 + 2, t * P:(t + 1) * P],
                                       ps[:, 0:2 * P].rearrange("p (c t) -> p c t", c=2)).then_inc(act_used, 1)
                    elif kind == "WO":
                        s = item[1]
                        act.wait_ge(dve_used, ring.dve[item])
                        if s >= 1 and (s - 1) < B:
                            act.wait_ge(h_split, s)
                        if s >= 1:
                            act.wait_ge(bank_filled, ring.filled(("LT", s - 1)))
                        shifted(s % B)
                    elif kind == "LB":
                        s = item[1]
                        l = s // B
                        if s >= 1:
                            act.wait_ge(n_ready, s)
                        nc.scalar.activation(n32[:], ps, ACT.Identity, bias=cols[:, l, 1:2], scale=cols[:, l, 0:1])\
                            .then_inc(act_used, 1)
                    elif kind == "G":
                        _, s, c = item
                        m = CH[c][1]
                        if s >= 1:
                            act.wait_ge(dve_used, ring.dve[("A", s - 1, c)])
                        nc.scalar.activation(gelu_g[0:m, c, :], ps[0:m], ACT.Gelu, bias=cols[0:m, s // B, 6 + c:7 + c])\
                            .then_inc(act_used, 1)
                    elif kind == "W2" and item[1] < B:
                        s = item[1]
                        act.wait_ge(dve_used, ring.dve[item])
                        act.wait_ge(bank_filled, ring.filled(("LT", s)))
                        shifted(s % B)
                    elif kind == "SLOT":
                        T = item[1]
                        if T < NT:
                            act.wait_ge(max_ready, T + 1)
                            if T >= NP:
                                act.wait_ge(wT_ready, T - NP + 1)
                            for c in range(4):
                                last = nc.scalar.activation(weights[:, T % NP, c * P:(c + 1) * P],
                                                            scores[:, T % 2, c * P:(c + 1) * P], ACT.Exp,
                                                            bias=negmax[:, T % 8, c:c + 1],
                                                            accum_out=rowsum[:, T % 8, c:c + 1])
                            last.then_inc(exp_ready, 1)

            @block.vector
            def _(dve):
                link = chained(dve, dve_link, [0])
                h32_uses = 0
                for item in items:
                    kind = item[0]
                    if item in ring.dve:
                        dve.wait_ge(bank_filled, ring.filled(item))
                        ps = bank[:, ring.bank(item), :]
                    if kind == "QK":
                        _, u, i = item
                        l = unit_step(u) // B
                        n = NI * u + i
                        dve.wait_ge(act_used, ring.act[item])
                        if n >= 2:
                            dve.wait_ge(rot_added, n - 1)
                        heads = ps.rearrange("p (m h d) -> p m h d", m=2, h=4)
                        cos = keep["tables"][:, l, 0, :, i, :].unsqueeze(2).to_broadcast([P, 2, 4, DH])
                        nc.vector.tensor_tensor(rot_a[:, n % 2, :].rearrange("p (m h d) -> p m h d", m=2, h=4),
                                                heads, cos, ALU.mult)
                        H2 = DH // 2
                        for half in range(2):
                            o, f = half * H2, (1 - half) * H2
                            sin = keep["tables"][:, l, 1, :, i, o:o + H2].unsqueeze(2).to_broadcast([P, 2, 4, H2])
                            out = rot_b[:, n % 2, :].rearrange("p (m h d) -> p m h d", m=2, h=4)
                            last = nc.vector.tensor_tensor(out[:, :, :, o:o + H2], heads[:, :, :, f:f + H2], sin,
                                                           ALU.mult)
                        last.then_inc(dve_used, 1)
                        if i == 0 and u >= 2:
                            dve.wait_ge(norm_ready, u - 1)
                        nc.vector.tensor_reduce(sumsq[:, u % 2, 8 * i:8 * i + 8],
                                                sq[:, n % 2, :].rearrange("p (h d) -> p h d", d=DH), AX_X,
                                                ALU.add).then_inc(sumsq_done, 1)
                    elif kind == "NORM":
                        u = item[1]
                        dve.wait_ge(sumsq_done, NI * (u + 1))
                        if u >= 2:
                            dve.wait_ge(norm_applied, NI * (u - 1))
                        link(nc.vector.tensor_scalar(sumsq[:, u % 2, :], sumsq[:, u % 2, :], NORM_FLOOR, None, ALU.max))
                        rsqrt_on_dve(nc, link, sumsq[:, u % 2, :], norm_inv[:, u % 2, :], newton, 32)
                        nc.vector.tensor_copy(newton[:, 0:1], newton[:, 1:2]).then_inc(norm_ready, 1)
                        dve.wait_ge(norm_ready, u + 1)
                    elif kind == "QT" and item[2] == 1:
                        _, u, _, p = item
                        if u >= 2:
                            dve.wait_ge(scores_ready, TU * (u - 1))
                        nc.vector.tensor_copy(KT[:, u % 2, p, :], ps).then_inc(dve_used, 1)
                    elif kind == "AV":
                        g = item[1]
                        u, t = g // TU, g % TU
                        dve.wait_ge(act_used, ring.act[item])
                        p0 = 2 * (u % 2)
                        nc.vector.tensor_tensor(OTL[:, p0:p0 + 2, t * P:(t + 1) * P],
                                                ps[:, 0:2 * P].rearrange("p (c t) -> p c t", c=2),
                                                f32(OTH[:, p0:p0 + 2, t * P:(t + 1) * P]), ALU.subtract)\
                            .then_inc(dve_used, 1)
                    elif kind == "WO":
                        s = item[1]
                        b = s % B
                        nc.vector.tensor_tensor(xresT[:, b, :], ps, xresT[:, b, :], ALU.add).then_inc(dve_used, 1)
                    elif kind == "LT":
                        s = item[1]
                        for i in range(NI):
                            link(nc.vector.bn_stats(stats[:, i, :], ps[:, i * P:(i + 1) * P]))
                        for i in range(NI):
                            link(nc.vector.bn_aggr(mv[:, i, :], stats[:, i, :]))
                        link(nc.vector.tensor_scalar(var[:], mv[:, :, 1], LN_EPS, None, ALU.add))
                        rsqrt_on_dve(nc, link, var, rstd, newton, NI)
                        if s >= 1:
                            dve.wait_ge(bank_filled, ring.filled(("LB", s - 1)))
                        for i in range(NI):
                            last = nc.vector.tensor_scalar(hn[:, i, :], ps[:, i * P:(i + 1) * P], mv[:, i, 0:1],
                                                           rstd[:, i:i + 1], ALU.subtract, ALU.mult)
                        last.then_inc(dve_used, 1)
                    elif kind == "LB":
                        s = item[1]
                        dve.wait_ge(act_used, ring.act[item])
                        if s >= 1:
                            dve.wait_ge(bank_filled, ring.filled(("A", s - 1, 2)))
                        link(nc.vector.tensor_copy(nH[:], n32[:]))
                        nc.vector.tensor_tensor(nL[:], n32[:], f32(nH[:]), ALU.subtract).then_inc(n_ready, 1)
                    elif kind == "A":
                        _, s, c = item
                        m = CH[c][1]
                        dve.wait_ge(act_used, ring.act[("G", s, c)])
                        if s or c:
                            dve.wait_ge(hid_ready, 3 * s + c)
                        nc.vector.scalar_tensor_tensor(hid[0:m, :], ps[0:m], cols[0:m, s // B, 3 + c:4 + c],
                                                       gelu_g[0:m, c, :], ALU.add, ALU.mult).then_inc(dve_used, 1)
                        dve.wait_ge(dve_used, ring.dve[item])
                        if s >= 1:
                            dve.wait_ge(bank_filled, ring.filled(("W2", s - 1)))
                        link(nc.vector.tensor_copy(HH[0:m, c, :], hid[0:m, :]))
                        nc.vector.tensor_tensor(HL[0:m, c, :], hid[0:m, :], f32(HH[0:m, c, :]),
                                                ALU.subtract).then_inc(hid_ready, 1)
                    elif kind == "W2":
                        s = item[1]
                        l, b = s // B, s % B
                        dve.wait_ge(h32_ready, h32_uses + 1)
                        h32_uses += 1
                        nc.vector.scalar_tensor_tensor(xresT[:, b, :], ps, cols[:, l, 2:3], xresT[:, b, :], ALU.add,
                                                       ALU.add).then_inc(dve_used, 1)
                        if l == 0:
                            h32_uses += 1
                            dve.wait_ge(h32_ready, h32_uses)
                            dve.wait_ge(bank_filled, ring.filled(("VP", 2 * s + 1, NI - 1)))
                            link(nc.vector.tensor_copy(hh[:, b, :], h32[:, 0:N]))
                            nc.vector.tensor_tensor(hl[:, b, :], h32[:, 0:N], f32(hh[:, b, :]), ALU.subtract)\
                                .then_inc(h_split, 1)
                    elif kind == "SLOT":
                        g = item[1]
                        if g < NT:
                            T = g
                            dve.wait_ge(scores_ready, T + 1)
                            if T >= 8:
                                dve.wait_ge(exp_ready, T - 7)
                            nc.vector.tensor_reduce(negmax[:, T % 8, :],
                                                    scores[:, T % 2, :].rearrange("p (c k) -> p c k", k=P), AX_X,
                                                    ALU.max, negate=True).then_inc(max_ready, 1)
                        if LAG <= g < NT + LAG:
                            T = g - LAG
                            dve.wait_ge(wT_ready, T + 1)
                            if T >= 2:
                                dve.wait_ge(bank_filled, ring.filled(("AV", T - 2)))
                            nc.vector.tensor_copy(wT[:, T % 2, :], wT_ps[:, T % 2, :]).then_inc(wT_copied, 1)
                        if 1 <= g <= NT:
                            T = g - 1
                            dve.wait_ge(exp_ready, T + 1)
                            if T >= 8:
                                dve.wait_ge(weights_ready, T - 7)
                            nc.vector.reciprocal(inv[:, T % 8, :], rowsum[:, T % 8, :]).then_inc(inv_ready, 1)

            @block.tensor
            def _(pe):
                for item in items:
                    kind = item[0]
                    if item in ring.at:
                        old = ring.before(item)
                        if old is not None:
                            if old in ring.dve:
                                pe.wait_ge(dve_used, ring.dve[old])
                            if old in ring.act:
                                pe.wait_ge(act_used, ring.act[old])
                        ps = bank[:, ring.bank(item), :]
                    if kind == "QK":
                        _, u, i = item
                        l, b = unit_step(u) // B, unit_step(u) % B
                        if l:
                            pe.wait_ge(h_split, b + 1)
                        c = (u % 2) * 2 * P
                        tok = slice(i * P, (i + 1) * P)
                        split_matmul(nc, ps, (hh[:, b, tok], hl[:, b, tok]),
                                     (LWH[l][0][:, 0:2, c:c + 2 * P], LWL[l][0][:, 0:2, c:c + 2 * P]))\
                            .then_inc(bank_filled, 1)
                    elif kind == "VP":
                        _, u, v = item
                        l, b = unit_step(u) // B, unit_step(u) % B
                        c = (u % 2) * 2 * P
                        for j in range(2 * v, min(2 * v + 2, NW - 1)):
                            tok = slice(j * WIN, j * WIN + P)
                            o = (j % 2) * 2 * P
                            last = split_matmul(nc, ps[:, o:o + 2 * P], (hh[:, b, tok], hl[:, b, tok]),
                                                (LWH[l][0][:, 2, c:c + 2 * P], LWL[l][0][:, 2, c:c + 2 * P]))
                        last.then_inc(bank_filled, 1)
                    elif kind == "QT":
                        _, u, m, p = item
                        pe.wait_ge(norm_applied, NI * (u + 1))
                        for i in range(NI):
                            c = (2 * m + p) * P
                            last = nc.tensor.transpose(ps[:, i * P:(i + 1) * P], rot[:, i, c:c + P], ident[:])
                        last.then_inc(bank_filled, 1)
                    elif kind == "AV":
                        g = item[1]
                        u, t = g // TU, g % TU
                        pe.wait_ge(wT_copied, g + 1)
                        pe.wait_ge(act_used, ring.act[("VP", u, NI - 1)])
                        for w in range(2):
                            j = max(2 * t + w - 1, 0)
                            for p in range(2):
                                for h in range(2):
                                    c = (2 * w + p) * P + h * WIN
                                    d = (2 * p + h) * DH
                                    last = nc.tensor.matmul(ps[h * 64:h * 64 + 64, p * P + w * WIN:p * P + (w + 1) * WIN],
                                                            V[:, u % 2, j, d:d + DH], wT[:, g % 2, c:c + WIN],
                                                            start=True, stop=True)
                        last.then_inc(bank_filled, 1)
                    elif kind == "WO":
                        s = item[1]
                        l = s // B
                        pe.wait_ge(dve_used, ring.dve[("AV", 2 * TU * (s + 1) - 1)])
                        for c in range(4):
                            last = split_matmul(nc, ps, (LWH[l][1][:, c, :], LWL[l][1][:, c, :]),
                                                (OTH[:, c, :], OTL[:, c, :]), start=c == 0, stop=c == 3)
                        last.then_inc(bank_filled, 1)
                    elif kind == "LT":
                        s = item[1]
                        pe.wait_ge(h32_ready, s + 1 + min(s, B))
                        for i in range(NI):
                            last = nc.tensor.transpose(ps[:, i * P:(i + 1) * P], h32[:, i * P:(i + 1) * P], ident[:])
                        last.then_inc(bank_filled, 1)
                    elif kind == "LB":
                        s = item[1]
                        pe.wait_ge(dve_used, ring.dve[("LT", s)])
                        for i in range(NI):
                            last = nc.tensor.transpose(ps[:, i * P:(i + 1) * P], hn[:, i, :], ident[:])
                        last.then_inc(bank_filled, 1)
                    elif kind in ("G", "A"):
                        _, s, c = item
                        l = s // B
                        pe.wait_ge(n_ready, s + 1)
                        c0, m = CH[c]
                        c0 += HID if kind == "G" else 0
                        split_matmul(nc, ps[0:m], (LWH[l][2][:, c0:c0 + m], LWL[l][2][:, c0:c0 + m]),
                                     (nH[:], nL[:])).then_inc(bank_filled, 1)
                    elif kind == "W2":
                        s = item[1]
                        l = s // B
                        pe.wait_ge(hid_ready, 3 * (s + 1))
                        for c in range(3):
                            m = CH[c][1]
                            last = split_matmul(nc, ps, (LWH[l][3][0:m, c, :], LWL[l][3][0:m, c, :]),
                                                (HH[0:m, c, :], HL[0:m, c, :]), start=c == 0, stop=c == 2)
                        last.then_inc(bank_filled, 1)
                    elif kind == "SLOT":
                        g = item[1]
                        if LAG <= g < NT + LAG:
                            T = g - LAG
                            pe.wait_ge(weights_ready, T + 1)
                            if T >= 2:
                                pe.wait_ge(wT_copied, T - 1)
                            for c in range(4):
                                last = nc.tensor.transpose(wT_ps[:, T % 2, c * P:(c + 1) * P],
                                                           weights[:, T % NP, c * P:(c + 1) * P], ident[:])
                            last.then_inc(wT_ready, 1)
                        if g < NT:
                            T = g
                            u, t = T // TU, T % TU
                            if t == 0:
                                pe.wait_ge(act_used, ring.act[("QT", u, 0, 1)])
                                pe.wait_ge(dve_used, ring.dve[("QT", u, 1, 1)])
                            if T >= 2:
                                pe.wait_ge(exp_ready, T - 1)
                            for w in range(2):
                                m = 1 if (t == 0 and w == 0) else 2
                                mask = keep["masks"][:, m:m + 1, :].to_broadcast([P, 2, P])
                                nc.tensor.matmul(scores[:, T % 2, w * 2 * P:(w + 1) * 2 * P], keep["ident_bf"][:],
                                                 mask, start=w == 0, stop=False)
                            for w in range(2):
                                k0 = max(2 * t + w - 1, 0) * WIN
                                for p in range(2):
                                    c = (2 * w + p) * P
                                    last = nc.tensor.matmul(
                                        scores[:, T % 2, c:c + P],
                                        QBD[:, u % 2, p, 2 * t + w, :, :].rearrange("p h q -> p (h q)"),
                                        KT[:, u % 2, p, k0:k0 + P], start=False, stop=w == 1 and p == 1)
                            last.then_inc(scores_ready, 1)


def build(nc, io):
    with ExitStack() as ctx:
        def sb(name, shape, dt=F32):
            return ctx.enter_context(nc.sbuf_tensor(name, shape, dt))

        keep = {
            "x_tok": sb("x_tok", [P, B * NI, P]),
            "xresT": sb("xresT", [P, B, N]),
            "ident": sb("ident", [P, P]),
        }
        with ExitStack() as inner:
            def sb(name, shape, dt=F32):
                return inner.enter_context(nc.sbuf_tensor(name, shape, dt))

            keep |= {
                "ident_bf": sb("ident_bf", [P, P], BF16),
                "masks": sb("masks", [P, 3, P], BF16),
                "hh": sb("hh", [P, B, N], F32R),
                "hl": sb("hl", [P, B, N], F32R),
                "h32": sb("h32", [P, N + 4]),
                "tables": sb("tables", [P, DEPTH, 2, 2, NI, DH]),
                "cols": sb("cols", [P, DEPTH, COLS]),
                "w_h": sb("w_h", [P, DEPTH * W_LAYER], F32R),
                "w_l": sb("w_l", [P, DEPTH * W_LAYER], F32R),
            }
            attention_block(nc, "l0", keep, io["l0"], True)
            windowed_block(nc, keep)
        attention_block(nc, "l1", keep, io["l1"], False)


def _constants():
    import numpy as np

    p, k = np.arange(P)[:, None], np.arange(P)[None, :]
    q = p % WIN
    masks = np.stack([np.where(k > p, MASKED, 0.0),
                      np.where(k > q, MASKED, 0.0),
                      np.where((k > q + WIN) | (k < q), MASKED, 0.0)], 1)
    f = np.float32
    half = np.arange(0, DH, 2, dtype=f)
    inv_freq = (f(1.0) / f(10000.0) ** (half / f(DH))).astype(f)
    t = np.arange(N, dtype=f)
    freqs = t[:, None] * inv_freq[None, :]
    base = ((half + f(0.4 * DH)) / f(1.4 * DH)).astype(f)
    power = (t - f(N // 2)) / f(WIN // 2)
    scale = base[None, :] ** power[:, None]
    two = lambda a: np.concatenate([a, a], -1)
    cos, sin, scale = two(np.cos(freqs)), two(np.sin(freqs)), two(scale)
    sin[:, :DH // 2] *= -1
    rot = np.stack([np.stack([8.0 * cos * scale, cos / scale], 0),
                    np.stack([8.0 * sin * scale, sin / scale], 0)], 0)
    rot = rot.reshape(2, 2, NI, P, DH).transpose(3, 0, 1, 2, 4)
    c = np.ascontiguousarray
    return np.eye(P, dtype=f), c(masks.astype(f)), c(rot.astype(f))


def kernel(**a):
    import numpy as np
    import concourse.bacc as bacc
    from concourse import mybir as mb
    from concourse.bass_utils import run_bass_kernel_spmd as run

    a = {k: np.asarray(v) for k, v in a.items()}
    c = np.ascontiguousarray
    rows = lambda w: w.reshape(-1, P, w.shape[-1]).transpose(1, 0, 2).reshape(P, -1)

    ident, masks, rotary = _constants()
    layers, cols, scales = [], [], []
    pad = lambda v, n: np.concatenate([v, np.zeros((n - v.shape[0],) + v.shape[1:], v.dtype)])
    for l in range(DEPTH):
        layers += [a["L0_ffn_wqkv"][l], rows(a["L0_ffn_wo"][l]), a["L0_ffn_w1"][l],
                   rows(pad(a["L0_ffn_w2"][l], 3 * P))]
        b1 = a["L0_ffn_b1"][l]
        cols.append(np.stack([a["L0_ffn_ln_g"][l], a["L0_ffn_ln_b"][l], a["L0_ffn_b2"][l]]
                             + [pad(b1[o + s:o + s + n], P) for o in (0, HID) for s, n in CH], 1))
        per = []
        for s in (a["L0_ffn_q_scale"][l], a["L0_ffn_k_scale"][l]):
            per.append(np.stack([s, np.concatenate([s[DH // 2:], s[:DH // 2]])]))
        scales.append(np.stack(per))
    l0 = {
        "x": a["L0_attn_X"], "ident": ident, "masks": masks, "rotary": rotary,
        "qk_scales": c(np.broadcast_to(np.stack(scales)[None], (P, DEPTH, 2, 2, DH))),
        "cols": c(np.stack(cols, 1)), "Wq": a["L0_attn_Wq"], "Wk": a["L0_attn_Wk"], "Wv": a["L0_attn_Wv"],
        "w_all": c(np.concatenate(layers, 1)),
    }
    heads = lambda w: w.transpose(1, 0, 2).reshape(P, -1)
    float_w = np.concatenate([heads(a["L1_attn_proj_q"]), a["L1_attn_proj_k"],
                              heads(a["L1_attn_proj_o"].transpose(0, 2, 1))], 1)
    l1 = {
        "Wv": a["L1_attn_proj_v"],
        "w_all": c(np.concatenate([float_w, np.zeros((P, 3 * FF), np.float32)], 1)),
        "w_int": c(np.concatenate([a["L1_ffn_w_gate"].T, a["L1_ffn_w_up"].T, rows(a["L1_ffn_w_down"].T)], 1)),
    }
    nc = bacc.Bacc("TRN2", target_bir_lowering=False, num_devices=1)
    io, arrays = {}, {}
    for tag, group in (("l0", l0), ("l1", l1)):
        io[tag] = {}
        for name, value in group.items():
            value = c(value)
            arrays[f"{tag}_{name}_in"] = value
            io[tag][name] = nc.dram_tensor(f"{tag}_{name}_in", value.shape, mb.dt.from_np(value.dtype),
                                           kind="ExternalInput").ap()
    io["l1"]["out"] = nc.dram_tensor("out_dram", (B, N, P), F32, kind="ExternalOutput").ap()
    build(nc, io)
    return run(nc, [arrays], core_ids=[0]).results[0]["out_dram"]
```

```python
from contextlib import ExitStack

import concourse.bass as bass
from concourse import mybir

F32 = mybir.dt.float32
F32R = mybir.dt.float32r
BF16 = mybir.dt.bfloat16
I32 = mybir.dt.int32
ALU = mybir.AluOpType
ACT = mybir.ActivationFunctionType
AX_X = mybir.AxisListType.X

P = 128
B, N = 4, 512
NI = N // P
DQ = 64
DEPTH, HEADS, DH = 2, 8, 64
WIN = 64
NW = N // WIN
INNER = HEADS * DH
HID = 341
CH = [(0, 128), (128, 128), (256, 85)]
NQ = 8
FF = 384
FC = FF // P
MASKED = -1.0e30
LN_EPS = 1e-5
NORM_FLOOR = 1e-24
RSQRT_MAGIC = float(0x5F3759DF)
NP = 4


def f32(ap):
    return ap.bitcast(F32)


class Ring:

    def __init__(self, banks, order, uses_act, uses_dve):
        self.banks = banks
        self.at = {job: j for j, job in enumerate(order)}
        self.order = order
        self.act, self.dve = {}, {}
        a = d = 0
        for job in order:
            if uses_act(job):
                a += 1
                self.act[job] = a
            if uses_dve(job):
                d += 1
                self.dve[job] = d

    def bank(self, job):
        return self.at[job] % self.banks

    def filled(self, job):
        return self.at[job] + 1

    def before(self, job):
        j = self.at[job] - self.banks
        return self.order[j] if j >= 0 else None


def split_matmul(nc, out, lhs, rhs, start=True, stop=True):
    (lh, ll), (rh, rl) = lhs, rhs
    nc.tensor.matmul(out, lh, rh, start=start, stop=False)
    nc.tensor.matmul(out, lh, rl, start=False, stop=False)
    return nc.tensor.matmul(out, ll, rh, start=False, stop=stop)


def chained(eng, sem, count):
    def link(ins):
        count[0] += 1
        ins.then_inc(sem, 1)
        eng.wait_ge(sem, count[0])
    return link


def rsqrt_on_dve(nc, link, v, y, t, n):
    link(nc.vector.tensor_scalar(y[:, 0:n].bitcast(I32), v[:, 0:n].bitcast(I32), 1, None,
                                 ALU.logical_shift_right))
    link(nc.vector.tensor_scalar(y[:, 0:n].bitcast(I32), y[:, 0:n].bitcast(I32), -1.0, RSQRT_MAGIC,
                                 ALU.mult, ALU.add))
    for _ in range(3):
        link(nc.vector.scalar_tensor_tensor(t[:, 0:n], y[:, 0:n], -0.5, y[:, 0:n], ALU.mult, ALU.mult))
        link(nc.vector.tensor_tensor(t[:, 0:n], t[:, 0:n], v[:, 0:n], ALU.mult))
        link(nc.vector.scalar_tensor_tensor(y[:, 0:n], t[:, 0:n], 1.5, y[:, 0:n], ALU.add, ALU.mult))


def attention_block(nc, tag, keep, io, causal):
    x_tok, xresT, ident = keep["x_tok"], keep["xresT"], keep["ident"]
    heads = 1 if causal else NQ
    jobs = [(b, h) for b in range(B) for h in range(heads)]
    tiles = [(j, i) for j in range(len(jobs)) for i in range(NI)]
    NT = len(tiles)

    AT = L0_AT if causal else L1_AT
    line = [(g + AT[kind], (kind, g)) for g in range(NT) for kind in ("S", "E", "I", "TR")]
    for j in range(len(jobs)):
        g = NI * j
        line += [(g + AT["Q"], ("Q", j)), (g + AT["O"], ("O", j))]
        line += [(g + AT["AV", k], ("AV", j, k)) for k in range(NI)]
        kind = "OT" if causal else "OP"
        line.append((g + AT[kind], (kind, j)))
    for b in range(B):
        g = heads * NI * b
        kinds = ("STATS", "LN", "HX", "K", "V") if causal else ("X1", "STATS", "LN", "K", "V", "DOWN", "YT")
        line += [(g + AT[kind], (kind, b)) for kind in kinds]
        if not causal:
            line += [(g + AT[kind, c], (kind, b, c)) for kind in ("GATE", "UP") for c in range(FC)]
    line += [(AT["W", l], ("W", l)) for l in range(2)]
    if causal:
        line.append((AT["CONSTS"], ("CONSTS",)))
    items = [item for _, item in sorted(line)]
    in_ring = [x for x in items if x[0] not in ("TR", "S", "I", "E", "AV", "O", "OP", "DOWN", "W", "STATS", "CONSTS", "HX")]
    by_act = {"LN", "K", "V", "Q", "GATE"}
    by_dve = {"K", "V", "Q", "X1", "OT", "YT", "UP", "GATE"}
    ring = Ring(2, in_ring, lambda x: x[0] in by_act, lambda x: x[0] in by_dve)

    with ExitStack() as ctx:
        def sb(name, shape, dt=F32):
            return ctx.enter_context(nc.sbuf_tensor(f"{tag}_{name}", shape, dt))

        def psum(name, shape):
            return ctx.enter_context(nc.psum_tensor(f"{tag}_{name}", shape, F32))

        def sem(name):
            return ctx.enter_context(nc.semaphore(f"{tag}_{name}"))

        scores = psum("scores", [P, 2, 512])
        wT_ps = psum("wT_ps", [P, 2, 512])
        bank = psum("bank", [P, 2, 512])
        o_ps = psum("o_ps", [P, 512])
        y_ps = psum("y_ps", [P, 512])

        xn_tok = sb("xn_tok", [P, NI, P])
        stats = sb("stats", [P, B * NI, 6])
        mv = sb("mv", [P, B * NI, 2])
        var = sb("var", [P, B * NI])
        rstd = sb("rstd", [P, B * NI])
        minus_half = sb("minus_half", [P, NI])
        xnT = xresT if causal else sb("xnT", [P, B, N])
        xh, xl = sb("xh", [P, B, N], F32R), sb("xl", [P, B, N], F32R)
        QH, QL = sb("QH", [P, 2, N], F32R), sb("QL", [P, 2, N], F32R)
        KH = sb("KH", [P, 2, N], F32R)
        KL = None if causal else sb("KL", [P, 2, N], F32R)
        VH, VL = sb("VH", [P, 2, NI, P], F32R), sb("VL", [P, 2, NI, P], F32R)
        negmax = sb("negmax", [P, 8])
        rowsum = sb("rowsum", [P, 8])
        inv = sb("inv", [P, 8])
        weights = sb("weights", [P, NP, N])
        WH, WL = sb("WH", [P, 2, NI, N], F32R), sb("WL", [P, 2, NI, N], F32R)
        oT = sb("oT", [P, N])
        if causal:
            raw = sb("raw", [P, W_LAYER])
            qk_raw = sb("qk_raw", [P, 2, P])
            wqk_h, wqk_l = sb("wqk_h", [P, 2, P], F32R), sb("wqk_l", [P, 2, P], F32R)
            wv = sb("wv", [P, P])
            mask32 = sb("mask32", [P, 3, P])
            h32 = keep["h32"]
            tab = sb("tab", [P, 2, 2, NI, DH])
            scl = sb("scl", [P, DEPTH, 2, 2, DH])
        else:
            nw = io["w_all"].shape[1]
            raw = sb("raw", [P, nw])
            w_h, w_l = sb("w_h", [P, nw], F32R), sb("w_l", [P, nw], F32R)
            int_w = sb("int_w", [P, 3 * FF], I32)
            wv = sb("wv", [P, P])
            OH, OL = sb("OH", [P, 2, N], F32R), sb("OL", [P, 2, N], F32R)
            tanh_g = sb("tanh_g", [P, N])
            silu_g = sb("silu_g", [P, 2, N])
            hid = sb("hid", [P, N])
            HH, HL = sb("HH", [P, FC, N], F32R), sb("HL", [P, FC, N], F32R)
            out_tok = sb("out_tok", [P, 2, NI, P])

        x_loaded = [sem(f"x_loaded{b}") for b in range(B)]
        consts_loaded = sem("consts_loaded")
        ident_loaded = sem("ident_loaded")
        w_loaded = sem("w_loaded")
        w_split = sem("w_split")
        tables_ready = sem("tables_ready")
        dve_link = sem("dve_link")
        consts_ready = sem("consts_ready")
        zeros_ready = sem("zeros_ready")
        stats_done = sem("stats_done")
        var_ready = sem("var_ready")
        rstd_ready = sem("rstd_ready")
        minus_half_ready = sem("minus_half_ready")
        h_high = sem("h_high")
        h_low = sem("h_low")
        xn_ready = sem("xn_ready")
        xT_split = sem("xT_split")
        bank_filled = sem("bank_filled")
        act_used = sem("act_used")
        dve_used = sem("dve_used")
        scores_ready = sem("scores_ready")
        max_ready = sem("max_ready")
        exp_ready = sem("exp_ready")
        inv_ready = sem("inv_ready")
        weights_ready = sem("weights_ready")
        wT_ready = sem("wT_ready")
        high_ready = sem("high_ready")
        low_ready = sem("low_ready")
        o_ready = sem("o_ready")
        o_high = sem("o_high")
        o_low = sem("o_low")
        out_proj_done = sem("out_proj_done")
        y_taken = sem("y_taken")
        down_done = sem("down_done")
        stored = [sem(f"stored{k}") for k in range(2)]

        if causal:
            w_parts = [(keep["w_l"][:, l * W_LAYER:(l + 1) * W_LAYER], keep["w_h"][:, l * W_LAYER:(l + 1) * W_LAYER],
                        slice(0, W_LAYER)) for l in range(DEPTH)]
        else:
            w_parts = [(w_l[:, cs], w_h[:, cs], cs) for cs in (slice(0, (NQ + 1) * P), slice((NQ + 1) * P, nw))]
            wq_c = lambda w, h: w[:, h * P:(h + 1) * P]
            wk_c = lambda w: w[:, NQ * P:(NQ + 1) * P]
            wo_c = lambda w, h: w[:, (NQ + 1 + h) * P:(NQ + 2 + h) * P]
            g0 = (2 * NQ + 1) * P
            wg_c = lambda w, c: w[:, g0 + c * P:g0 + (c + 1) * P]
            wu_c = lambda w, c: w[:, g0 + FF + c * P:g0 + FF + (c + 1) * P]
            wd_c = lambda w, c: w[:, g0 + 2 * FF + c * P:g0 + 2 * FF + (c + 1) * P]

        with nc.Block() as block:

            @block.sync
            def _(sp):
                if causal:
                    for b in range(B):
                        sp.dma_start(x_tok[:, b * NI:(b + 1) * NI, :],
                                     io["x"][b].rearrange("(i p) d -> p i d", p=P)).then_inc(x_loaded[b], 16)
                    sp.dma_start(ident[:], io["ident"]).then_inc(ident_loaded, 16)
                    sp.dma_start(mask32[:], io["masks"]).then_inc(consts_loaded, 16)
                    sp.dma_start(tab[:], io["rotary"]).then_inc(consts_loaded, 16)
                    sp.dma_start(scl[:], io["qk_scales"]).then_inc(consts_loaded, 16)
                    sp.dma_start(keep["cols"][:], io["cols"]).then_inc(consts_loaded, 16)
                    for m in range(2):
                        for r in range(2):
                            sp.dma_start(qk_raw[:, m, r * DQ:(r + 1) * DQ], (io["Wq"], io["Wk"])[m])\
                              .then_inc(consts_loaded, 16)
                    sp.dma_start(wv[:], io["Wv"]).then_inc(consts_loaded, 16)
                    for l in range(DEPTH):
                        if l:
                            sp.wait_ge(w_split, 2 * l)
                        sp.dma_start(raw[:], io["w_all"][:, l * W_LAYER:(l + 1) * W_LAYER]).then_inc(w_loaded, 16)
                else:
                    sp.dma_start(wv[:], io["Wv"]).then_inc(consts_loaded, 16)
                    sp.dma_start(raw[:, 0:g0], io["w_all"][:, 0:g0]).then_inc(w_loaded, 16)
                    sp.dma_start(int_w[:], io["w_int"]).then_inc(w_loaded, 16)
                    for b in range(B):
                        sp.wait_ge(dve_used, ring.dve[("YT", b)])
                        sp.dma_start(io["out"][b].rearrange("(i p) d -> p i d", p=P),
                                     out_tok[:, b % 2]).then_inc(stored[b % 2], 16)
                    for k in range(2):
                        sp.wait_ge(stored[k], 16 * B // 2)

            @block.gpsimd
            def _(pool):
                nc.gpsimd.memset(minus_half[:], -0.5).then_inc(minus_half_ready, 1)
                if causal:
                    nc.gpsimd.memset(WH[:, :, NI - 1, 2 * P:3 * P].bitcast(F32), 0.0).then_inc(zeros_ready, 1)
                    nc.gpsimd.memset(WL[:, :, NI - 1, 2 * P:3 * P].bitcast(F32), 0.0).then_inc(zeros_ready, 1)
                    nc.gpsimd.memset(h32[:], 0.0).then_inc(zeros_ready, 1)
                for item in items:
                    if item[0] == "CONSTS":
                        pool.wait_ge(consts_loaded, 16 * 9)
                        for l in range(DEPTH):
                            for m in range(2):
                                for r in range(2):
                                    nc.gpsimd.tensor_tensor(keep["tables"][:, l, r, m], tab[:, r, m],
                                                            scl[:, l, m, r:r + 1, :].to_broadcast([P, NI, DH]),
                                                            ALU.mult).then_inc(tables_ready, 1)
                    if item[0] == "STATS":
                        b = item[1]
                        pool.wait_ge(minus_half_ready, 1)
                        pool.wait_ge(var_ready, b + 1)
                        bt = slice(b * NI, (b + 1) * NI)
                        nc.gpsimd.tensor_tensor(rstd[:, bt], var[:, bt], minus_half[:], ALU.pow).then_inc(rstd_ready, 1)
                    if item[0] == "HX":
                        b = item[1]
                        pool.wait_ge(h_high, b + 1)
                        nc.gpsimd.tensor_tensor(keep["hl"][:, b, :], h32[:, 0:N], f32(keep["hh"][:, b, :]),
                                                ALU.subtract).then_inc(h_low, 1)
                    if item[0] == "W":
                        l = item[1]
                        pool.wait_ge(w_split, 2 * l + 1)
                        dst, hi, cs = w_parts[l]
                        nc.gpsimd.tensor_tensor(dst, raw[:, cs], f32(hi), ALU.subtract).then_inc(w_split, 1)
                    if item[0] == "I":
                        T = item[1]
                        i = tiles[T][1]
                        n = P * (i + 1) if causal else N
                        pool.wait_ge(inv_ready, T + 1)
                        w = weights[:, T % NP, 0:n]
                        nc.gpsimd.tensor_tensor(w, w, inv[:, T % 8:T % 8 + 1].to_broadcast([P, n]), ALU.mult)\
                            .then_inc(weights_ready, 1)

            @block.scalar
            def _(act):
                for item in items:
                    kind = item[0]
                    if kind in by_act:
                        act.wait_ge(bank_filled, ring.filled(item))
                        ps = bank[:, ring.bank(item), :]
                    if kind == "LN":
                        b = item[1]
                        nc.scalar.copy(xnT[:, b, :], ps).then_inc(act_used, 1)
                    elif kind == "K":
                        b = item[1]
                        if b >= 2:
                            act.wait_ge(scores_ready, (b - 1) * heads * NI)
                        nc.scalar.copy(KH[:, b % 2, :], ps).then_inc(act_used, 1)
                    elif kind == "V":
                        b = item[1]
                        if b >= 2:
                            act.wait_ge(o_ready, (b - 1) * heads)
                        nc.scalar.copy(VH[:, b % 2], ps).then_inc(act_used, 1)
                    elif kind == "Q":
                        j = item[1]
                        if j >= 2:
                            act.wait_ge(scores_ready, (j - 1) * NI)
                        nc.scalar.activation(QH[:, j % 2, :], ps, ACT.Copy, scale=0.125 if causal else 1.0)\
                            .then_inc(act_used, 1)
                    elif kind == "O":
                        j = item[1]
                        act.wait_ge(o_ready, j + 1)
                        if causal:
                            if j >= 1:
                                act.wait_ge(bank_filled, ring.filled(("OT", j - 1)))
                            nc.scalar.copy(oT[:], o_ps[:]).then_inc(o_high, 1)
                        else:
                            if j >= 2:
                                act.wait_ge(out_proj_done, j - 1)
                            nc.scalar.copy(OH[:, j % 2, :], o_ps[:]).then_inc(o_high, 1)
                    elif kind == "GATE":
                        _, b, c = item
                        if b or c:
                            last = (b, c - 1) if c else (b - 1, FC - 1)
                            act.wait_ge(dve_used, ring.dve[("GATE", *last)])
                        nc.scalar.activation(tanh_g[:], ps, ACT.Tanh, scale=0.5).then_inc(act_used, 1)
                    elif kind == "YT" and not causal:
                        b = item[1]
                        act.wait_ge(out_proj_done, NQ * (b + 1))
                        if b >= 1:
                            act.wait_ge(bank_filled, ring.filled(("YT", b - 1)))
                        nc.scalar.copy(oT[:], y_ps[:]).then_inc(y_taken, 1)
                    elif kind == "TR":
                        T = item[1]
                        j, i = tiles[T]
                        n = i + 1 if causal else NI
                        act.wait_ge(wT_ready, T + 1)
                        if j >= 2:
                            act.wait_ge(o_ready, j - 1)
                        nc.scalar.copy(WH[:, j % 2, 0:n, i * P:(i + 1) * P],
                                       wT_ps[:, T % 2, 0:n * P].rearrange("p (k q) -> p k q", q=P))\
                            .then_inc(high_ready, 1)
                    elif kind == "E":
                        T = item[1]
                        i = tiles[T][1]
                        n = P * (i + 1) if causal else N
                        act.wait_ge(max_ready, T + 1)
                        if T >= NP:
                            act.wait_ge(wT_ready, T - NP + 1)
                        nc.scalar.activation(weights[:, T % NP, 0:n], scores[:, T % 2, 0:n], ACT.Exp,
                                             bias=negmax[:, T % 8:T % 8 + 1],
                                             accum_out=rowsum[:, T % 8:T % 8 + 1]).then_inc(exp_ready, 1)

            @block.vector
            def _(dve):
                link = chained(dve, dve_link, [0])

                for item in items:
                    kind = item[0]
                    if kind == "STATS":
                        b = item[1]
                        if causal:
                            dve.wait_ge(x_loaded[b], 16)
                        for t in range(b * NI, (b + 1) * NI):
                            nc.vector.bn_stats(stats[:, t, :], x_tok[:, t, :]).then_inc(stats_done, 1)
                        for t in range(b * NI, (b + 1) * NI):
                            dve.wait_ge(stats_done, (2 * b + 1) * NI)
                            nc.vector.bn_aggr(mv[:, t, :], stats[:, t, :]).then_inc(stats_done, 1)
                        dve.wait_ge(stats_done, 2 * (b + 1) * NI)
                        bt = slice(b * NI, (b + 1) * NI)
                        nc.vector.tensor_scalar(var[:, bt], mv[:, bt, 1], LN_EPS, None, ALU.add).then_inc(var_ready, 1)
                    elif kind == "CONSTS":
                        dve.wait_ge(consts_loaded, 16 * 9)
                        dve.wait_ge(ident_loaded, 16)
                        nc.vector.tensor_copy(keep["ident_bf"][:], ident[:]).then_inc(consts_ready, 1)
                        nc.vector.tensor_copy(keep["masks"][:], mask32[:]).then_inc(consts_ready, 1)
                        nc.vector.tensor_copy(wqk_h[:], qk_raw[:]).then_inc(consts_ready, 1)
                        dve.wait_ge(consts_ready, 3)
                        nc.vector.tensor_tensor(wqk_l[:], qk_raw[:], f32(wqk_h[:]), ALU.subtract)\
                            .then_inc(consts_ready, 1)
                    elif kind == "LN":
                        b = item[1]
                        if b >= 1:
                            dve.wait_ge(bank_filled, ring.filled(("LN", b - 1)))
                        dve.wait_ge(rstd_ready, b + 1)
                        for i in range(NI):
                            t = b * NI + i
                            nc.vector.tensor_scalar(xn_tok[:, i, :], x_tok[:, t, :], mv[:, t, 0:1],
                                                    rstd[:, t:t + 1], ALU.subtract, ALU.mult).then_inc(xn_ready, 1)
                        dve.wait_ge(act_used, ring.act[item])
                        nc.vector.tensor_copy(xh[:, b, :], xnT[:, b, :]).then_inc(xT_split, 1)
                        dve.wait_ge(xT_split, 2 * b + 1)
                        nc.vector.tensor_tensor(xl[:, b, :], xnT[:, b, :], f32(xh[:, b, :]), ALU.subtract)\
                            .then_inc(xT_split, 1)
                    elif kind == "HX":
                        b = item[1]
                        if b == 0:
                            dve.wait_ge(zeros_ready, 3)
                        else:
                            dve.wait_ge(h_low, b)
                        link(nc.vector.tensor_copy(h32[0:64, 0:N], xnT[0:64, b, :]))
                        link(nc.vector.tensor_copy(h32[64:128, 1:N + 1], xnT[64:128, b, :]))
                        nc.vector.tensor_copy(keep["hh"][:, b, :], h32[:, 0:N]).then_inc(h_high, 1)
                    elif kind == "W":
                        l = item[1]
                        _, hi, cs = w_parts[l]
                        if causal:
                            dve.wait_ge(w_loaded, 16 * (l + 1))
                        elif l == 0:
                            dve.wait_ge(w_loaded, 32)
                        else:
                            link(nc.vector.tensor_copy(raw[:, g0:], int_w[:]))
                            link(nc.vector.tensor_scalar(raw[:, g0:], raw[:, g0:], 1.0 / 127.0, None, ALU.mult))
                        if l:
                            dve.wait_ge(w_split, 2 * l)
                        nc.vector.tensor_copy(hi, raw[:, cs]).then_inc(w_split, 1)
                    elif kind == "X1":
                        b = item[1]
                        dve.wait_ge(bank_filled, ring.filled(item))
                        xt = x_tok[:, b * NI:(b + 1) * NI, :]
                        nc.vector.tensor_tensor(xt, bank[:, ring.bank(item), :].rearrange("p (i d) -> p i d", d=P),
                                                xt, ALU.add).then_inc(dve_used, 1)
                        dve.wait_ge(dve_used, ring.dve[item])
                    elif kind == "K":
                        b = item[1]
                        dve.wait_ge(act_used, ring.act[item])
                        ps = bank[:, ring.bank(item), :]
                        if causal:
                            nc.vector.tensor_tensor(KH[64:128, b % 2, :], ps[64:128, :],
                                                    f32(KH[64:128, b % 2, :]), ALU.subtract)\
                                .then_inc(dve_used, 1)
                        else:
                            nc.vector.tensor_tensor(KL[:, b % 2, :], ps, f32(KH[:, b % 2, :]), ALU.subtract)\
                                .then_inc(dve_used, 1)
                    elif kind == "V":
                        b = item[1]
                        dve.wait_ge(act_used, ring.act[item])
                        nc.vector.tensor_tensor(VL[:, b % 2], bank[:, ring.bank(item), :]
                                                .rearrange("p (i d) -> p i d", d=P), f32(VH[:, b % 2]),
                                                ALU.subtract).then_inc(dve_used, 1)
                    elif kind == "Q":
                        j = item[1]
                        dve.wait_ge(act_used, ring.act[item])
                        nc.vector.scalar_tensor_tensor(QL[:, j % 2, :], bank[:, ring.bank(item), :],
                                                       0.125 if causal else 1.0, f32(QH[:, j % 2, :]),
                                                       ALU.mult, ALU.subtract).then_inc(dve_used, 1)
                    elif kind == "O" and not causal:
                        j = item[1]
                        dve.wait_ge(o_high, j + 1)
                        nc.vector.tensor_tensor(OL[:, j % 2, :], o_ps[:], f32(OH[:, j % 2, :]), ALU.subtract)\
                            .then_inc(o_low, 1)
                    elif kind == "OT":
                        j = item[1]
                        dve.wait_ge(bank_filled, ring.filled(item))
                        xt = x_tok[:, j * NI:(j + 1) * NI, :]
                        nc.vector.tensor_tensor(xt, bank[:, ring.bank(item), :].rearrange("p (i d) -> p i d", d=P),
                                                xt, ALU.add).then_inc(dve_used, 1)
                    elif kind == "GATE":
                        _, b, c = item
                        dve.wait_ge(act_used, ring.act[item])
                        if b or c >= 2:
                            k = b * FC + c - 2
                            if k >= 0:
                                dve.wait_ge(dve_used, ring.dve[("UP", k // FC, k % FC)])
                        nc.vector.scalar_tensor_tensor(silu_g[:, (b * FC + c) % 2, :], tanh_g[:], 1.0,
                                                       bank[:, ring.bank(item), :], ALU.add, ALU.mult)\
                            .then_inc(dve_used, 1)
                    elif kind == "UP":
                        _, b, c = item
                        dve.wait_ge(bank_filled, ring.filled(item))
                        dve.wait_ge(dve_used, ring.dve[("GATE", b, c)])
                        if b >= 1:
                            dve.wait_ge(down_done, b)
                        link(nc.vector.scalar_tensor_tensor(hid[:], silu_g[:, (b * FC + c) % 2, :], 0.5,
                                                            bank[:, ring.bank(item), :], ALU.mult, ALU.mult))
                        link(nc.vector.tensor_copy(HH[:, c, :], hid[:]))
                        nc.vector.tensor_tensor(HL[:, c, :], hid[:], f32(HH[:, c, :]), ALU.subtract)\
                            .then_inc(dve_used, 1)
                        dve.wait_ge(dve_used, ring.dve[item])
                    elif kind == "YT":
                        b = item[1]
                        dve.wait_ge(bank_filled, ring.filled(item))
                        if b >= 2:
                            dve.wait_ge(stored[b % 2], 16 * (b // 2))
                        nc.vector.tensor_tensor(out_tok[:, b % 2], bank[:, ring.bank(item), :]
                                                .rearrange("p (i d) -> p i d", d=P),
                                                x_tok[:, b * NI:(b + 1) * NI, :], ALU.add)\
                            .then_inc(dve_used, 1)
                    elif kind == "S":
                        T = item[1]
                        i = tiles[T][1]
                        n = P * (i + 1) if causal else N
                        dve.wait_ge(scores_ready, T + 1)
                        if T >= 8:
                            dve.wait_ge(exp_ready, T - 7)
                        nc.vector.tensor_reduce(negmax[:, T % 8:T % 8 + 1], scores[:, T % 2, 0:n], AX_X,
                                                ALU.max, negate=True).then_inc(max_ready, 1)
                    elif kind == "I":
                        T = item[1]
                        dve.wait_ge(exp_ready, T + 1)
                        if T >= 8:
                            dve.wait_ge(weights_ready, T - 7)
                        nc.vector.reciprocal(inv[:, T % 8:T % 8 + 1], rowsum[:, T % 8:T % 8 + 1])\
                            .then_inc(inv_ready, 1)
                    elif kind == "TR":
                        T = item[1]
                        j, i = tiles[T]
                        n = i + 1 if causal else NI
                        dve.wait_ge(high_ready, T + 1)
                        nc.vector.tensor_tensor(WL[:, j % 2, 0:n, i * P:(i + 1) * P],
                                                wT_ps[:, T % 2, 0:n * P].rearrange("p (k q) -> p k q", q=P),
                                                f32(WH[:, j % 2, 0:n, i * P:(i + 1) * P]), ALU.subtract)\
                            .then_inc(low_ready, 1)

            @block.tensor
            def _(pe):
                def claim(item):
                    old = ring.before(item)
                    if old is not None:
                        if old in ring.dve:
                            pe.wait_ge(dve_used, ring.dve[old])
                        if old in ring.act:
                            pe.wait_ge(act_used, ring.act[old])
                    return bank[:, ring.bank(item), :]

                if causal:
                    pe.wait_ge(ident_loaded, 16)
                else:
                    pe.wait_ge(consts_loaded, 16)
                for item in items:
                    kind = item[0]
                    if kind == "LN":
                        b = item[1]
                        ps = claim(item)
                        pe.wait_ge(xn_ready, NI * (b + 1))
                        for i in range(NI):
                            last = nc.tensor.transpose(ps[:, i * P:(i + 1) * P], xn_tok[:, i, :], ident[:])
                        last.then_inc(bank_filled, 1)
                    elif kind == "X1":
                        b = item[1]
                        ps = claim(item)
                        for i in range(NI):
                            last = nc.tensor.transpose(ps[:, i * P:(i + 1) * P],
                                                       xresT[:, b, i * P:(i + 1) * P], ident[:])
                        last.then_inc(bank_filled, 1)
                    elif kind == "K":
                        b = item[1]
                        ps = claim(item)
                        pe.wait_ge(xT_split, 2 * (b + 1))
                        if causal:
                            pe.wait_ge(consts_ready, 4)
                            w = (wqk_h[:, 1, :], wqk_l[:, 1, :])
                        else:
                            pe.wait_ge(w_split, 2)
                            w = (wk_c(w_h), wk_c(w_l))
                        split_matmul(nc, ps, w, (xh[:, b, :], xl[:, b, :])).then_inc(bank_filled, 1)
                    elif kind == "V":
                        b = item[1]
                        ps = claim(item)
                        for i in range(NI):
                            last = nc.tensor.matmul(ps[:, i * P:(i + 1) * P], xnT[:, b, i * P:(i + 1) * P],
                                                    wv[:], start=True, stop=True)
                        last.then_inc(bank_filled, 1)
                    elif kind == "Q":
                        b, h = jobs[item[1]]
                        ps = claim(item)
                        w = (wqk_h[:, 0, :], wqk_l[:, 0, :]) if causal else (wq_c(w_h, h), wq_c(w_l, h))
                        split_matmul(nc, ps, w, (xh[:, b, :], xl[:, b, :])).then_inc(bank_filled, 1)
                    elif kind == "AV":
                        _, j, k = item
                        b = jobs[j][0]
                        if k == 0:
                            pe.wait_ge(low_ready, NI * (j + 1))
                            pe.wait_ge(dve_used, ring.dve[("V", b)])
                            if causal:
                                pe.wait_ge(zeros_ready, 2)
                            if j >= 1:
                                pe.wait_ge(o_high, j)
                                if not causal:
                                    pe.wait_ge(o_low, j)
                        q0 = min(P * k, N - 2 * P) if causal else 0
                        last = split_matmul(nc, o_ps[:, q0:N], (VH[:, b % 2, k, :], VL[:, b % 2, k, :]),
                                            (WH[:, j % 2, k, q0:N], WL[:, j % 2, k, q0:N]),
                                            start=k == 0, stop=k == NI - 1)
                        if k == NI - 1:
                            last.then_inc(o_ready, 1)
                    elif kind == "OT":
                        ps = claim(item)
                        pe.wait_ge(o_high, item[1] + 1)
                        for i in range(NI):
                            last = nc.tensor.transpose(ps[:, i * P:(i + 1) * P], oT[:, i * P:(i + 1) * P], ident[:])
                        last.then_inc(bank_filled, 1)
                    elif kind == "OP":
                        j = item[1]
                        b, h = jobs[j]
                        pe.wait_ge(o_low, j + 1)
                        if h == 0 and b >= 1:
                            pe.wait_ge(y_taken, b)
                        if j == 0:
                            pe.wait_ge(w_split, 4)
                        ins = split_matmul(nc, y_ps[:], (wo_c(w_h, h), wo_c(w_l, h)),
                                           (OH[:, j % 2, :], OL[:, j % 2, :]), start=h == 0, stop=h == NQ - 1)
                        ins.then_inc(out_proj_done, 1)
                    elif kind in ("GATE", "UP"):
                        _, b, c = item
                        ps = claim(item)
                        wc = wg_c if kind == "GATE" else wu_c
                        if b == 0:
                            pe.wait_ge(w_split, 4)
                        split_matmul(nc, ps, (wc(w_h, c), wc(w_l, c)), (xh[:, b, :], xl[:, b, :]))\
                            .then_inc(bank_filled, 1)
                    elif kind == "DOWN":
                        b = item[1]
                        pe.wait_ge(dve_used, ring.dve[("UP", b, FC - 1)])
                        for c in range(FC):
                            last = split_matmul(nc, y_ps[:], (wd_c(w_h, c), wd_c(w_l, c)),
                                                (HH[:, c, :], HL[:, c, :]), start=False, stop=False)
                        last.then_inc(down_done, 1)
                    elif kind == "YT":
                        b = item[1]
                        ps = claim(item)
                        pe.wait_ge(y_taken, b + 1)
                        for i in range(NI):
                            last = nc.tensor.transpose(ps[:, i * P:(i + 1) * P], oT[:, i * P:(i + 1) * P], ident[:])
                        last.then_inc(bank_filled, 1)
                    elif kind == "TR":
                        T = item[1]
                        j, i = tiles[T]
                        n = i + 1 if causal else NI
                        pe.wait_ge(weights_ready, T + 1)
                        if T >= 2:
                            pe.wait_ge(low_ready, T - 1)
                        for k in range(n):
                            last = nc.tensor.transpose(wT_ps[:, T % 2, k * P:(k + 1) * P],
                                                       weights[:, T % NP, k * P:(k + 1) * P], ident[:])
                        last.then_inc(wT_ready, 1)
                    elif kind == "S":
                        T = item[1]
                        j, i = tiles[T]
                        b = jobs[j][0]
                        pe.wait_ge(dve_used, ring.dve[("Q", j)])
                        if T >= 2:
                            pe.wait_ge(exp_ready, T - 1)
                        qh, ql = QH[:, j % 2, i * P:(i + 1) * P], QL[:, j % 2, i * P:(i + 1) * P]
                        if causal:
                            n = max(P * (i + 1), 2 * P)
                            ps = scores[:, T % 2, 0:n]
                            nc.tensor.matmul(ps, qh, KH[:, b % 2, 0:n], start=True, stop=False)
                            nc.tensor.matmul(ps, ql, KH[:, b % 2, 0:n], start=False, stop=False)
                            nc.tensor.matmul(scores[:, T % 2, i * P:(i + 1) * P], keep["ident_bf"][:],
                                             keep["masks"][:, 0, :], start=False, stop=True)\
                                .then_inc(scores_ready, 1)
                        else:
                            split_matmul(nc, scores[:, T % 2, :], (qh, ql),
                                         (KH[:, b % 2, :], KL[:, b % 2, :])).then_inc(scores_ready, 1)


L0_AT = {
    "STATS": -7.261, "CONSTS": -6.597, "LN": -3.484, ("W", 0): -1.942, "K": -1.736, "Q": -1.044,
    "S": 0.5, "E": 1.298, "I": 1.712, "TR": 3.985, ("W", 1): 6.07, "V": 6.545, ("AV", 0): 8.579,
    ("AV", 1): 9.699, ("AV", 2): 9.716, "HX": 9.726, ("AV", 3): 11.102, "O": 11.184, "OT": 11.932,
}
L1_AT = {
    "X1": -18.38, "STATS": -11.45, ("W", 0): -7.948, "LN": -6.883, ("W", 1): -4.137, "K": -1.953,
    "Q": -1.05, "S": 0.5, "E": 1.735, "I": 1.79, "V": 2.022, "TR": 4.118, ("GATE", 0): 6.422,
    ("UP", 0): 7.685, ("AV", 0): 8.574, ("AV", 1): 9.098, ("GATE", 1): 9.779, ("AV", 2): 9.979,
    ("AV", 3): 10.51, "O": 10.797, ("UP", 1): 12.148, "OP": 12.375, ("GATE", 2): 36.09,
    ("UP", 2): 36.239, "DOWN": 38.532, "YT": 40.852,
}
WIN_AT = {
    ("QK", 0): -5.248, ("QK", 1): -5.085, ("QK", 2): -4.369, ("QK", 3): -4.132, ("NORM", 0): -3.247,
    ("NORM", 1): -3.241, ("NORM", 2): -2.965, ("NA", 0): -2.955, ("NA", 1): -2.338, ("NA", 2): -2.171,
    ("NA", 3): -1.687, ("QT", 0): -0.988, ("QT", 1): -0.983, ("QT", 2): -0.78, ("QT", 3): -0.465,
    "S": 0.5, ("VP", 0): 0.827, "E": 0.931, ("VP", 1): 1.02, "I": 1.549, ("VP", 2): 1.593,
    ("VP", 3): 2.307, "TR": 2.565, "WO": 3.19, "LT": 3.642, "AV": 3.704, "LS": 3.805, "LN": 6.037,
    "LB": 6.842, ("G", 0): 7.983, ("A", 0): 8.122, ("G", 1): 8.418, ("A", 1): 8.529, ("G", 2): 8.539,
    ("A", 2): 8.689, "W2": 10.037, "HS": 10.568,
}
W_LAYER = 3 * INNER + 4 * P + 2 * HID + 3 * P
COLS = 3 + 6


def windowed_block(nc, keep):
    tag = "win"
    xresT, hh, hl, h32, ident = keep["xresT"], keep["hh"], keep["hl"], keep["h32"], keep["ident"]
    cols = keep["cols"]
    S = DEPTH * B
    U = 2 * S
    TU = NW // 2
    NT = U * TU
    unit_step = lambda u: u // 2
    NP, RB = 3, 4

    line = []
    for u in range(U):
        g = TU * u
        line += [(g + WIN_AT["QK", i], ("QK", u, i)) for i in range(NI)]
        line += [(g + WIN_AT["NORM", i], ("NORM", u, i)) for i in range(3)]
        line += [(g + WIN_AT["NA", i], ("NA", u, i)) for i in range(NI)]
        line += [(g + WIN_AT["QT", i], ("QT", u, i // 2, i % 2)) for i in range(NI)]
        line += [(g + WIN_AT["VP", i], ("VP", u, i)) for i in range(NI)]
    for g in range(NT):
        line += [(g + WIN_AT[kind], (kind, g)) for kind in ("S", "E", "I", "TR", "AV")]
    for s in range(S):
        g = 2 * TU * (s + 1)
        line += [(g + WIN_AT[kind], (kind, s)) for kind in ("WO", "LT", "LS", "LN", "LB", "W2")]
        line += [(g + WIN_AT[kind, c], (kind, s, c)) for kind in ("G", "A") for c in range(3)]
        if s < B:
            line.append((g + WIN_AT["HS"], ("HS", s)))
    items = [item for _, item in sorted(line)]
    acts = {"QK", "QT", "VP", "AV", "LT", "LB", "G"}
    dves = {"QK", "AV", "WO", "A", "W2"}
    ring = Ring(RB, [x for x in items if x[0] not in ("TR", "S", "I", "E", "NORM", "NA", "LS", "LN", "HS")],
                lambda x: x[0] in acts, lambda x: x[0] in dves)

    def layer_w(w, l):
        o = l * W_LAYER
        qkv = w[:, o:o + 3 * INNER].rearrange("p (m n) -> p m n", m=3)
        wo = w[:, o + 3 * INNER:o + 3 * INNER + 4 * P].rearrange("p (c n) -> p c n", c=4)
        o += 3 * INNER + 4 * P
        w1 = w[:, o:o + 2 * HID]
        w2 = w[:, o + 2 * HID:o + 2 * HID + 3 * P].rearrange("p (c n) -> p c n", c=3)
        return qkv, wo, w1, w2

    LWH = [layer_w(keep["w_h"], l) for l in range(DEPTH)]
    LWL = [layer_w(keep["w_l"], l) for l in range(DEPTH)]

    with ExitStack() as ctx:
        def sb(name, shape, dt=F32):
            return ctx.enter_context(nc.sbuf_tensor(f"{tag}_{name}", shape, dt))

        def psum(name, shape):
            return ctx.enter_context(nc.psum_tensor(f"{tag}_{name}", shape, F32))

        def sem(name):
            return ctx.enter_context(nc.semaphore(f"{tag}_{name}"))

        scores = psum("scores", [P, 2, 4 * P])
        wT_ps = psum("wT_ps", [P, 2, 4 * P])
        bank = psum("bank", [P, RB, 512])
        QBD = sb("QBD", [P, 2, 2, NW, 2, WIN])
        KT = sb("KT", [P, 2, 2, N])
        V = sb("V", [P, 2, NW - 1, 2 * P])
        rot = sb("rot", [P, NI, 2 * 2 * P])
        rot_a = sb("rot_a", [P, 2, 512])
        rot_b = sb("rot_b", [P, 2, 512])
        sq = sb("sq", [P, 2, 512])
        sumsq = sb("sumsq", [P, 2, 32])
        norm_inv = sb("norm_inv", [P, 2, 32])
        newton = sb("newton", [P, 32])
        negmax = sb("negmax", [P, 8, 4])
        rowsum = sb("rowsum", [P, 8, 4])
        inv = sb("inv", [P, 8, 4])
        weights = sb("weights", [P, NP, 4 * P])
        wT = sb("wT", [P, 2, 4 * P])
        OTH, OTL = sb("OTH", [P, 4, N], F32R), sb("OTL", [P, 4, N], F32R)
        stats = sb("stats", [P, NI, 6])
        mv = sb("mv", [P, NI, 2])
        var = sb("var", [P, NI])
        rstd = sb("rstd", [P, NI])
        minus_half = sb("minus_half", [P, NI])
        h_tok = sb("h_tok", [P, NI, P])
        n32 = sb("n32", [P, N])
        nH, nL = sb("nH", [P, N], F32R), sb("nL", [P, N], F32R)
        gelu_g = sb("gelu_g", [P, 3, N])
        hid = sb("hid", [P, 2, N])
        HH, HL = sb("HH", [P, 3, N], F32R), sb("HL", [P, 3, N], F32R)

        dve_link = sem("dve_link")
        zeros_ready = sem("zeros_ready")
        bank_filled = sem("bank_filled")
        act_used = sem("act_used")
        dve_used = sem("dve_used")
        sumsq_done = sem("sumsq_done")
        rot_added = sem("rot_added")
        norm_ready = sem("norm_ready")
        norm_applied = sem("norm_applied")
        scores_ready = sem("scores_ready")
        max_ready = sem("max_ready")
        exp_ready = sem("exp_ready")
        inv_ready = sem("inv_ready")
        weights_ready = sem("weights_ready")
        wT_ready = sem("wT_ready")
        wT_copied = sem("wT_copied")
        h32_ready = sem("h32_ready")
        h_tok_stats = sem("h_tok_stats")
        var_ready = sem("var_ready")
        rstd_ready = sem("rstd_ready")
        hn_ready = sem("hn_ready")
        nH_ready = sem("nH_ready")
        n_ready = sem("n_ready")
        HH_ready = sem("HH_ready")
        hid_ready = sem("hid_ready")
        hh_ready = sem("hh_ready")
        h_split = sem("h_split")

        with nc.Block() as block:

            @block.gpsimd
            def _(pool):
                nc.gpsimd.memset(QBD[:], 0.0).then_inc(zeros_ready, 1)
                nc.gpsimd.memset(minus_half[:], -0.5).then_inc(zeros_ready, 1)
                for item in items:
                    kind = item[0]
                    if kind == "QK":
                        _, u, i = item
                        n = NI * u + i
                        pool.wait_ge(dve_used, ring.dve[item])
                        if u >= 1:
                            pool.wait_ge(bank_filled, ring.filled(("QT", u - 1, 1, 1)))
                        nc.gpsimd.tensor_tensor(rot[:, i, :], rot_a[:, n % 2, :], rot_b[:, n % 2, :], ALU.add)\
                            .then_inc(rot_added, 1)
                    elif kind == "NA":
                        _, u, i = item
                        pool.wait_ge(norm_ready, u + 1)
                        pool.wait_ge(rot_added, NI * (u + 1))
                        r = rot[:, i, :].rearrange("p (h d) -> p h d", d=DH)
                        k = norm_inv[:, u % 2, 8 * i:8 * i + 8].unsqueeze(2).to_broadcast([P, 8, DH])
                        nc.gpsimd.tensor_tensor(r, r, k, ALU.mult).then_inc(norm_applied, 1)
                    elif kind == "HS":
                        s = item[1]
                        pool.wait_ge(hh_ready, s + 1)
                        nc.gpsimd.tensor_tensor(hl[:, s, :], h32[:, 0:N], f32(hh[:, s, :]), ALU.subtract)\
                            .then_inc(h_split, 1)
                    elif kind == "LB":
                        s = item[1]
                        pool.wait_ge(nH_ready, s + 1)
                        nc.gpsimd.tensor_tensor(nL[:], n32[:], f32(nH[:]), ALU.subtract).then_inc(n_ready, 1)
                    elif kind == "A":
                        _, s, c = item
                        m = CH[c][1]
                        pool.wait_ge(HH_ready, 3 * s + c + 1)
                        nc.gpsimd.tensor_tensor(HL[0:m, c, :], hid[0:m, (s + c) % 2, :], f32(HH[0:m, c, :]),
                                                ALU.subtract).then_inc(hid_ready, 1)
                    elif kind == "LS":
                        s = item[1]
                        pool.wait_ge(var_ready, s + 1)
                        if s >= 1:
                            pool.wait_ge(hn_ready, s)
                        pool.wait_ge(zeros_ready, 2)
                        nc.gpsimd.tensor_tensor(rstd[:], var[:], minus_half[:], ALU.pow).then_inc(rstd_ready, 1)
                    elif kind == "I":
                        T = item[1]
                        pool.wait_ge(inv_ready, T + 1)
                        w = weights[:, T % NP, :].rearrange("p (c k) -> p c k", k=P)
                        k = inv[:, T % 8, :].unsqueeze(2).to_broadcast([P, 4, P])
                        nc.gpsimd.tensor_tensor(w, w, k, ALU.mult).then_inc(weights_ready, 1)

            @block.scalar
            def _(act):
                h32_count = 0

                def shifted(b):
                    nc.scalar.copy(h32[0:64, 0:N], xresT[0:64, b, :])
                    nc.scalar.copy(h32[64:128, 1:N + 1], xresT[64:128, b, :]).then_inc(h32_ready, 1)

                for item in items:
                    kind = item[0]
                    if item in ring.act:
                        act.wait_ge(bank_filled, ring.filled(item))
                        ps = bank[:, ring.bank(item), :]
                    if kind == "QK":
                        _, u, i = item
                        n = NI * u + i
                        if n >= 2:
                            act.wait_ge(sumsq_done, n - 1)
                        nc.scalar.activation(sq[:, n % 2, :], ps, ACT.Square).then_inc(act_used, 1)
                    elif kind == "VP":
                        _, u, v = item
                        if u >= 2:
                            act.wait_ge(bank_filled, ring.filled(("AV", TU * (u - 1) - 1)))
                        n = 2 if v < NI - 1 else 1
                        nc.scalar.copy(V[:, u % 2, 2 * v:2 * v + n, :],
                                       ps[:, 0:n * 2 * P].rearrange("p (j d) -> p j d", j=n)).then_inc(act_used, 1)
                    elif kind == "QT" and item[2] == 1:
                        _, u, _, p = item
                        if u >= 2:
                            act.wait_ge(scores_ready, TU * (u - 1))
                        nc.scalar.copy(KT[:, u % 2, p, :], ps).then_inc(act_used, 1)
                    elif kind == "QT":
                        _, u, _, p = item
                        if u >= 2:
                            act.wait_ge(scores_ready, TU * (u - 1))
                        act.wait_ge(zeros_ready, 1)
                        src = ps.rearrange("p (w q) -> p w q", w=NW)
                        nc.scalar.copy(QBD[0:64, u % 2, p, :, 0, :], src[0:64])
                        nc.scalar.copy(QBD[64:128, u % 2, p, :, 1, :], src[64:128]).then_inc(act_used, 1)
                    elif kind == "AV":
                        g = item[1]
                        u, t = g // TU, g % TU
                        s = unit_step(u)
                        if s >= 1:
                            act.wait_ge(bank_filled, ring.filled(("WO", s - 1)))
                        p0 = 2 * (u % 2)
                        nc.scalar.copy(OTH[:, p0:p0 + 2, t * P:(t + 1) * P],
                                       ps[:, 0:2 * P].rearrange("p (c t) -> p c t", c=2)).then_inc(act_used, 1)
                    elif kind == "WO":
                        s = item[1]
                        act.wait_ge(dve_used, ring.dve[item])
                        if s >= 1 and (s - 1) < B:
                            act.wait_ge(h_split, s)
                        if s >= 1:
                            act.wait_ge(bank_filled, ring.filled(("LT", s - 1)))
                        shifted(s % B)
                    elif kind == "LB":
                        s = item[1]
                        l = s // B
                        if s >= 1:
                            act.wait_ge(n_ready, s)
                        nc.scalar.activation(n32[:], ps, ACT.Identity, bias=cols[:, l, 1:2], scale=cols[:, l, 0:1])\
                            .then_inc(act_used, 1)
                    elif kind == "G":
                        _, s, c = item
                        m = CH[c][1]
                        if s >= 1:
                            act.wait_ge(dve_used, ring.dve[("A", s - 1, c)])
                        nc.scalar.activation(gelu_g[0:m, c, :], ps[0:m], ACT.Gelu, bias=cols[0:m, s // B, 6 + c:7 + c])\
                            .then_inc(act_used, 1)
                    elif kind == "W2" and item[1] < B:
                        s = item[1]
                        act.wait_ge(dve_used, ring.dve[item])
                        act.wait_ge(bank_filled, ring.filled(("LT", s)))
                        shifted(s % B)
                    elif kind == "LT":
                        s = item[1]
                        if s >= 1:
                            act.wait_ge(bank_filled, ring.filled(("LB", s - 1)))
                        nc.scalar.copy(h_tok[:], ps.rearrange("p (i d) -> p i d", d=P)).then_inc(act_used, 1)
                    elif kind == "E":
                        T = item[1]
                        act.wait_ge(max_ready, T + 1)
                        if T >= NP:
                            act.wait_ge(wT_ready, T - NP + 1)
                        for c in range(4):
                            last = nc.scalar.activation(weights[:, T % NP, c * P:(c + 1) * P],
                                                        scores[:, T % 2, c * P:(c + 1) * P], ACT.Exp,
                                                        bias=negmax[:, T % 8, c:c + 1],
                                                        accum_out=rowsum[:, T % 8, c:c + 1])
                        last.then_inc(exp_ready, 1)

            @block.vector
            def _(dve):
                link = chained(dve, dve_link, [0])
                h32_uses = 0
                for item in items:
                    kind = item[0]
                    if item in ring.dve:
                        dve.wait_ge(bank_filled, ring.filled(item))
                        ps = bank[:, ring.bank(item), :]
                    if kind == "QK":
                        _, u, i = item
                        l = unit_step(u) // B
                        n = NI * u + i
                        dve.wait_ge(act_used, ring.act[item])
                        if n >= 2:
                            dve.wait_ge(rot_added, n - 1)
                        heads = ps.rearrange("p (m h d) -> p m h d", m=2, h=4)
                        cos = keep["tables"][:, l, 0, :, i, :].unsqueeze(2).to_broadcast([P, 2, 4, DH])
                        nc.vector.tensor_tensor(rot_a[:, n % 2, :].rearrange("p (m h d) -> p m h d", m=2, h=4),
                                                heads, cos, ALU.mult)
                        H2 = DH // 2
                        for half in range(2):
                            o, f = half * H2, (1 - half) * H2
                            sin = keep["tables"][:, l, 1, :, i, o:o + H2].unsqueeze(2).to_broadcast([P, 2, 4, H2])
                            out = rot_b[:, n % 2, :].rearrange("p (m h d) -> p m h d", m=2, h=4)
                            last = nc.vector.tensor_tensor(out[:, :, :, o:o + H2], heads[:, :, :, f:f + H2], sin,
                                                           ALU.mult)
                        last.then_inc(dve_used, 1)
                        if i == 0 and u >= 2:
                            dve.wait_ge(norm_ready, u - 1)
                        nc.vector.tensor_reduce(sumsq[:, u % 2, 8 * i:8 * i + 8],
                                                sq[:, n % 2, :].rearrange("p (h d) -> p h d", d=DH), AX_X,
                                                ALU.add).then_inc(sumsq_done, 1)
                    elif kind == "NORM":
                        _, u, part = item
                        v, y, t = sumsq[:, u % 2, :], norm_inv[:, u % 2, :], newton[:]
                        if part == 0:
                            dve.wait_ge(sumsq_done, NI * (u + 1))
                            if u >= 2:
                                dve.wait_ge(norm_applied, NI * (u - 1))
                            link(nc.vector.tensor_scalar(v, v, NORM_FLOOR, None, ALU.max))
                            link(nc.vector.tensor_scalar(y.bitcast(I32), v.bitcast(I32), 1, None,
                                                         ALU.logical_shift_right))
                            link(nc.vector.tensor_scalar(y.bitcast(I32), y.bitcast(I32), -1.0, RSQRT_MAGIC,
                                                         ALU.mult, ALU.add))
                        link(nc.vector.scalar_tensor_tensor(t, y, -0.5, y, ALU.mult, ALU.mult))
                        link(nc.vector.tensor_tensor(t, t, v, ALU.mult))
                        last = nc.vector.scalar_tensor_tensor(y, t, 1.5, y, ALU.add, ALU.mult)
                        if part < 2:
                            link(last)
                        else:
                            last.then_inc(norm_ready, 1)
                    elif kind == "AV":
                        g = item[1]
                        u, t = g // TU, g % TU
                        dve.wait_ge(act_used, ring.act[item])
                        p0 = 2 * (u % 2)
                        nc.vector.tensor_tensor(OTL[:, p0:p0 + 2, t * P:(t + 1) * P],
                                                ps[:, 0:2 * P].rearrange("p (c t) -> p c t", c=2),
                                                f32(OTH[:, p0:p0 + 2, t * P:(t + 1) * P]), ALU.subtract)\
                            .then_inc(dve_used, 1)
                    elif kind == "WO":
                        s = item[1]
                        b = s % B
                        nc.vector.tensor_tensor(xresT[:, b, :], ps, xresT[:, b, :], ALU.add).then_inc(dve_used, 1)
                    elif kind == "LS":
                        s = item[1]
                        dve.wait_ge(act_used, ring.act[("LT", s)])
                        if s >= 1:
                            dve.wait_ge(hn_ready, s)
                        for i in range(NI):
                            nc.vector.bn_stats(stats[:, i, :], h_tok[:, i, :]).then_inc(h_tok_stats, 1)
                        for i in range(NI):
                            dve.wait_ge(h_tok_stats, 2 * NI * s + NI)
                            nc.vector.bn_aggr(mv[:, i, :], stats[:, i, :]).then_inc(h_tok_stats, 1)
                        dve.wait_ge(h_tok_stats, 2 * NI * (s + 1))
                        nc.vector.tensor_scalar(var[:], mv[:, :, 1], LN_EPS, None, ALU.add).then_inc(var_ready, 1)
                    elif kind == "LN":
                        s = item[1]
                        dve.wait_ge(rstd_ready, s + 1)
                        for i in range(NI):
                            last = nc.vector.tensor_scalar(h_tok[:, i, :], h_tok[:, i, :], mv[:, i, 0:1],
                                                           rstd[:, i:i + 1], ALU.subtract, ALU.mult)
                        last.then_inc(hn_ready, 1)
                    elif kind == "LB":
                        s = item[1]
                        dve.wait_ge(act_used, ring.act[item])
                        if s >= 1:
                            dve.wait_ge(bank_filled, ring.filled(("A", s - 1, 2)))
                        nc.vector.tensor_copy(nH[:], n32[:]).then_inc(nH_ready, 1)
                    elif kind == "A":
                        _, s, c = item
                        m = CH[c][1]
                        dve.wait_ge(act_used, ring.act[("G", s, c)])
                        if 3 * s + c >= 2:
                            dve.wait_ge(hid_ready, 3 * s + c - 1)
                        nc.vector.scalar_tensor_tensor(hid[0:m, (s + c) % 2, :], ps[0:m], cols[0:m, s // B, 3 + c:4 + c],
                                                       gelu_g[0:m, c, :], ALU.add, ALU.mult).then_inc(dve_used, 1)
                        dve.wait_ge(dve_used, ring.dve[item])
                        if s >= 1:
                            dve.wait_ge(bank_filled, ring.filled(("W2", s - 1)))
                        nc.vector.tensor_copy(HH[0:m, c, :], hid[0:m, (s + c) % 2, :]).then_inc(HH_ready, 1)
                    elif kind == "W2":
                        s = item[1]
                        l, b = s // B, s % B
                        dve.wait_ge(h32_ready, h32_uses + 1)
                        h32_uses += 1
                        nc.vector.scalar_tensor_tensor(xresT[:, b, :], ps, cols[:, l, 2:3], xresT[:, b, :], ALU.add,
                                                       ALU.add).then_inc(dve_used, 1)
                        if l == 0:
                            h32_uses += 1
                    elif kind == "HS":
                        s = item[1]
                        dve.wait_ge(h32_ready, 2 * (s + 1))
                        dve.wait_ge(bank_filled, ring.filled(("VP", 2 * s + 1, NI - 1)))
                        nc.vector.tensor_copy(hh[:, s, :], h32[:, 0:N]).then_inc(hh_ready, 1)
                    elif kind == "S":
                        T = item[1]
                        dve.wait_ge(scores_ready, T + 1)
                        if T >= 8:
                            dve.wait_ge(exp_ready, T - 7)
                        nc.vector.tensor_reduce(negmax[:, T % 8, :],
                                                scores[:, T % 2, :].rearrange("p (c k) -> p c k", k=P), AX_X,
                                                ALU.max, negate=True).then_inc(max_ready, 1)
                    elif kind == "TR":
                        T = item[1]
                        dve.wait_ge(wT_ready, T + 1)
                        if T >= 2:
                            dve.wait_ge(bank_filled, ring.filled(("AV", T - 2)))
                        nc.vector.tensor_copy(wT[:, T % 2, :], wT_ps[:, T % 2, :]).then_inc(wT_copied, 1)
                    elif kind == "I":
                        T = item[1]
                        dve.wait_ge(exp_ready, T + 1)
                        if T >= 8:
                            dve.wait_ge(weights_ready, T - 7)
                        nc.vector.reciprocal(inv[:, T % 8, :], rowsum[:, T % 8, :]).then_inc(inv_ready, 1)

            @block.tensor
            def _(pe):
                for item in items:
                    kind = item[0]
                    if item in ring.at:
                        old = ring.before(item)
                        if old is not None:
                            if old in ring.dve:
                                pe.wait_ge(dve_used, ring.dve[old])
                            if old in ring.act:
                                pe.wait_ge(act_used, ring.act[old])
                        ps = bank[:, ring.bank(item), :]
                    if kind == "QK":
                        _, u, i = item
                        l, b = unit_step(u) // B, unit_step(u) % B
                        if l:
                            pe.wait_ge(h_split, b + 1)
                        c = (u % 2) * 2 * P
                        tok = slice(i * P, (i + 1) * P)
                        split_matmul(nc, ps, (hh[:, b, tok], hl[:, b, tok]),
                                     (LWH[l][0][:, 0:2, c:c + 2 * P], LWL[l][0][:, 0:2, c:c + 2 * P]))\
                            .then_inc(bank_filled, 1)
                    elif kind == "VP":
                        _, u, v = item
                        l, b = unit_step(u) // B, unit_step(u) % B
                        c = (u % 2) * 2 * P
                        for j in range(2 * v, min(2 * v + 2, NW - 1)):
                            tok = slice(j * WIN, j * WIN + P)
                            o = (j % 2) * 2 * P
                            last = split_matmul(nc, ps[:, o:o + 2 * P], (hh[:, b, tok], hl[:, b, tok]),
                                                (LWH[l][0][:, 2, c:c + 2 * P], LWL[l][0][:, 2, c:c + 2 * P]))
                        last.then_inc(bank_filled, 1)
                    elif kind == "QT":
                        _, u, m, p = item
                        pe.wait_ge(norm_applied, NI * (u + 1))
                        for i in range(NI):
                            c = (2 * m + p) * P
                            last = nc.tensor.transpose(ps[:, i * P:(i + 1) * P], rot[:, i, c:c + P], ident[:])
                        last.then_inc(bank_filled, 1)
                    elif kind == "AV":
                        g = item[1]
                        u, t = g // TU, g % TU
                        pe.wait_ge(wT_copied, g + 1)
                        pe.wait_ge(act_used, ring.act[("VP", u, NI - 1)])
                        for w in range(2):
                            j = max(2 * t + w - 1, 0)
                            for p in range(2):
                                for h in range(2):
                                    c = (2 * w + p) * P + h * WIN
                                    d = (2 * p + h) * DH
                                    last = nc.tensor.matmul(ps[h * 64:h * 64 + 64, p * P + w * WIN:p * P + (w + 1) * WIN],
                                                            V[:, u % 2, j, d:d + DH], wT[:, g % 2, c:c + WIN],
                                                            start=True, stop=True)
                        last.then_inc(bank_filled, 1)
                    elif kind == "WO":
                        s = item[1]
                        l = s // B
                        pe.wait_ge(dve_used, ring.dve[("AV", 2 * TU * (s + 1) - 1)])
                        for c in range(4):
                            last = split_matmul(nc, ps, (LWH[l][1][:, c, :], LWL[l][1][:, c, :]),
                                                (OTH[:, c, :], OTL[:, c, :]), start=c == 0, stop=c == 3)
                        last.then_inc(bank_filled, 1)
                    elif kind == "LT":
                        s = item[1]
                        pe.wait_ge(h32_ready, s + 1 + min(s, B))
                        for i in range(NI):
                            last = nc.tensor.transpose(ps[:, i * P:(i + 1) * P], h32[:, i * P:(i + 1) * P], ident[:])
                        last.then_inc(bank_filled, 1)
                    elif kind == "LB":
                        s = item[1]
                        pe.wait_ge(hn_ready, s + 1)
                        for i in range(NI):
                            last = nc.tensor.transpose(ps[:, i * P:(i + 1) * P], h_tok[:, i, :], ident[:])
                        last.then_inc(bank_filled, 1)
                    elif kind in ("G", "A"):
                        _, s, c = item
                        l = s // B
                        pe.wait_ge(n_ready, s + 1)
                        c0, m = CH[c]
                        c0 += HID if kind == "G" else 0
                        split_matmul(nc, ps[0:m], (LWH[l][2][:, c0:c0 + m], LWL[l][2][:, c0:c0 + m]),
                                     (nH[:], nL[:])).then_inc(bank_filled, 1)
                    elif kind == "W2":
                        s = item[1]
                        l = s // B
                        pe.wait_ge(hid_ready, 3 * (s + 1))
                        for c in range(3):
                            m = CH[c][1]
                            last = split_matmul(nc, ps, (LWH[l][3][0:m, c, :], LWL[l][3][0:m, c, :]),
                                                (HH[0:m, c, :], HL[0:m, c, :]), start=c == 0, stop=c == 2)
                        last.then_inc(bank_filled, 1)
                    elif kind == "TR":
                        T = item[1]
                        pe.wait_ge(weights_ready, T + 1)
                        if T >= 2:
                            pe.wait_ge(wT_copied, T - 1)
                        for c in range(4):
                            last = nc.tensor.transpose(wT_ps[:, T % 2, c * P:(c + 1) * P],
                                                       weights[:, T % NP, c * P:(c + 1) * P], ident[:])
                        last.then_inc(wT_ready, 1)
                    elif kind == "S":
                        T = item[1]
                        u, t = T // TU, T % TU
                        if t == 0:
                            pe.wait_ge(act_used, ring.act[("QT", u, 1, 1)])
                        if T >= 2:
                            pe.wait_ge(exp_ready, T - 1)
                        for w in range(2):
                            m = 1 if (t == 0 and w == 0) else 2
                            mask = keep["masks"][:, m:m + 1, :].to_broadcast([P, 2, P])
                            nc.tensor.matmul(scores[:, T % 2, w * 2 * P:(w + 1) * 2 * P], keep["ident_bf"][:],
                                             mask, start=w == 0, stop=False)
                        for w in range(2):
                            k0 = max(2 * t + w - 1, 0) * WIN
                            for p in range(2):
                                c = (2 * w + p) * P
                                last = nc.tensor.matmul(
                                    scores[:, T % 2, c:c + P],
                                    QBD[:, u % 2, p, 2 * t + w, :, :].rearrange("p h q -> p (h q)"),
                                    KT[:, u % 2, p, k0:k0 + P], start=False, stop=w == 1 and p == 1)
                        last.then_inc(scores_ready, 1)


def build(nc, io):
    with ExitStack() as ctx:
        def sb(name, shape, dt=F32):
            return ctx.enter_context(nc.sbuf_tensor(name, shape, dt))

        keep = {
            "x_tok": sb("x_tok", [P, B * NI, P]),
            "xresT": sb("xresT", [P, B, N]),
            "ident": sb("ident", [P, P]),
        }
        with ExitStack() as inner:
            def sb(name, shape, dt=F32):
                return inner.enter_context(nc.sbuf_tensor(name, shape, dt))

            keep |= {
                "ident_bf": sb("ident_bf", [P, P], BF16),
                "masks": sb("masks", [P, 3, P], BF16),
                "hh": sb("hh", [P, B, N], F32R),
                "hl": sb("hl", [P, B, N], F32R),
                "h32": sb("h32", [P, N + 4]),
                "tables": sb("tables", [P, DEPTH, 2, 2, NI, DH]),
                "cols": sb("cols", [P, DEPTH, COLS]),
                "w_h": sb("w_h", [P, DEPTH * W_LAYER], F32R),
                "w_l": sb("w_l", [P, DEPTH * W_LAYER], F32R),
            }
            attention_block(nc, "l0", keep, io["l0"], True)
            windowed_block(nc, keep)
        attention_block(nc, "l1", keep, io["l1"], False)


def _constants():
    import numpy as np

    p, k = np.arange(P)[:, None], np.arange(P)[None, :]
    q = p % WIN
    masks = np.stack([np.where(k > p, MASKED, 0.0),
                      np.where(k > q, MASKED, 0.0),
                      np.where((k > q + WIN) | (k < q), MASKED, 0.0)], 1)
    f = np.float32
    half = np.arange(0, DH, 2, dtype=f)
    inv_freq = (f(1.0) / f(10000.0) ** (half / f(DH))).astype(f)
    t = np.arange(N, dtype=f)
    freqs = t[:, None] * inv_freq[None, :]
    base = ((half + f(0.4 * DH)) / f(1.4 * DH)).astype(f)
    power = (t - f(N // 2)) / f(WIN // 2)
    scale = base[None, :] ** power[:, None]
    two = lambda a: np.concatenate([a, a], -1)
    cos, sin, scale = two(np.cos(freqs)), two(np.sin(freqs)), two(scale)
    sin[:, :DH // 2] *= -1
    rot = np.stack([np.stack([8.0 * cos * scale, cos / scale], 0),
                    np.stack([8.0 * sin * scale, sin / scale], 0)], 0)
    rot = rot.reshape(2, 2, NI, P, DH).transpose(3, 0, 1, 2, 4)
    c = np.ascontiguousarray
    return np.eye(P, dtype=f), c(masks.astype(f)), c(rot.astype(f))


def kernel(**a):
    import numpy as np
    import concourse.bacc as bacc
    from concourse import mybir as mb
    from concourse.bass_utils import run_bass_kernel_spmd as run

    a = {k: np.asarray(v) for k, v in a.items()}
    c = np.ascontiguousarray
    rows = lambda w: w.reshape(-1, P, w.shape[-1]).transpose(1, 0, 2).reshape(P, -1)

    ident, masks, rotary = _constants()
    layers, cols, scales = [], [], []
    pad = lambda v, n: np.concatenate([v, np.zeros((n - v.shape[0],) + v.shape[1:], v.dtype)])
    for l in range(DEPTH):
        layers += [a["L0_ffn_wqkv"][l], rows(a["L0_ffn_wo"][l]), a["L0_ffn_w1"][l],
                   rows(pad(a["L0_ffn_w2"][l], 3 * P))]
        b1 = a["L0_ffn_b1"][l]
        cols.append(np.stack([a["L0_ffn_ln_g"][l], a["L0_ffn_ln_b"][l], a["L0_ffn_b2"][l]]
                             + [pad(b1[o + s:o + s + n], P) for o in (0, HID) for s, n in CH], 1))
        per = []
        for s in (a["L0_ffn_q_scale"][l], a["L0_ffn_k_scale"][l]):
            per.append(np.stack([s, np.concatenate([s[DH // 2:], s[:DH // 2]])]))
        scales.append(np.stack(per))
    l0 = {
        "x": a["L0_attn_X"], "ident": ident, "masks": masks, "rotary": rotary,
        "qk_scales": c(np.broadcast_to(np.stack(scales)[None], (P, DEPTH, 2, 2, DH))),
        "cols": c(np.stack(cols, 1)), "Wq": a["L0_attn_Wq"], "Wk": a["L0_attn_Wk"], "Wv": a["L0_attn_Wv"],
        "w_all": c(np.concatenate(layers, 1)),
    }
    heads = lambda w: w.transpose(1, 0, 2).reshape(P, -1)
    float_w = np.concatenate([heads(a["L1_attn_proj_q"]), a["L1_attn_proj_k"],
                              heads(a["L1_attn_proj_o"].transpose(0, 2, 1))], 1)
    l1 = {
        "Wv": a["L1_attn_proj_v"],
        "w_all": c(np.concatenate([float_w, np.zeros((P, 3 * FF), np.float32)], 1)),
        "w_int": c(np.concatenate([a["L1_ffn_w_gate"].T, a["L1_ffn_w_up"].T, rows(a["L1_ffn_w_down"].T)], 1)),
    }
    nc = bacc.Bacc("TRN2", target_bir_lowering=False, num_devices=1)
    io, arrays = {}, {}
    for tag, group in (("l0", l0), ("l1", l1)):
        io[tag] = {}
        for name, value in group.items():
            value = c(value)
            arrays[f"{tag}_{name}_in"] = value
            io[tag][name] = nc.dram_tensor(f"{tag}_{name}_in", value.shape, mb.dt.from_np(value.dtype),
                                           kind="ExternalInput").ap()
    io["l1"]["out"] = nc.dram_tensor("out_dram", (B, N, P), F32, kind="ExternalOutput").ap()
    build(nc, io)
    return run(nc, [arrays], core_ids=[0]).results[0]["out_dram"]
```

```python
from contextlib import ExitStack

import concourse.bass as bass
from concourse import mybir

F32 = mybir.dt.float32
F32R = mybir.dt.float32r
BF16 = mybir.dt.bfloat16
I32 = mybir.dt.int32
ALU = mybir.AluOpType
ACT = mybir.ActivationFunctionType
AX_X = mybir.AxisListType.X

P = 128
B, N = 4, 512
NI = N // P
DQ = 64
DEPTH, HEADS, DH = 2, 8, 64
WIN = 64
NW = N // WIN
INNER = HEADS * DH
HID = 341
CH = [(0, 128), (128, 128), (256, 85)]
NQ = 8
FF = 384
FC = FF // P
MASKED = -1.0e30
LN_EPS = 1e-5
NORM_FLOOR = 1e-24
RSQRT_MAGIC = float(0x5F3759DF)


def f32(ap):
    return ap.bitcast(F32)


class Ring:

    def __init__(self, banks, order, act_order, dve_order):
        self.banks = banks
        self.order = order
        self.at = {job: j for j, job in enumerate(order)}
        self.act = {job: j + 1 for j, job in enumerate(act_order)}
        self.dve = {job: j + 1 for j, job in enumerate(dve_order)}

    def bank(self, job):
        return self.at[job] % self.banks

    def filled(self, job):
        return self.at[job] + 1

    def before(self, job):
        j = self.at[job] - self.banks
        return self.order[j] if j >= 0 else None


def split_matmul(nc, out, lhs, rhs, start=True, stop=True):
    (lh, ll), (rh, rl) = lhs, rhs
    nc.tensor.matmul(out, lh, rh, start=start, stop=False)
    nc.tensor.matmul(out, lh, rl, start=False, stop=False)
    return nc.tensor.matmul(out, ll, rh, start=False, stop=stop)


def chained(eng, sem, count):
    def link(ins):
        count[0] += 1
        ins.then_inc(sem, 1)
        eng.wait_ge(sem, count[0])
    return link


def layer_w(w, l):
    o = l * W_LAYER
    qkv = w[:, o:o + 3 * INNER].rearrange("p (m n) -> p m n", m=3)
    wo = w[:, o + 3 * INNER:o + 3 * INNER + 4 * P].rearrange("p (c n) -> p c n", c=4)
    o += 3 * INNER + 4 * P
    w1 = w[:, o:o + 2 * HID]
    w2 = w[:, o + 2 * HID:o + 2 * HID + 3 * P].rearrange("p (c n) -> p c n", c=3)
    return qkv, wo, w1, w2


def project_qk(nc, ps, keep, l, b, i, u):
    wh, wl = layer_w(keep["w_h"], l)[0], layer_w(keep["w_l"], l)[0]
    c = (u % 2) * 2 * P
    tok = slice(i * P, (i + 1) * P)
    return split_matmul(nc, ps, (keep["hh"][:, b, tok], keep["hl"][:, b, tok]),
                        (wh[:, 0:2, c:c + 2 * P], wl[:, 0:2, c:c + 2 * P]))


def rotate_on_dve(nc, ps, keep, l, i):
    heads = ps.rearrange("p (m h d) -> p m h d", m=2, h=4)
    cos = keep["tables"][:, l, 0, :, i, :].unsqueeze(2).to_broadcast([P, 2, 4, DH])
    nc.vector.tensor_tensor(keep["rot_a"][:, i % 2, :].rearrange("p (m h d) -> p m h d", m=2, h=4),
                            heads, cos, ALU.mult)
    H2 = DH // 2
    for half in range(2):
        o, f = half * H2, (1 - half) * H2
        sin = keep["tables"][:, l, 1, :, i, o:o + H2].unsqueeze(2).to_broadcast([P, 2, 4, H2])
        out = keep["rot_b"][:, i % 2, :].rearrange("p (m h d) -> p m h d", m=2, h=4)
        last = nc.vector.tensor_tensor(out[:, :, :, o:o + H2], heads[:, :, :, f:f + H2], sin, ALU.mult)
    return last


def sum_squares(nc, keep, u, i):
    return nc.vector.tensor_reduce(keep["sumsq"][:, u % 2, 8 * i:8 * i + 8],
                                   keep["sq"][:, i % 2, :].rearrange("p (h d) -> p h d", d=DH), AX_X, ALU.add)


def norm_part(nc, link, keep, u, part):
    v, y, t = keep["sumsq"][:, u % 2, :], keep["norm_inv"][:, u % 2, :], keep["newton"][:]
    if part == 0:
        link(nc.vector.tensor_scalar(v, v, NORM_FLOOR, None, ALU.max))
        link(nc.vector.tensor_scalar(y.bitcast(I32), v.bitcast(I32), 1, None, ALU.logical_shift_right))
        link(nc.vector.tensor_scalar(y.bitcast(I32), y.bitcast(I32), -1.0, RSQRT_MAGIC, ALU.mult, ALU.add))
    link(nc.vector.scalar_tensor_tensor(t, y, -0.5, y, ALU.mult, ALU.mult))
    link(nc.vector.tensor_tensor(t, t, v, ALU.mult))
    return nc.vector.scalar_tensor_tensor(y, t, 1.5, y, ALU.add, ALU.mult)


def add_rotation(nc, keep, i):
    return nc.gpsimd.tensor_tensor(keep["rot"][:, i, :], keep["rot_a"][:, i % 2, :], keep["rot_b"][:, i % 2, :],
                                   ALU.add)


def apply_norm(nc, keep, u, i):
    r = keep["rot"][:, i, :].rearrange("p (h d) -> p h d", d=DH)
    k = keep["norm_inv"][:, u % 2, 8 * i:8 * i + 8].unsqueeze(2).to_broadcast([P, 8, DH])
    return nc.gpsimd.tensor_tensor(r, r, k, ALU.mult)


def attention_block(nc, tag, keep, io, causal):
    x_tok, xresT, ident = keep["x_tok"], keep["xresT"], keep["ident"]
    heads = 1 if causal else NQ
    jobs = [(b, h) for b in range(B) for h in range(heads)]
    tiles = [(j, i) for j in range(len(jobs)) for i in range(NI)]
    NT = len(tiles)

    AT = L0_AT if causal else L1_AT
    NP = 3 if causal else 4
    B0 = 0 if causal else 1
    line = [(g + AT[kind], (kind, g)) for g in range(NT) for kind in ("S", "E", "I", "TR")]
    for j in range(len(jobs)):
        g = NI * j
        line += [(g + AT["Q"], ("Q", j)), (g + AT["O"], ("O", j))]
        line += [(g + AT["AV", k], ("AV", j, k)) for k in range(NI)]
        kind = "OT" if causal else "OP"
        line.append((g + AT[kind], (kind, j)))
    for b in range(B):
        g = heads * NI * b
        kinds = ("STATS", "LN", "XL", "K", "V") + (("HX",) if causal else ("X1", "DOWN", "YT"))
        line += [(g + AT[kind], (kind, b)) for kind in kinds
                 if b >= B0 or kind not in ("X1", "STATS", "LN", "XL")]
        if not causal:
            line += [(g + AT[kind, c], (kind, b, c)) for kind in ("GATE", "UP") for c in range(FC)]
    line += [(AT["W", n], ("W", n)) for n in range(W_PARTS if causal else 1)]
    if causal:
        line += [(AT[kind], (kind,)) for kind in ("QKW", "CONSTS", "TABLES")]
        line += [(AT["QK", i], ("QK", i)) for i in range(NI)] + [(AT["NA", i], ("NA", i)) for i in range(NI)]
        line += [(AT["NORM", i], ("NORM", i)) for i in range(3)]
    items = [item for _, item in sorted(line)]
    by_act = {"LN", "K", "V", "Q", "GATE", "QK"}
    by_dve = {"K", "V", "Q", "X1", "OT", "YT", "UP", "GATE", "QK"}
    RB = 3 if causal else 2
    ring = Ring(RB, [x for x in items if x[0] in by_act | by_dve], [x for x in items if x[0] in by_act],
                [x for x in items if x[0] in by_dve])

    with ExitStack() as ctx:
        def sb(name, shape, dt=F32):
            return ctx.enter_context(nc.sbuf_tensor(f"{tag}_{name}", shape, dt))

        def psum(name, shape):
            return ctx.enter_context(nc.psum_tensor(f"{tag}_{name}", shape, F32))

        def sem(name):
            return ctx.enter_context(nc.semaphore(f"{tag}_{name}"))

        scores = psum("scores", [P, 2, 512])
        wT_ps = psum("wT_ps", [P, 2, 512])
        bank = psum("bank", [P, RB, 512])
        o_ps = psum("o_ps", [P, 512])
        if not causal:
            y_ps = psum("y_ps", [P, 512])

        xn_tok = sb("xn_tok", [P, NI, P])
        stats = sb("stats", [P, B * NI, 6])
        mv = sb("mv", [P, B * NI, 2])
        var = sb("var", [P, B * NI])
        rstd = sb("rstd", [P, B * NI])
        minus_half = sb("minus_half", [P, NI])
        xnT = xresT
        if causal:
            xh, xl = sb("xh", [P, B, N], F32R), sb("xl", [P, B, N], F32R)
        else:
            xh, xl = keep["hh"], keep["hl"]
        QH, QL = sb("QH", [P, 2, N], F32R), sb("QL", [P, 2, N], F32R)
        KH = sb("KH", [P, 2, N], F32R)
        VH, VL = sb("VH", [P, 2, NI, P], F32R), sb("VL", [P, 2, NI, P], F32R)
        negmax = sb("negmax", [P, 8])
        rowsum = sb("rowsum", [P, 8])
        inv = sb("inv", [P, 8])
        weights = sb("weights", [P, NP, N])
        WH, WL = sb("WH", [P, 2, NI, N], F32R), sb("WL", [P, 2, NI, N], F32R)
        oT = sb("oT", [P, N])
        if causal:
            raw = sb("raw", [P, W_PART])
            qk_raw = sb("qk_raw", [P, 2, P])
            wqk_h, wqk_l = sb("wqk_h", [P, 2, P], F32R), sb("wqk_l", [P, 2, P], F32R)
            wv = sb("wv", [P, P])
            mask32 = sb("mask32", [P, 3, P])
            h32 = keep["h32"]
            tab = sb("tab", [P, 2, 2, NI, DH])
            scl = sb("scl", [P, DEPTH, 2, 2, DH])
        else:
            nw = io["w_all"].shape[1]
            raw = sb("raw", [P, nw - QK_COLS])
            w_h, w_l = keep["w_h"][:, 0:nw], keep["w_l"][:, 0:nw]
            int_w = sb("int_w", [P, 3 * FF], I32)
            wv = sb("wv", [P, P])
            OH, OL = sb("OH", [P, 2, N], F32R), sb("OL", [P, 2, N], F32R)
            KL = sb("KL", [P, 2, N], F32R)
            tanh_g = sb("tanh_g", [P, N])
            silu_g = sb("silu_g", [P, 2, N])
            hid = sb("hid", [P, N])
            HH, HL = sb("HH", [P, FC, N], F32R), sb("HL", [P, FC, N], F32R)
            out_tok = sb("out_tok", [P, 2, NI, P])

        sumsq_done = sem("sumsq_done")
        rot_added = sem("rot_added")
        norm_ready = sem("norm_ready")
        norm_applied = sem("norm_applied")
        x_loaded = [sem(f"x_loaded{b}") for b in range(B)]
        qk_loaded = sem("qk_loaded")
        masks_loaded = sem("masks_loaded")
        wv_loaded = sem("wv_loaded")
        tables_loaded = sem("tables_loaded")
        ident_loaded = sem("ident_loaded")
        w_loaded = sem("w_loaded")
        w_split = sem("w_split")
        tables_ready = sem("tables_ready")
        dve_link = sem("dve_link")
        qkw_split = sem("qkw_split")
        consts_ready = sem("consts_ready")
        zeros_ready = sem("zeros_ready")
        stats_done = sem("stats_done")
        var_ready = sem("var_ready")
        rstd_ready = sem("rstd_ready")
        minus_half_ready = sem("minus_half_ready")
        h_shifted = sem("h_shifted")
        h_high = sem("h_high")
        h_low = sem("h_low")
        xn_ready = sem("xn_ready")
        xT_split = sem("xT_split")
        bank_filled = sem("bank_filled")
        act_used = sem("act_used")
        dve_used = sem("dve_used")
        scores_ready = sem("scores_ready")
        max_ready = sem("max_ready")
        exp_ready = sem("exp_ready")
        inv_ready = sem("inv_ready")
        weights_ready = sem("weights_ready")
        wT_ready = sem("wT_ready")
        high_ready = sem("high_ready")
        low_ready = sem("low_ready")
        o_ready = sem("o_ready")
        o_high = sem("o_high")
        o_low = sem("o_low")
        out_proj_done = sem("out_proj_done")
        y_taken = sem("y_taken")
        down_done = sem("down_done")
        stored = [sem(f"stored{k}") for k in range(2)]

        if causal:
            w_parts = [(keep["w_l"][:, c:c + W_PART], keep["w_h"][:, c:c + W_PART], raw[:])
                       for c in range(0, W_PARTS * W_PART, W_PART)]
        else:
            g0 = (2 * NQ + 1) * P
            w_parts = [(w_l[:, QK_COLS:], w_h[:, QK_COLS:], raw[:])]
            wq_c = lambda w, h: w[:, h * P:(h + 1) * P]
            wk_c = lambda w: w[:, NQ * P:(NQ + 1) * P]
            wo_c = lambda w, h: w[:, (NQ + 1 + h) * P:(NQ + 2 + h) * P]
            wg_c = lambda w, c: w[:, g0 + c * P:g0 + (c + 1) * P]
            wu_c = lambda w, c: w[:, g0 + FF + c * P:g0 + FF + (c + 1) * P]
            wd_c = lambda w, c: w[:, g0 + 2 * FF + c * P:g0 + 2 * FF + (c + 1) * P]

        with nc.Block() as block:

            @block.sync
            def _(sp):
                if causal:
                    def load_x(b):
                        sp.dma_start(x_tok[:, b * NI:(b + 1) * NI, :],
                                     io["x"][b].rearrange("(i p) d -> p i d", p=P)).then_inc(x_loaded[b], 16)
                    load_x(0)
                    sp.dma_start(ident[:], io["ident"]).then_inc(ident_loaded, 16)
                    for m in range(2):
                        for r in range(2):
                            sp.dma_start(qk_raw[:, m, r * DQ:(r + 1) * DQ], (io["Wq"], io["Wk"])[m])\
                              .then_inc(qk_loaded, 16)
                    load_x(1)
                    sp.dma_start(mask32[:], io["masks"]).then_inc(masks_loaded, 16)
                    sp.dma_start(wv[:], io["Wv"]).then_inc(wv_loaded, 16)
                    load_x(2)
                    load_x(3)
                    sp.dma_start(tab[:], io["rotary"]).then_inc(tables_loaded, 16)
                    sp.dma_start(scl[:], io["qk_scales"]).then_inc(tables_loaded, 16)
                    sp.dma_start(keep["cols"][:], io["cols"]).then_inc(tables_loaded, 16)
                    for n in range(len(w_parts)):
                        if n:
                            sp.wait_ge(w_split, 2 * n)
                        sp.dma_start(raw[:], io["w_all"][:, n * W_PART:(n + 1) * W_PART]).then_inc(w_loaded, 16)
                else:
                    sp.dma_start(wv[:], io["Wv"]).then_inc(wv_loaded, 16)
                    sp.dma_start(raw[:, 0:g0 - QK_COLS], io["w_all"][:, QK_COLS:g0]).then_inc(w_loaded, 16)
                    sp.dma_start(int_w[:], io["w_int"]).then_inc(w_loaded, 16)
                    for b in range(B):
                        sp.wait_ge(dve_used, ring.dve[("YT", b)])
                        sp.dma_start(io["out"][b].rearrange("(i p) d -> p i d", p=P),
                                     out_tok[:, b % 2]).then_inc(stored[b % 2], 16)
                    for k in range(2):
                        sp.wait_ge(stored[k], 16 * B // 2)

            @block.gpsimd
            def _(pool):
                nc.gpsimd.memset(minus_half[:], -0.5).then_inc(minus_half_ready, 1)
                if causal:
                    nc.gpsimd.memset(WH[:, :, NI - 1, 2 * P:3 * P].bitcast(F32), 0.0).then_inc(zeros_ready, 1)
                    nc.gpsimd.memset(WL[:, :, NI - 1, 2 * P:3 * P].bitcast(F32), 0.0).then_inc(zeros_ready, 1)
                    nc.gpsimd.memset(h32[:], 0.0).then_inc(zeros_ready, 1)
                for item in items:
                    if item[0] == "TABLES":
                        pool.wait_ge(tables_loaded, 48)
                        for l in range(DEPTH):
                            for m in range(2):
                                for r in range(2):
                                    nc.gpsimd.tensor_tensor(keep["tables"][:, l, r, m], tab[:, r, m],
                                                            scl[:, l, m, r:r + 1, :].to_broadcast([P, NI, DH]),
                                                            ALU.mult).then_inc(tables_ready, 1)
                    if item[0] == "STATS":
                        b = item[1]
                        pool.wait_ge(minus_half_ready, 1)
                        pool.wait_ge(var_ready, b - B0 + 1)
                        bt = slice(b * NI, (b + 1) * NI)
                        nc.gpsimd.tensor_tensor(rstd[:, bt], var[:, bt], minus_half[:], ALU.pow).then_inc(rstd_ready, 1)
                    if item[0] == "HX":
                        b = item[1]
                        pool.wait_ge(h_high, b + 1)
                        nc.gpsimd.tensor_tensor(keep["hl"][:, b, :], h32[:, 0:N], f32(keep["hh"][:, b, :]),
                                                ALU.subtract).then_inc(h_low, 1)
                    if item[0] == "W":
                        n = item[1]
                        pool.wait_ge(w_split, 2 * n + 1)
                        low, high, whole = w_parts[n]
                        nc.gpsimd.tensor_tensor(low, whole, f32(high), ALU.subtract).then_inc(w_split, 1)
                    if item[0] == "QK":
                        pool.wait_ge(dve_used, ring.dve[item])
                        add_rotation(nc, keep, item[1]).then_inc(rot_added, 1)
                    if item[0] == "NA":
                        pool.wait_ge(norm_ready, 1)
                        pool.wait_ge(rot_added, NI)
                        apply_norm(nc, keep, 0, item[1]).then_inc(norm_applied, 1)
                    if item[0] == "I":
                        T = item[1]
                        i = tiles[T][1]
                        n = P * (i + 1) if causal else N
                        pool.wait_ge(inv_ready, T + 1)
                        w = weights[:, T % NP, 0:n]
                        nc.gpsimd.tensor_tensor(w, w, inv[:, T % 8:T % 8 + 1].to_broadcast([P, n]), ALU.mult)\
                            .then_inc(weights_ready, 1)

            @block.scalar
            def _(act):
                for item in items:
                    kind = item[0]
                    if kind in by_act:
                        act.wait_ge(bank_filled, ring.filled(item))
                        ps = bank[:, ring.bank(item), :]
                    if kind == "LN":
                        b = item[1]
                        nc.scalar.copy(xnT[:, b, :], ps)
                        nc.scalar.copy(xh[:, b, :], ps).then_inc(act_used, 1)
                    elif kind == "QK":
                        i = item[1]
                        if i >= 2:
                            act.wait_ge(sumsq_done, i - 1)
                        nc.scalar.activation(keep["sq"][:, i % 2, :], ps, ACT.Square).then_inc(act_used, 1)
                    elif kind == "HX":
                        b = item[1]
                        if b == 0:
                            act.wait_ge(zeros_ready, 3)
                        else:
                            act.wait_ge(h_low, b)
                        act.wait_ge(act_used, ring.act[("LN", b)])
                        nc.scalar.copy(h32[0:64, 0:N], xnT[0:64, b, :])
                        nc.scalar.copy(h32[64:128, 1:N + 1], xnT[64:128, b, :]).then_inc(h_shifted, 1)
                    elif kind == "K":
                        b = item[1]
                        if b >= 2:
                            act.wait_ge(scores_ready, (b - 1) * heads * NI)
                        nc.scalar.copy(KH[:, b % 2, :], ps).then_inc(act_used, 1)
                    elif kind == "V":
                        b = item[1]
                        if b >= 2:
                            act.wait_ge(o_ready, (b - 1) * heads)
                        nc.scalar.copy(VH[:, b % 2], ps).then_inc(act_used, 1)
                    elif kind == "Q":
                        j = item[1]
                        if j >= 2:
                            act.wait_ge(scores_ready, (j - 1) * NI)
                        nc.scalar.activation(QH[:, j % 2, :], ps, ACT.Copy, scale=0.125 if causal else 1.0)\
                            .then_inc(act_used, 1)
                    elif kind == "O":
                        j = item[1]
                        act.wait_ge(o_ready, j + 1)
                        if causal:
                            if j >= 1:
                                act.wait_ge(bank_filled, ring.filled(("OT", j - 1)))
                            nc.scalar.copy(oT[:], o_ps[:]).then_inc(o_high, 1)
                        else:
                            if j >= 2:
                                act.wait_ge(out_proj_done, j - 1)
                            nc.scalar.copy(OH[:, j % 2, :], o_ps[:]).then_inc(o_high, 1)
                    elif kind == "GATE":
                        _, b, c = item
                        if b or c:
                            last = (b, c - 1) if c else (b - 1, FC - 1)
                            act.wait_ge(dve_used, ring.dve[("GATE", *last)])
                        nc.scalar.activation(tanh_g[:], ps, ACT.Tanh, scale=0.5).then_inc(act_used, 1)
                    elif kind == "YT" and not causal:
                        b = item[1]
                        act.wait_ge(out_proj_done, NQ * (b + 1))
                        if b >= 1:
                            act.wait_ge(bank_filled, ring.filled(("YT", b - 1)))
                        nc.scalar.copy(oT[:], y_ps[:]).then_inc(y_taken, 1)
                    elif kind == "TR":
                        T = item[1]
                        j, i = tiles[T]
                        n = i + 1 if causal else NI
                        act.wait_ge(wT_ready, T + 1)
                        if j >= 2:
                            act.wait_ge(o_ready, j - 1)
                        nc.scalar.copy(WH[:, j % 2, 0:n, i * P:(i + 1) * P],
                                       wT_ps[:, T % 2, 0:n * P].rearrange("p (k q) -> p k q", q=P))\
                            .then_inc(high_ready, 1)
                    elif kind == "E":
                        T = item[1]
                        i = tiles[T][1]
                        n = P * (i + 1) if causal else N
                        act.wait_ge(max_ready, T + 1)
                        if T >= NP:
                            act.wait_ge(wT_ready, T - NP + 1)
                        nc.scalar.activation(weights[:, T % NP, 0:n], scores[:, T % 2, 0:n], ACT.Exp,
                                             bias=negmax[:, T % 8:T % 8 + 1],
                                             accum_out=rowsum[:, T % 8:T % 8 + 1]).then_inc(exp_ready, 1)

            @block.vector
            def _(dve):
                link = chained(dve, dve_link, [0])

                for item in items:
                    kind = item[0]
                    if kind == "STATS":
                        b = item[1]
                        if causal:
                            dve.wait_ge(x_loaded[b], 16)
                        for t in range(b * NI, (b + 1) * NI):
                            nc.vector.bn_stats(stats[:, t, :], x_tok[:, t, :]).then_inc(stats_done, 1)
                        for t in range(b * NI, (b + 1) * NI):
                            dve.wait_ge(stats_done, (2 * (b - B0) + 1) * NI)
                            nc.vector.bn_aggr(mv[:, t, :], stats[:, t, :]).then_inc(stats_done, 1)
                        dve.wait_ge(stats_done, 2 * (b - B0 + 1) * NI)
                        bt = slice(b * NI, (b + 1) * NI)
                        nc.vector.tensor_scalar(var[:, bt], mv[:, bt, 1], LN_EPS, None, ALU.add).then_inc(var_ready, 1)
                    elif kind == "QK":
                        i = item[1]
                        dve.wait_ge(act_used, ring.act[item])
                        dve.wait_ge(tables_ready, 4 * DEPTH)
                        if i >= 2:
                            dve.wait_ge(rot_added, i - 1)
                        rotate_on_dve(nc, bank[:, ring.bank(item), :], keep, 0, i).then_inc(dve_used, 1)
                        sum_squares(nc, keep, 0, i).then_inc(sumsq_done, 1)
                    elif kind == "NORM":
                        part = item[1]
                        if part == 0:
                            dve.wait_ge(sumsq_done, NI)
                        last = norm_part(nc, link, keep, 0, part)
                        if part < 2:
                            link(last)
                        else:
                            last.then_inc(norm_ready, 1)
                    elif kind == "QKW":
                        dve.wait_ge(qk_loaded, 64)
                        nc.vector.tensor_copy(wqk_h[:], qk_raw[:]).then_inc(qkw_split, 1)
                        dve.wait_ge(qkw_split, 1)
                        nc.vector.tensor_tensor(wqk_l[:], qk_raw[:], f32(wqk_h[:]), ALU.subtract)\
                            .then_inc(qkw_split, 1)
                    elif kind == "CONSTS":
                        dve.wait_ge(ident_loaded, 16)
                        nc.vector.tensor_copy(keep["ident_bf"][:], ident[:]).then_inc(consts_ready, 1)
                        dve.wait_ge(masks_loaded, 16)
                        nc.vector.tensor_copy(keep["masks"][:], mask32[:]).then_inc(consts_ready, 1)
                    elif kind == "LN":
                        b = item[1]
                        if b > B0:
                            dve.wait_ge(bank_filled, ring.filled(("LN", b - 1)))
                        dve.wait_ge(rstd_ready, b - B0 + 1)
                        for i in range(NI):
                            t = b * NI + i
                            nc.vector.tensor_scalar(xn_tok[:, i, :], x_tok[:, t, :], mv[:, t, 0:1],
                                                    rstd[:, t:t + 1], ALU.subtract, ALU.mult).then_inc(xn_ready, 1)
                    elif kind == "XL":
                        b = item[1]
                        dve.wait_ge(act_used, ring.act[("LN", b)])
                        nc.vector.tensor_tensor(xl[:, b, :], xnT[:, b, :], f32(xh[:, b, :]), ALU.subtract)\
                            .then_inc(xT_split, 1)
                    elif kind == "HX":
                        b = item[1]
                        dve.wait_ge(h_shifted, b + 1)
                        nc.vector.tensor_copy(keep["hh"][:, b, :], h32[:, 0:N]).then_inc(h_high, 1)
                    elif kind == "W":
                        n = item[1]
                        low, high, whole = w_parts[n]
                        if causal:
                            dve.wait_ge(w_loaded, 16 * (n + 1))
                        else:
                            dve.wait_ge(w_loaded, 32)
                            ints = raw[:, g0 - QK_COLS:]
                            link(nc.vector.tensor_copy(ints, int_w[:]))
                            link(nc.vector.tensor_scalar(ints, ints, 1.0 / 127.0, None, ALU.mult))
                        if n:
                            dve.wait_ge(w_split, 2 * n)
                        nc.vector.tensor_copy(high, whole).then_inc(w_split, 1)
                    elif kind == "X1":
                        b = item[1]
                        dve.wait_ge(bank_filled, ring.filled(item))
                        xt = x_tok[:, b * NI:(b + 1) * NI, :]
                        nc.vector.tensor_tensor(xt, bank[:, ring.bank(item), :].rearrange("p (i d) -> p i d", d=P),
                                                xt, ALU.add).then_inc(dve_used, 1)
                        dve.wait_ge(dve_used, ring.dve[item])
                    elif kind == "K":
                        b = item[1]
                        dve.wait_ge(act_used, ring.act[item])
                        ps = bank[:, ring.bank(item), :]
                        if causal:
                            nc.vector.tensor_tensor(KH[64:128, b % 2, :], ps[64:128, :],
                                                    f32(KH[64:128, b % 2, :]), ALU.subtract)\
                                .then_inc(dve_used, 1)
                        else:
                            nc.vector.tensor_tensor(KL[:, b % 2, :], ps, f32(KH[:, b % 2, :]), ALU.subtract)\
                                .then_inc(dve_used, 1)
                    elif kind == "V":
                        b = item[1]
                        dve.wait_ge(act_used, ring.act[item])
                        nc.vector.tensor_tensor(VL[:, b % 2], bank[:, ring.bank(item), :]
                                                .rearrange("p (i d) -> p i d", d=P), f32(VH[:, b % 2]),
                                                ALU.subtract).then_inc(dve_used, 1)
                    elif kind == "Q":
                        j = item[1]
                        dve.wait_ge(act_used, ring.act[item])
                        nc.vector.scalar_tensor_tensor(QL[:, j % 2, :], bank[:, ring.bank(item), :],
                                                       0.125 if causal else 1.0, f32(QH[:, j % 2, :]),
                                                       ALU.mult, ALU.subtract).then_inc(dve_used, 1)
                    elif kind == "O" and not causal:
                        j = item[1]
                        dve.wait_ge(o_high, j + 1)
                        nc.vector.tensor_tensor(OL[:, j % 2, :], o_ps[:], f32(OH[:, j % 2, :]), ALU.subtract)\
                            .then_inc(o_low, 1)
                    elif kind == "OT":
                        j = item[1]
                        dve.wait_ge(bank_filled, ring.filled(item))
                        xt = x_tok[:, j * NI:(j + 1) * NI, :]
                        nc.vector.tensor_tensor(xt, bank[:, ring.bank(item), :].rearrange("p (i d) -> p i d", d=P),
                                                xt, ALU.add).then_inc(dve_used, 1)
                    elif kind == "GATE":
                        _, b, c = item
                        dve.wait_ge(act_used, ring.act[item])
                        if b or c >= 2:
                            k = b * FC + c - 2
                            if k >= 0:
                                dve.wait_ge(dve_used, ring.dve[("UP", k // FC, k % FC)])
                        nc.vector.scalar_tensor_tensor(silu_g[:, (b * FC + c) % 2, :], tanh_g[:], 1.0,
                                                       bank[:, ring.bank(item), :], ALU.add, ALU.mult)\
                            .then_inc(dve_used, 1)
                    elif kind == "UP":
                        _, b, c = item
                        dve.wait_ge(bank_filled, ring.filled(item))
                        dve.wait_ge(dve_used, ring.dve[("GATE", b, c)])
                        if b >= 1:
                            dve.wait_ge(down_done, b)
                        link(nc.vector.scalar_tensor_tensor(hid[:], silu_g[:, (b * FC + c) % 2, :], 0.5,
                                                            bank[:, ring.bank(item), :], ALU.mult, ALU.mult))
                        link(nc.vector.tensor_copy(HH[:, c, :], hid[:]))
                        nc.vector.tensor_tensor(HL[:, c, :], hid[:], f32(HH[:, c, :]), ALU.subtract)\
                            .then_inc(dve_used, 1)
                        dve.wait_ge(dve_used, ring.dve[item])
                    elif kind == "YT":
                        b = item[1]
                        dve.wait_ge(bank_filled, ring.filled(item))
                        if b >= 2:
                            dve.wait_ge(stored[b % 2], 16 * (b // 2))
                        nc.vector.tensor_tensor(out_tok[:, b % 2], bank[:, ring.bank(item), :]
                                                .rearrange("p (i d) -> p i d", d=P),
                                                x_tok[:, b * NI:(b + 1) * NI, :], ALU.add)\
                            .then_inc(dve_used, 1)
                    elif kind == "S":
                        T = item[1]
                        i = tiles[T][1]
                        n = P * (i + 1) if causal else N
                        dve.wait_ge(scores_ready, T + 1)
                        if T >= 8:
                            dve.wait_ge(exp_ready, T - 7)
                        nc.vector.tensor_reduce(negmax[:, T % 8:T % 8 + 1], scores[:, T % 2, 0:n], AX_X,
                                                ALU.max, negate=True).then_inc(max_ready, 1)
                    elif kind == "I":
                        T = item[1]
                        dve.wait_ge(exp_ready, T + 1)
                        if T >= 8:
                            dve.wait_ge(weights_ready, T - 7)
                        nc.vector.reciprocal(inv[:, T % 8:T % 8 + 1], rowsum[:, T % 8:T % 8 + 1])\
                            .then_inc(inv_ready, 1)
                    elif kind == "TR":
                        T = item[1]
                        j, i = tiles[T]
                        n = i + 1 if causal else NI
                        dve.wait_ge(high_ready, T + 1)
                        nc.vector.tensor_tensor(WL[:, j % 2, 0:n, i * P:(i + 1) * P],
                                                wT_ps[:, T % 2, 0:n * P].rearrange("p (k q) -> p k q", q=P),
                                                f32(WH[:, j % 2, 0:n, i * P:(i + 1) * P]), ALU.subtract)\
                            .then_inc(low_ready, 1)

            @block.tensor
            def _(pe):
                def claim(item):
                    old = ring.before(item)
                    if old is not None:
                        if old in ring.dve:
                            pe.wait_ge(dve_used, ring.dve[old])
                        if old in ring.act:
                            pe.wait_ge(act_used, ring.act[old])
                    return bank[:, ring.bank(item), :]

                if causal:
                    pe.wait_ge(ident_loaded, 16)
                for item in items:
                    kind = item[0]
                    if kind == "LN":
                        b = item[1]
                        ps = claim(item)
                        pe.wait_ge(xn_ready, NI * (b - B0 + 1))
                        for i in range(NI):
                            last = nc.tensor.transpose(ps[:, i * P:(i + 1) * P], xn_tok[:, i, :], ident[:])
                        last.then_inc(bank_filled, 1)
                    elif kind == "QK":
                        ps = claim(item)
                        pe.wait_ge(h_low, 1)
                        pe.wait_ge(w_split, 2)
                        project_qk(nc, ps, keep, 0, 0, item[1], 0).then_inc(bank_filled, 1)
                    elif kind == "X1":
                        b = item[1]
                        ps = claim(item)
                        for i in range(NI):
                            last = nc.tensor.transpose(ps[:, i * P:(i + 1) * P],
                                                       xresT[:, b, i * P:(i + 1) * P], ident[:])
                        last.then_inc(bank_filled, 1)
                    elif kind == "K":
                        b = item[1]
                        ps = claim(item)
                        if b >= B0:
                            pe.wait_ge(xT_split, b - B0 + 1)
                        if causal:
                            pe.wait_ge(qkw_split, 2)
                            w = (wqk_h[:, 1, :], wqk_l[:, 1, :])
                        else:
                            w = (wk_c(w_h), wk_c(w_l))
                        split_matmul(nc, ps, w, (xh[:, b, :], xl[:, b, :])).then_inc(bank_filled, 1)
                    elif kind == "V":
                        b = item[1]
                        ps = claim(item)
                        pe.wait_ge(wv_loaded, 16)
                        for i in range(NI):
                            last = nc.tensor.matmul(ps[:, i * P:(i + 1) * P], xnT[:, b, i * P:(i + 1) * P],
                                                    wv[:], start=True, stop=True)
                        last.then_inc(bank_filled, 1)
                    elif kind == "Q":
                        b, h = jobs[item[1]]
                        ps = claim(item)
                        w = (wqk_h[:, 0, :], wqk_l[:, 0, :]) if causal else (wq_c(w_h, h), wq_c(w_l, h))
                        split_matmul(nc, ps, w, (xh[:, b, :], xl[:, b, :])).then_inc(bank_filled, 1)
                    elif kind == "AV":
                        _, j, k = item
                        b = jobs[j][0]
                        if k == 0:
                            pe.wait_ge(low_ready, NI * (j + 1))
                            pe.wait_ge(dve_used, ring.dve[("V", b)])
                            if causal:
                                pe.wait_ge(zeros_ready, 2)
                            if j >= 1:
                                pe.wait_ge(o_high, j)
                                if not causal:
                                    pe.wait_ge(o_low, j)
                        q0 = min(P * k, N - 2 * P) if causal else 0
                        last = split_matmul(nc, o_ps[:, q0:N], (VH[:, b % 2, k, :], VL[:, b % 2, k, :]),
                                            (WH[:, j % 2, k, q0:N], WL[:, j % 2, k, q0:N]),
                                            start=k == 0, stop=k == NI - 1)
                        if k == NI - 1:
                            last.then_inc(o_ready, 1)
                    elif kind == "OT":
                        ps = claim(item)
                        pe.wait_ge(o_high, item[1] + 1)
                        for i in range(NI):
                            last = nc.tensor.transpose(ps[:, i * P:(i + 1) * P], oT[:, i * P:(i + 1) * P], ident[:])
                        last.then_inc(bank_filled, 1)
                    elif kind == "OP":
                        j = item[1]
                        b, h = jobs[j]
                        pe.wait_ge(o_low, j + 1)
                        if h == 0 and b >= 1:
                            pe.wait_ge(y_taken, b)
                        if j == 0:
                            pe.wait_ge(w_split, 2)
                        ins = split_matmul(nc, y_ps[:], (wo_c(w_h, h), wo_c(w_l, h)),
                                           (OH[:, j % 2, :], OL[:, j % 2, :]), start=h == 0, stop=h == NQ - 1)
                        ins.then_inc(out_proj_done, 1)
                    elif kind in ("GATE", "UP"):
                        _, b, c = item
                        ps = claim(item)
                        wc = wg_c if kind == "GATE" else wu_c
                        if b == 0:
                            pe.wait_ge(w_split, 2)
                        split_matmul(nc, ps, (wc(w_h, c), wc(w_l, c)), (xh[:, b, :], xl[:, b, :]))\
                            .then_inc(bank_filled, 1)
                    elif kind == "DOWN":
                        b = item[1]
                        pe.wait_ge(dve_used, ring.dve[("UP", b, FC - 1)])
                        for c in range(FC):
                            last = split_matmul(nc, y_ps[:], (wd_c(w_h, c), wd_c(w_l, c)),
                                                (HH[:, c, :], HL[:, c, :]), start=False, stop=False)
                        last.then_inc(down_done, 1)
                    elif kind == "YT":
                        b = item[1]
                        ps = claim(item)
                        pe.wait_ge(y_taken, b + 1)
                        for i in range(NI):
                            last = nc.tensor.transpose(ps[:, i * P:(i + 1) * P], oT[:, i * P:(i + 1) * P], ident[:])
                        last.then_inc(bank_filled, 1)
                    elif kind == "TR":
                        T = item[1]
                        j, i = tiles[T]
                        n = i + 1 if causal else NI
                        pe.wait_ge(weights_ready, T + 1)
                        if T >= 2:
                            pe.wait_ge(low_ready, T - 1)
                        for k in range(n):
                            last = nc.tensor.transpose(wT_ps[:, T % 2, k * P:(k + 1) * P],
                                                       weights[:, T % NP, k * P:(k + 1) * P], ident[:])
                        last.then_inc(wT_ready, 1)
                    elif kind == "S":
                        T = item[1]
                        j, i = tiles[T]
                        b = jobs[j][0]
                        pe.wait_ge(dve_used, ring.dve[("Q", j)])
                        if T >= 2:
                            pe.wait_ge(exp_ready, T - 1)
                        qh, ql = QH[:, j % 2, i * P:(i + 1) * P], QL[:, j % 2, i * P:(i + 1) * P]
                        if causal:
                            pe.wait_ge(consts_ready, 2)
                            n = max(P * (i + 1), 2 * P)
                            ps = scores[:, T % 2, 0:n]
                            nc.tensor.matmul(ps, qh, KH[:, b % 2, 0:n], start=True, stop=False)
                            nc.tensor.matmul(ps, ql, KH[:, b % 2, 0:n], start=False, stop=False)
                            nc.tensor.matmul(scores[:, T % 2, i * P:(i + 1) * P], keep["ident_bf"][:],
                                             keep["masks"][:, 0, :], start=False, stop=True)\
                                .then_inc(scores_ready, 1)
                        else:
                            split_matmul(nc, scores[:, T % 2, :], (qh, ql),
                                         (KH[:, b % 2, :], KL[:, b % 2, :])).then_inc(scores_ready, 1)


L0_AT = {
    "STATS": -7.708, "LN": -4.2, "QKW": -3.978, "XL": -3.155, "CONSTS": -2.17, "HX": -1.88,
    ("W", 0): -1.12, "K": -1.079, "Q": -0.517, "TABLES": 0.229, "S": 0.5, "E": 1.797, "I": 1.912,
    "TR": 4.372, "V": 5.098, ("W", 1): 5.231, ("W", 2): 7.883, ("QK", 0): 8.54, ("QK", 1): 8.848,
    ("W", 3): 9.112, ("AV", 0): 9.292, ("QK", 2): 9.455, ("AV", 1): 10.066, ("QK", 3): 10.408,
    ("AV", 2): 11.206, ("AV", 3): 12.111, ("W", 4): 12.256, "O": 12.308, ("NORM", 0): 12.495,
    ("NORM", 1): 13.385, ("NORM", 2): 14.646, ("NA", 0): 15.616, "OT": 16.622, ("NA", 1): 17.627,
    ("W", 5): 19.195, ("NA", 2): 22.203, ("NA", 3): 24.927,
}
L1_AT = {
    "X1": -18.992, "STATS": -11.189, "LN": -7.019, "XL": -6.422, "K": -1.937, "Q": -0.927,
    ("W", 0): -0.33, "V": -0.02, "S": 0.5, "E": 1.561, "I": 2.024, "TR": 4.09, ("GATE", 0): 6.032,
    ("UP", 0): 8.125, ("AV", 0): 8.646, ("AV", 1): 8.911, ("AV", 2): 9.671, ("AV", 3): 10.342,
    "O": 10.973, ("GATE", 1): 12.011, "OP": 12.332, ("UP", 1): 12.506, ("GATE", 2): 15.292,
    ("UP", 2): 36.163, "DOWN": 39.891, "YT": 42.504,
}
WIN_AT = {
    ("QK", 0): -5.018, ("QK", 1): -4.886, ("QK", 2): -4.298, ("QK", 3): -3.78, ("NA", 0): -3.054,
    ("NA", 1): -3.051, ("NA", 2): -3.006, ("NA", 3): -2.761, ("NORM", 0): -2.573, ("NORM", 1): -2.391,
    ("NORM", 2): -2.293, ("QT", 0): -0.732, ("QT", 1): -0.681, ("QT", 2): -0.473, ("QT", 3): -0.453,
    "S": 0.5, "E": 0.532, "I": 1.278, ("VP", 0): 1.635, ("VP", 1): 2.252, "TR": 2.703, "WO": 3.2,
    "AV": 3.737, "LS": 4.149, "LT": 4.538, "LN": 5.681, "LB": 6.904, ("G", 0): 8.266, ("A", 0): 8.431,
    ("G", 1): 8.549, ("A", 1): 8.75, ("G", 2): 8.855, ("A", 2): 8.968, "W2": 10.527, "HS": 10.929,
    ("LW", 0): 43.384, ("LW", 1): 54.289, "X1": 60.751, "STATS1": 63.669, "LN1": 68.824, "XL1": 72.018,
}
WIN_SHIFT = {
    "ACT": {"QK": 0.067, "VP": 0.582, "QT": 0.179, "AV": 0.239, "WO": 0.718, "LB": 0.086, "G": 0.412,
            "W2": 0.392, "LT": -0.14, "E": 0.882},
    "DVE": {"QK": -0.019, "NORM": -0.134, "AV": -0.039, "WO": -0.067, "LS": 0.225, "LN": 0.37,
            "LB": 0.204, "A": -0.009, "W2": -0.46, "HS": 0.182, "S": -0.224, "TR": -0.058, "I": 0.097},
    "Pool": {"QK": -0.125, "NA": 0.887, "HS": -0.188, "LB": 0.08, "A": 0.58, "LS": 0.465, "I": 0.29},
}

W_LAYER = 3 * INNER + 4 * P + 2 * HID + 3 * P
QK_COLS = (NQ + 1) * P
W_PARTS = 6
W_PART = DEPTH * W_LAYER // W_PARTS
assert W_PART * W_PARTS == DEPTH * W_LAYER and W_PART >= 2 * INNER
COLS = 3 + 6


def windowed_block(nc, keep, l1_w):
    tag = "win"
    xresT, hh, hl, h32, ident = keep["xresT"], keep["hh"], keep["hl"], keep["h32"], keep["ident"]
    cols, x_tok = keep["cols"], keep["x_tok"]
    S = DEPTH * B
    U = 2 * S
    TU = NW // 2
    NT = U * TU
    unit_step = lambda u: u // 2
    NP, RB = 3, 4

    line = []
    for u in range(U):
        g = TU * u
        if u:
            line += [(g + WIN_AT["QK", i], ("QK", u, i)) for i in range(NI)]
            line += [(g + WIN_AT["NORM", i], ("NORM", u, i)) for i in range(3)]
            line += [(g + WIN_AT["NA", i], ("NA", u, i)) for i in range(NI)]
        line += [(g + WIN_AT["QT", i], ("QT", u, i // 2, i % 2)) for i in range(NI)]
        line += [(g + WIN_AT["VP", i], ("VP", u, i)) for i in range(2)]
    for g in range(NT):
        line += [(g + WIN_AT[kind], (kind, g)) for kind in ("S", "E", "I", "TR", "AV")]
    for s in range(S):
        g = 2 * TU * (s + 1)
        line += [(g + WIN_AT[kind], (kind, s)) for kind in ("WO", "LT", "LS", "LN", "LB", "W2")]
        line += [(g + WIN_AT[kind, c], (kind, s, c)) for kind in ("G", "A") for c in range(3)]
        if s < B:
            line.append((g + WIN_AT["HS"], ("HS", s)))
    line += [(WIN_AT["LW", n], ("LW", n)) for n in range(2)]
    line += [(WIN_AT[kind], (kind,)) for kind in ("X1", "STATS1", "LN1", "XL1")]

    def order(engine):
        shift = WIN_SHIFT.get(engine, {})
        return [item for _, item in sorted((t + shift.get(item[0], 0), item) for t, item in line)]

    acts = {"QK", "QT", "VP", "AV", "LT", "LB", "G", "LN1"}
    dves = {"QK", "AV", "WO", "A", "W2", "X1"}
    ring = Ring(RB, [x for x in order("PE") if x[0] in acts | dves],
                [x for x in order("ACT") if x[0] in acts], [x for x in order("DVE") if x[0] in dves])

    LWH = [layer_w(keep["w_h"], l) for l in range(DEPTH)]
    LWL = [layer_w(keep["w_l"], l) for l in range(DEPTH)]

    with ExitStack() as ctx:
        def sb(name, shape, dt=F32):
            return ctx.enter_context(nc.sbuf_tensor(f"{tag}_{name}", shape, dt))

        def psum(name, shape):
            return ctx.enter_context(nc.psum_tensor(f"{tag}_{name}", shape, F32))

        def sem(name):
            return ctx.enter_context(nc.semaphore(f"{tag}_{name}"))

        scores = psum("scores", [P, 2, 4 * P])
        wT_ps = psum("wT_ps", [P, 2, 4 * P])
        bank = psum("bank", [P, RB, 512])
        QBD = sb("QBD", [P, 2, 2, NW, 2, WIN])
        KT = sb("KT", [P, 2, 2, N])
        V = sb("V", [P, 2, NW - 1, 2 * P])
        negmax = sb("negmax", [P, 8, 4])
        rowsum = sb("rowsum", [P, 8, 4])
        inv = sb("inv", [P, 8, 4])
        weights = sb("weights", [P, NP, 4 * P])
        wT = sb("wT", [P, 2, 4 * P])
        OTH, OTL = sb("OTH", [P, 4, N], F32R), sb("OTL", [P, 4, N], F32R)
        stats = sb("stats", [P, NI, 6])
        mv = sb("mv", [P, NI, 2])
        var = sb("var", [P, NI])
        rstd = sb("rstd", [P, NI])
        stats1, mv1 = sb("stats1", [P, NI, 6]), sb("mv1", [P, NI, 2])
        var1, rstd1 = sb("var1", [P, NI]), sb("rstd1", [P, NI])
        xn_tok = weights[:, NT % NP, :].rearrange("p (i d) -> p i d", d=P)
        LW = QK_COLS // 2
        stage = keep["tables"][:, 0].rearrange("p r m i d -> p (r m i d)")[:, 0:LW]
        minus_half = sb("minus_half", [P, NI])
        h_tok = sb("h_tok", [P, NI, P])
        n32 = sb("n32", [P, N])
        nH, nL = sb("nH", [P, N], F32R), sb("nL", [P, N], F32R)
        gelu_g = sb("gelu_g", [P, 3, N])
        hid = sb("hid", [P, 2, N])
        HH, HL = sb("HH", [P, 3, N], F32R), sb("HL", [P, 3, N], F32R)

        dve_link = sem("dve_link")
        zeros_ready = sem("zeros_ready")
        bank_filled = sem("bank_filled")
        act_used = sem("act_used")
        dve_used = sem("dve_used")
        sumsq_done = sem("sumsq_done")
        rot_added = sem("rot_added")
        norm_ready = sem("norm_ready")
        norm_applied = sem("norm_applied")
        scores_ready = sem("scores_ready")
        max_ready = sem("max_ready")
        exp_ready = sem("exp_ready")
        inv_ready = sem("inv_ready")
        weights_ready = sem("weights_ready")
        wT_ready = sem("wT_ready")
        wT_copied = sem("wT_copied")
        h32_ready = sem("h32_ready")
        h_tok_stats = sem("h_tok_stats")
        var_ready = sem("var_ready")
        rstd_ready = sem("rstd_ready")
        hn_ready = sem("hn_ready")
        nH_ready = sem("nH_ready")
        n_ready = sem("n_ready")
        HH_ready = sem("HH_ready")
        hid_ready = sem("hid_ready")
        hh_ready = sem("hh_ready")
        h_split = sem("h_split")

        lw_loaded = sem("lw_loaded")
        lw_split = sem("lw_split")
        x_stats = sem("x_stats")
        x_var_ready = sem("x_var_ready")
        x_rstd_ready = sem("x_rstd_ready")
        xn_ready = sem("xn_ready")
        xl_ready = sem("xl_ready")
        v_shifted = [sem(f"v_shifted{k}") for k in range(2)]

        with nc.Block() as block:

            @block.sync
            def _(sp):
                for u in range(U):
                    if u == U // 2 + 2:
                        sp.wait_ge(dve_used, ring.dve[("QK", U // 2 - 1, NI - 1)])
                        sp.dma_start(stage, l1_w[:, 0:LW]).then_inc(lw_loaded, 16)
                    elif u == U // 2 + 4:
                        sp.wait_ge(lw_split, 2)
                        sp.dma_start(stage, l1_w[:, LW:2 * LW]).then_inc(lw_loaded, 16)
                    sp.wait_ge(act_used, ring.act[("VP", u, 1)])
                    v = V[:, u % 2]
                    sp.dma_start(v[0:WIN, 1:NW - 2:2, :], v[WIN:P, 0:NW - 3:2, :]).then_inc(v_shifted[u % 2], 16)
                    sp.dma_start(v[WIN:P, 1:NW - 2:2, :], v[0:WIN, 2:NW - 1:2, :]).then_inc(v_shifted[u % 2], 16)

            @block.gpsimd
            def _(pool):
                nc.gpsimd.memset(QBD[:], 0.0).then_inc(zeros_ready, 1)
                nc.gpsimd.memset(minus_half[:], -0.5).then_inc(zeros_ready, 1)
                for item in order("Pool"):
                    kind = item[0]
                    if kind == "QK":
                        _, u, i = item
                        pool.wait_ge(dve_used, ring.dve[item])
                        pool.wait_ge(bank_filled, ring.filled(("QT", u - 1, 1, 1)))
                        add_rotation(nc, keep, i).then_inc(rot_added, 1)
                    elif kind == "NA":
                        _, u, i = item
                        pool.wait_ge(norm_ready, u)
                        pool.wait_ge(rot_added, NI * u)
                        apply_norm(nc, keep, u, i).then_inc(norm_applied, 1)
                    elif kind == "LW":
                        n = item[1]
                        pool.wait_ge(lw_split, 2 * n + 1)
                        cs = slice(n * LW, (n + 1) * LW)
                        nc.gpsimd.tensor_tensor(keep["w_l"][:, cs], stage, f32(keep["w_h"][:, cs]), ALU.subtract)\
                            .then_inc(lw_split, 1)
                    elif kind == "STATS1":
                        pool.wait_ge(x_var_ready, 1)
                        nc.gpsimd.tensor_tensor(rstd1[:], var1[:], minus_half[:], ALU.pow).then_inc(x_rstd_ready, 1)
                    elif kind == "HS":
                        s = item[1]
                        pool.wait_ge(hh_ready, s + 1)
                        nc.gpsimd.tensor_tensor(hl[:, s, :], h32[:, 0:N], f32(hh[:, s, :]), ALU.subtract)\
                            .then_inc(h_split, 1)
                    elif kind == "LB":
                        s = item[1]
                        pool.wait_ge(nH_ready, s + 1)
                        nc.gpsimd.tensor_tensor(nL[:], n32[:], f32(nH[:]), ALU.subtract).then_inc(n_ready, 1)
                    elif kind == "A":
                        _, s, c = item
                        m = CH[c][1]
                        pool.wait_ge(HH_ready, 3 * s + c + 1)
                        nc.gpsimd.tensor_tensor(HL[0:m, c, :], hid[0:m, (s + c) % 2, :], f32(HH[0:m, c, :]),
                                                ALU.subtract).then_inc(hid_ready, 1)
                    elif kind == "LS":
                        s = item[1]
                        pool.wait_ge(var_ready, s + 1)
                        if s >= 1:
                            pool.wait_ge(hn_ready, s)
                        pool.wait_ge(zeros_ready, 2)
                        nc.gpsimd.tensor_tensor(rstd[:], var[:], minus_half[:], ALU.pow).then_inc(rstd_ready, 1)
                    elif kind == "I":
                        T = item[1]
                        pool.wait_ge(inv_ready, T + 1)
                        w = weights[:, T % NP, :].rearrange("p (c k) -> p c k", k=P)
                        k = inv[:, T % 8, :].unsqueeze(2).to_broadcast([P, 4, P])
                        nc.gpsimd.tensor_tensor(w, w, k, ALU.mult).then_inc(weights_ready, 1)

            @block.scalar
            def _(act):
                def shifted(b):
                    nc.scalar.copy(h32[0:64, 0:N], xresT[0:64, b, :])
                    nc.scalar.copy(h32[64:128, 1:N + 1], xresT[64:128, b, :]).then_inc(h32_ready, 1)

                for item in order("ACT"):
                    kind = item[0]
                    if item in ring.act:
                        act.wait_ge(bank_filled, ring.filled(item))
                        ps = bank[:, ring.bank(item), :]
                    if kind == "QK":
                        _, u, i = item
                        n = NI * (u - 1) + i
                        if n >= 2:
                            act.wait_ge(sumsq_done, n - 1)
                        nc.scalar.activation(keep["sq"][:, i % 2, :], ps, ACT.Square).then_inc(act_used, 1)
                    elif kind == "VP":
                        _, u, v = item
                        if u >= 2:
                            act.wait_ge(bank_filled, ring.filled(("AV", TU * (u - 1) - 1)))
                        nc.scalar.copy(V[:, u % 2, 4 * v:4 * v + 3:2, :],
                                       ps.rearrange("p (j d) -> p j d", j=2)).then_inc(act_used, 1)
                    elif kind == "QT" and item[2] == 1:
                        _, u, _, p = item
                        if u >= 2:
                            act.wait_ge(scores_ready, TU * (u - 1))
                        nc.scalar.copy(KT[:, u % 2, p, :], ps).then_inc(act_used, 1)
                    elif kind == "QT":
                        _, u, _, p = item
                        if u >= 2:
                            act.wait_ge(scores_ready, TU * (u - 1))
                        act.wait_ge(zeros_ready, 1)
                        src = ps.rearrange("p (w q) -> p w q", w=NW)
                        nc.scalar.copy(QBD[0:64, u % 2, p, :, 0, :], src[0:64])
                        nc.scalar.copy(QBD[64:128, u % 2, p, :, 1, :], src[64:128]).then_inc(act_used, 1)
                    elif kind == "AV":
                        g = item[1]
                        u, t = g // TU, g % TU
                        s = unit_step(u)
                        if s >= 1:
                            act.wait_ge(bank_filled, ring.filled(("WO", s - 1)))
                        p0 = 2 * (u % 2)
                        nc.scalar.copy(OTH[:, p0:p0 + 2, t * P:(t + 1) * P],
                                       ps[:, 0:2 * P].rearrange("p (c t) -> p c t", c=2)).then_inc(act_used, 1)
                    elif kind == "WO":
                        s = item[1]
                        act.wait_ge(dve_used, ring.dve[item])
                        if s >= 1 and (s - 1) < B:
                            act.wait_ge(h_split, s)
                        if s >= 1:
                            act.wait_ge(bank_filled, ring.filled(("LT", s - 1)))
                        shifted(s % B)
                    elif kind == "LN1":
                        nc.scalar.copy(xresT[:, 0, :], ps)
                        nc.scalar.copy(hh[:, 0, :], ps).then_inc(act_used, 1)
                    elif kind == "LB":
                        s = item[1]
                        l = s // B
                        if s >= 1:
                            act.wait_ge(n_ready, s)
                        nc.scalar.activation(n32[:], ps, ACT.Identity, bias=cols[:, l, 1:2], scale=cols[:, l, 0:1])\
                            .then_inc(act_used, 1)
                    elif kind == "G":
                        _, s, c = item
                        m = CH[c][1]
                        if s >= 1:
                            act.wait_ge(dve_used, ring.dve[("A", s - 1, c)])
                        nc.scalar.activation(gelu_g[0:m, c, :], ps[0:m], ACT.Gelu, bias=cols[0:m, s // B, 6 + c:7 + c])\
                            .then_inc(act_used, 1)
                    elif kind == "W2" and item[1] < B:
                        s = item[1]
                        act.wait_ge(dve_used, ring.dve[item])
                        act.wait_ge(bank_filled, ring.filled(("LT", s)))
                        shifted(s % B)
                    elif kind == "LT":
                        s = item[1]
                        if s >= 1:
                            act.wait_ge(bank_filled, ring.filled(("LB", s - 1)))
                        nc.scalar.copy(h_tok[:], ps.rearrange("p (i d) -> p i d", d=P)).then_inc(act_used, 1)
                    elif kind == "E":
                        T = item[1]
                        act.wait_ge(max_ready, T + 1)
                        if T >= NP:
                            act.wait_ge(wT_ready, T - NP + 1)
                        for c in range(4):
                            last = nc.scalar.activation(weights[:, T % NP, c * P:(c + 1) * P],
                                                        scores[:, T % 2, c * P:(c + 1) * P], ACT.Exp,
                                                        bias=negmax[:, T % 8, c:c + 1],
                                                        accum_out=rowsum[:, T % 8, c:c + 1])
                        last.then_inc(exp_ready, 1)

            @block.vector
            def _(dve):
                link = chained(dve, dve_link, [0])
                h32_uses = 0
                for item in order("DVE"):
                    kind = item[0]
                    if item in ring.dve:
                        dve.wait_ge(bank_filled, ring.filled(item))
                        ps = bank[:, ring.bank(item), :]
                    if kind == "QK":
                        _, u, i = item
                        n = NI * (u - 1) + i
                        dve.wait_ge(act_used, ring.act[item])
                        if n >= 2:
                            dve.wait_ge(rot_added, n - 1)
                        rotate_on_dve(nc, ps, keep, unit_step(u) // B, i).then_inc(dve_used, 1)
                        if i == 0 and u >= 3:
                            dve.wait_ge(norm_ready, u - 2)
                        sum_squares(nc, keep, u, i).then_inc(sumsq_done, 1)
                    elif kind == "NORM":
                        _, u, part = item
                        if part == 0:
                            dve.wait_ge(sumsq_done, NI * u)
                            if u >= 3:
                                dve.wait_ge(norm_applied, NI * (u - 2))
                        last = norm_part(nc, link, keep, u, part)
                        if part < 2:
                            link(last)
                        else:
                            last.then_inc(norm_ready, 1)
                    elif kind == "AV":
                        g = item[1]
                        u, t = g // TU, g % TU
                        dve.wait_ge(act_used, ring.act[item])
                        p0 = 2 * (u % 2)
                        nc.vector.tensor_tensor(OTL[:, p0:p0 + 2, t * P:(t + 1) * P],
                                                ps[:, 0:2 * P].rearrange("p (c t) -> p c t", c=2),
                                                f32(OTH[:, p0:p0 + 2, t * P:(t + 1) * P]), ALU.subtract)\
                            .then_inc(dve_used, 1)
                    elif kind == "WO":
                        s = item[1]
                        b = s % B
                        nc.vector.tensor_tensor(xresT[:, b, :], ps, xresT[:, b, :], ALU.add).then_inc(dve_used, 1)
                    elif kind == "LS":
                        s = item[1]
                        dve.wait_ge(act_used, ring.act[("LT", s)])
                        if s >= 1:
                            dve.wait_ge(hn_ready, s)
                        for i in range(NI):
                            nc.vector.bn_stats(stats[:, i, :], h_tok[:, i, :]).then_inc(h_tok_stats, 1)
                        for i in range(NI):
                            dve.wait_ge(h_tok_stats, 2 * NI * s + NI)
                            nc.vector.bn_aggr(mv[:, i, :], stats[:, i, :]).then_inc(h_tok_stats, 1)
                        dve.wait_ge(h_tok_stats, 2 * NI * (s + 1))
                        nc.vector.tensor_scalar(var[:], mv[:, :, 1], LN_EPS, None, ALU.add).then_inc(var_ready, 1)
                    elif kind == "LN":
                        s = item[1]
                        dve.wait_ge(rstd_ready, s + 1)
                        for i in range(NI):
                            last = nc.vector.tensor_scalar(h_tok[:, i, :], h_tok[:, i, :], mv[:, i, 0:1],
                                                           rstd[:, i:i + 1], ALU.subtract, ALU.mult)
                        last.then_inc(hn_ready, 1)
                    elif kind == "LB":
                        s = item[1]
                        dve.wait_ge(act_used, ring.act[item])
                        if s >= 1:
                            dve.wait_ge(bank_filled, ring.filled(("A", s - 1, 2)))
                        nc.vector.tensor_copy(nH[:], n32[:]).then_inc(nH_ready, 1)
                    elif kind == "A":
                        _, s, c = item
                        m = CH[c][1]
                        dve.wait_ge(act_used, ring.act[("G", s, c)])
                        if 3 * s + c >= 2:
                            dve.wait_ge(hid_ready, 3 * s + c - 1)
                        nc.vector.scalar_tensor_tensor(hid[0:m, (s + c) % 2, :], ps[0:m],
                                                       cols[0:m, s // B, 3 + c:4 + c], gelu_g[0:m, c, :],
                                                       ALU.add, ALU.mult).then_inc(dve_used, 1)
                        dve.wait_ge(dve_used, ring.dve[item])
                        if s >= 1:
                            dve.wait_ge(bank_filled, ring.filled(("W2", s - 1)))
                        nc.vector.tensor_copy(HH[0:m, c, :], hid[0:m, (s + c) % 2, :]).then_inc(HH_ready, 1)
                    elif kind == "W2":
                        s = item[1]
                        l, b = s // B, s % B
                        dve.wait_ge(h32_ready, h32_uses + 1)
                        h32_uses += 1
                        nc.vector.scalar_tensor_tensor(xresT[:, b, :], ps, cols[:, l, 2:3], xresT[:, b, :], ALU.add,
                                                       ALU.add).then_inc(dve_used, 1)
                        if l == 0:
                            h32_uses += 1
                    elif kind == "LW":
                        n = item[1]
                        dve.wait_ge(lw_loaded, 16 * (n + 1))
                        dve.wait_ge(bank_filled, ring.filled(("W2", B - 1)))
                        nc.vector.tensor_copy(keep["w_h"][:, n * LW:(n + 1) * LW], stage).then_inc(lw_split, 1)
                    elif kind == "X1":
                        xt = x_tok[:, 0:NI, :]
                        nc.vector.tensor_tensor(xt, ps.rearrange("p (i d) -> p i d", d=P), xt, ALU.add)\
                            .then_inc(dve_used, 1)
                    elif kind == "STATS1":
                        dve.wait_ge(dve_used, ring.dve[("X1",)])
                        for i in range(NI):
                            nc.vector.bn_stats(stats1[:, i, :], x_tok[:, i, :]).then_inc(x_stats, 1)
                        for i in range(NI):
                            dve.wait_ge(x_stats, NI)
                            nc.vector.bn_aggr(mv1[:, i, :], stats1[:, i, :]).then_inc(x_stats, 1)
                        dve.wait_ge(x_stats, 2 * NI)
                        nc.vector.tensor_scalar(var1[:], mv1[:, :, 1], LN_EPS, None, ALU.add).then_inc(x_var_ready, 1)
                    elif kind == "LN1":
                        dve.wait_ge(x_rstd_ready, 1)
                        dve.wait_ge(wT_ready, NT - NP + 1)
                        for i in range(NI):
                            last = nc.vector.tensor_scalar(xn_tok[:, i, :], x_tok[:, i, :], mv1[:, i, 0:1],
                                                           rstd1[:, i:i + 1], ALU.subtract, ALU.mult)
                        last.then_inc(xn_ready, 1)
                    elif kind == "XL1":
                        dve.wait_ge(act_used, ring.act[("LN1",)])
                        nc.vector.tensor_tensor(hl[:, 0, :], xresT[:, 0, :], f32(hh[:, 0, :]), ALU.subtract)\
                            .then_inc(xl_ready, 1)
                    elif kind == "HS":
                        s = item[1]
                        dve.wait_ge(h32_ready, 2 * (s + 1))
                        dve.wait_ge(bank_filled, ring.filled(("VP", 2 * s + 1, 1)))
                        nc.vector.tensor_copy(hh[:, s, :], h32[:, 0:N]).then_inc(hh_ready, 1)
                    elif kind == "S":
                        T = item[1]
                        dve.wait_ge(scores_ready, T + 1)
                        if T >= 8:
                            dve.wait_ge(exp_ready, T - 7)
                        nc.vector.tensor_reduce(negmax[:, T % 8, :],
                                                scores[:, T % 2, :].rearrange("p (c k) -> p c k", k=P), AX_X,
                                                ALU.max, negate=True).then_inc(max_ready, 1)
                    elif kind == "TR":
                        T = item[1]
                        dve.wait_ge(wT_ready, T + 1)
                        if T >= 2:
                            dve.wait_ge(bank_filled, ring.filled(("AV", T - 2)))
                        nc.vector.tensor_copy(wT[:, T % 2, :], wT_ps[:, T % 2, :]).then_inc(wT_copied, 1)
                    elif kind == "I":
                        T = item[1]
                        dve.wait_ge(exp_ready, T + 1)
                        if T >= 8:
                            dve.wait_ge(weights_ready, T - 7)
                        nc.vector.reciprocal(inv[:, T % 8, :], rowsum[:, T % 8, :]).then_inc(inv_ready, 1)

            @block.tensor
            def _(pe):
                for item in order("PE"):
                    kind = item[0]
                    if item in ring.at:
                        old = ring.before(item)
                        if old is not None:
                            if old in ring.dve:
                                pe.wait_ge(dve_used, ring.dve[old])
                            if old in ring.act:
                                pe.wait_ge(act_used, ring.act[old])
                        ps = bank[:, ring.bank(item), :]
                    if kind == "QK":
                        _, u, i = item
                        l, b = unit_step(u) // B, unit_step(u) % B
                        if l:
                            pe.wait_ge(h_split, b + 1)
                        project_qk(nc, ps, keep, l, b, i, u).then_inc(bank_filled, 1)
                    elif kind == "VP":
                        _, u, v = item
                        l, b = unit_step(u) // B, unit_step(u) % B
                        c = (u % 2) * 2 * P
                        for k in range(2):
                            tok = slice((2 * v + k) * P, (2 * v + k + 1) * P)
                            last = split_matmul(nc, ps[:, k * 2 * P:(k + 1) * 2 * P], (hh[:, b, tok], hl[:, b, tok]),
                                                (LWH[l][0][:, 2, c:c + 2 * P], LWL[l][0][:, 2, c:c + 2 * P]))
                        last.then_inc(bank_filled, 1)
                    elif kind == "QT":
                        _, u, m, p = item
                        if u:
                            pe.wait_ge(norm_applied, NI * u)
                        for i in range(NI):
                            c = (2 * m + p) * P
                            last = nc.tensor.transpose(ps[:, i * P:(i + 1) * P], keep["rot"][:, i, c:c + P], ident[:])
                        last.then_inc(bank_filled, 1)
                    elif kind == "AV":
                        g = item[1]
                        u, t = g // TU, g % TU
                        pe.wait_ge(wT_copied, g + 1)
                        if t == 0:
                            pe.wait_ge(act_used, ring.act[("VP", u, 1)])
                        elif t == 1:
                            pe.wait_ge(v_shifted[u % 2], 32 * (u // 2 + 1))
                        for w in range(2):
                            j = max(2 * t + w - 1, 0)
                            for p in range(2):
                                for h in range(2):
                                    c = (2 * w + p) * P + h * WIN
                                    d = (2 * p + h) * DH
                                    last = nc.tensor.matmul(ps[h * 64:h * 64 + 64, p * P + w * WIN:p * P + (w + 1) * WIN],
                                                            V[:, u % 2, j, d:d + DH], wT[:, g % 2, c:c + WIN],
                                                            start=True, stop=True)
                        last.then_inc(bank_filled, 1)
                    elif kind == "WO":
                        s = item[1]
                        l = s // B
                        pe.wait_ge(dve_used, ring.dve[("AV", 2 * TU * (s + 1) - 1)])
                        for c in range(4):
                            last = split_matmul(nc, ps, (LWH[l][1][:, c, :], LWL[l][1][:, c, :]),
                                                (OTH[:, c, :], OTL[:, c, :]), start=c == 0, stop=c == 3)
                        last.then_inc(bank_filled, 1)
                    elif kind == "X1":
                        pe.wait_ge(dve_used, ring.dve[("W2", B)])
                        for i in range(NI):
                            tok = slice(i * P, (i + 1) * P)
                            last = nc.tensor.transpose(ps[:, tok], xresT[:, 0, tok], ident[:])
                        last.then_inc(bank_filled, 1)
                    elif kind == "LN1":
                        pe.wait_ge(xn_ready, 1)
                        for i in range(NI):
                            last = nc.tensor.transpose(ps[:, i * P:(i + 1) * P], xn_tok[:, i, :], ident[:])
                        last.then_inc(bank_filled, 1)
                    elif kind == "LT":
                        s = item[1]
                        pe.wait_ge(h32_ready, s + 1 + min(s, B))
                        for i in range(NI):
                            last = nc.tensor.transpose(ps[:, i * P:(i + 1) * P], h32[:, i * P:(i + 1) * P], ident[:])
                        last.then_inc(bank_filled, 1)
                    elif kind == "LB":
                        s = item[1]
                        pe.wait_ge(hn_ready, s + 1)
                        for i in range(NI):
                            last = nc.tensor.transpose(ps[:, i * P:(i + 1) * P], h_tok[:, i, :], ident[:])
                        last.then_inc(bank_filled, 1)
                    elif kind in ("G", "A"):
                        _, s, c = item
                        l = s // B
                        pe.wait_ge(n_ready, s + 1)
                        c0, m = CH[c]
                        c0 += HID if kind == "G" else 0
                        split_matmul(nc, ps[0:m], (LWH[l][2][:, c0:c0 + m], LWL[l][2][:, c0:c0 + m]),
                                     (nH[:], nL[:])).then_inc(bank_filled, 1)
                    elif kind == "W2":
                        s = item[1]
                        l = s // B
                        pe.wait_ge(hid_ready, 3 * (s + 1))
                        for c in range(3):
                            m = CH[c][1]
                            last = split_matmul(nc, ps, (LWH[l][3][0:m, c, :], LWL[l][3][0:m, c, :]),
                                                (HH[0:m, c, :], HL[0:m, c, :]), start=c == 0, stop=c == 2)
                        last.then_inc(bank_filled, 1)
                    elif kind == "TR":
                        T = item[1]
                        pe.wait_ge(weights_ready, T + 1)
                        if T >= 2:
                            pe.wait_ge(wT_copied, T - 1)
                        for c in range(4):
                            last = nc.tensor.transpose(wT_ps[:, T % 2, c * P:(c + 1) * P],
                                                       weights[:, T % NP, c * P:(c + 1) * P], ident[:])
                        last.then_inc(wT_ready, 1)
                    elif kind == "S":
                        T = item[1]
                        u, t = T // TU, T % TU
                        if t == 0:
                            pe.wait_ge(act_used, ring.act[("QT", u, 1, 1)])
                        if T >= 2:
                            pe.wait_ge(exp_ready, T - 1)
                        for w in range(2):
                            m = 1 if (t == 0 and w == 0) else 2
                            mask = keep["masks"][:, m:m + 1, :].to_broadcast([P, 2, P])
                            nc.tensor.matmul(scores[:, T % 2, w * 2 * P:(w + 1) * 2 * P], keep["ident_bf"][:],
                                             mask, start=w == 0, stop=False)
                        for w in range(2):
                            k0 = max(2 * t + w - 1, 0) * WIN
                            for p in range(2):
                                c = (2 * w + p) * P
                                last = nc.tensor.matmul(
                                    scores[:, T % 2, c:c + P],
                                    QBD[:, u % 2, p, 2 * t + w, :, :].rearrange("p h q -> p (h q)"),
                                    KT[:, u % 2, p, k0:k0 + P], start=False, stop=w == 1 and p == 1)
                        last.then_inc(scores_ready, 1)


def build(nc, io):
    with ExitStack() as ctx:
        def sb(name, shape, dt=F32):
            return ctx.enter_context(nc.sbuf_tensor(name, shape, dt))

        keep = {
            "x_tok": sb("x_tok", [P, B * NI, P]),
            "xresT": sb("xresT", [P, B, N]),
            "ident": sb("ident", [P, P]),
            "hh": sb("hh", [P, B, N], F32R),
            "hl": sb("hl", [P, B, N], F32R),
            "w_h": sb("w_h", [P, DEPTH * W_LAYER], F32R),
            "w_l": sb("w_l", [P, DEPTH * W_LAYER], F32R),
        }
        with ExitStack() as inner:
            def sb(name, shape, dt=F32):
                return inner.enter_context(nc.sbuf_tensor(name, shape, dt))

            keep |= {
                "ident_bf": sb("ident_bf", [P, P], BF16),
                "masks": sb("masks", [P, 3, P], BF16),
                "h32": sb("h32", [P, N + 4]),
                "tables": sb("tables", [P, DEPTH, 2, 2, NI, DH]),
                "rot": sb("rot", [P, NI, 2 * 2 * P]),
                "rot_a": sb("rot_a", [P, 2, 512]),
                "rot_b": sb("rot_b", [P, 2, 512]),
                "sq": sb("sq", [P, 2, 512]),
                "sumsq": sb("sumsq", [P, 2, 32]),
                "norm_inv": sb("norm_inv", [P, 2, 32]),
                "newton": sb("newton", [P, 32]),
                "cols": sb("cols", [P, DEPTH, COLS]),
            }
            attention_block(nc, "l0", keep, io["l0"], True)
            windowed_block(nc, keep, io["l1"]["w_all"])
        attention_block(nc, "l1", keep, io["l1"], False)


def _constants():
    import numpy as np

    p, k = np.arange(P)[:, None], np.arange(P)[None, :]
    q = p % WIN
    masks = np.stack([np.where(k > p, MASKED, 0.0),
                      np.where(k > q, MASKED, 0.0),
                      np.where((k > q + WIN) | (k < q), MASKED, 0.0)], 1)
    f = np.float32
    half = np.arange(0, DH, 2, dtype=f)
    inv_freq = (f(1.0) / f(10000.0) ** (half / f(DH))).astype(f)
    t = np.arange(N, dtype=f)
    freqs = t[:, None] * inv_freq[None, :]
    base = ((half + f(0.4 * DH)) / f(1.4 * DH)).astype(f)
    power = (t - f(N // 2)) / f(WIN // 2)
    scale = base[None, :] ** power[:, None]
    two = lambda a: np.concatenate([a, a], -1)
    cos, sin, scale = two(np.cos(freqs)), two(np.sin(freqs)), two(scale)
    sin[:, :DH // 2] *= -1
    rot = np.stack([np.stack([8.0 * cos * scale, cos / scale], 0),
                    np.stack([8.0 * sin * scale, sin / scale], 0)], 0)
    rot = rot.reshape(2, 2, NI, P, DH).transpose(3, 0, 1, 2, 4)
    c = np.ascontiguousarray
    return np.eye(P, dtype=f), c(masks.astype(f)), c(rot.astype(f))


def kernel(**a):
    import numpy as np
    import concourse.bacc as bacc
    from concourse import mybir as mb
    from concourse.bass_utils import run_bass_kernel_spmd as run

    a = {k: np.asarray(v) for k, v in a.items()}
    c = np.ascontiguousarray
    rows = lambda w: w.reshape(-1, P, w.shape[-1]).transpose(1, 0, 2).reshape(P, -1)

    ident, masks, rotary = _constants()
    layers, cols, scales = [], [], []
    pad = lambda v, n: np.concatenate([v, np.zeros((n - v.shape[0],) + v.shape[1:], v.dtype)])
    for l in range(DEPTH):
        layers += [a["L0_ffn_wqkv"][l], rows(a["L0_ffn_wo"][l]), a["L0_ffn_w1"][l],
                   rows(pad(a["L0_ffn_w2"][l], 3 * P))]
        b1 = a["L0_ffn_b1"][l]
        cols.append(np.stack([a["L0_ffn_ln_g"][l], a["L0_ffn_ln_b"][l], a["L0_ffn_b2"][l]]
                             + [pad(b1[o + s:o + s + n], P) for o in (0, HID) for s, n in CH], 1))
        per = []
        for s in (a["L0_ffn_q_scale"][l], a["L0_ffn_k_scale"][l]):
            per.append(np.stack([s, np.concatenate([s[DH // 2:], s[:DH // 2]])]))
        scales.append(np.stack(per))
    l0 = {
        "x": a["L0_attn_X"], "ident": ident, "masks": masks, "rotary": rotary,
        "qk_scales": c(np.broadcast_to(np.stack(scales)[None], (P, DEPTH, 2, 2, DH))),
        "cols": c(np.stack(cols, 1)), "Wq": a["L0_attn_Wq"], "Wk": a["L0_attn_Wk"], "Wv": a["L0_attn_Wv"],
        "w_all": c(np.concatenate(layers, 1)),
    }
    heads = lambda w: w.transpose(1, 0, 2).reshape(P, -1)
    float_w = np.concatenate([heads(a["L1_attn_proj_q"]), a["L1_attn_proj_k"],
                              heads(a["L1_attn_proj_o"].transpose(0, 2, 1))], 1)
    l1 = {
        "Wv": a["L1_attn_proj_v"],
        "w_all": c(np.concatenate([float_w, np.zeros((P, 3 * FF), np.float32)], 1)),
        "w_int": c(np.concatenate([a["L1_ffn_w_gate"].T, a["L1_ffn_w_up"].T, rows(a["L1_ffn_w_down"].T)], 1)),
    }
    nc = bacc.Bacc("TRN2", target_bir_lowering=False, num_devices=1)
    io, arrays = {}, {}
    for tag, group in (("l0", l0), ("l1", l1)):
        io[tag] = {}
        for name, value in group.items():
            value = c(value)
            arrays[f"{tag}_{name}_in"] = value
            io[tag][name] = nc.dram_tensor(f"{tag}_{name}_in", value.shape, mb.dt.from_np(value.dtype),
                                           kind="ExternalInput").ap()
    io["l1"]["out"] = nc.dram_tensor("out_dram", (B, N, P), F32, kind="ExternalOutput").ap()
    build(nc, io)
    return run(nc, [arrays], core_ids=[0]).results[0]["out_dram"]
```
